# Optimizing a Trainium2 kernel written in Bass

```python
import numpy as np
import jax
import jax.numpy as jnp

def _softmax(x, axis=-1):
    return jax.nn.softmax(x, axis=axis)

def _gelu(x):
    return jax.nn.gelu(x, approximate=True)

def _silu(x):
    return jax.nn.silu(x)

def _sigmoid(x):
    return jax.nn.sigmoid(x)

def _layernorm(x, axis=-1, eps=1e-05):
    m = jnp.mean(x, axis=axis, keepdims=True)
    v = jnp.var(x, axis=axis, keepdims=True)
    return (x - m) / jnp.sqrt(v + eps)

def _scatter_add(tgt, idx, src, axis=0):
    return tgt.at[idx].add(src)

def _segment_sum(src, seg, n):
    return jax.ops.segment_sum(src, seg, n)
kernel_name = 'mk_perceiver_d1_seqx_r2_2397cb'

def setup_inputs(seed: int=0):
    np.random.seed(seed)
    _w = jnp.asarray

    def _rec_inputs():
        import jax
        import jax.numpy as jnp
        _rk = jax.random.key(seed)
        x = 7.22e-05 + 1 * jax.random.normal(jax.random.fold_in(_rk, 1), (4, 128, 512), jnp.float32)
        _lenS = 128 - jax.random.randint(jax.random.fold_in(_rk, 7), (4,), 0, max(1, 128 // 4) + 1, jnp.int32)
        _lenS2 = 2048 - jax.random.randint(jax.random.fold_in(_rk, 8), (4,), 0, max(1, 2048 // 4) + 1, jnp.int32)
        _ctx_1024P = jax.random.normal(jax.random.fold_in(_rk, 11), (4, 16, 512), jnp.float32)
        _ctx_1024c = jax.random.dirichlet(jax.random.fold_in(_rk, 511), 0.3 * jnp.ones((16,), jnp.float32), (4, 2048))
        _ctx_1024t = jnp.einsum('bsk,bkd->bsd', _ctx_1024c, _ctx_1024P)
        _ctx_1024t = _ctx_1024t * jax.lax.rsqrt(jnp.mean(jnp.square(_ctx_1024t)) + 1e-12) * 0.953939
        ctx_1024 = 4.13588e-05 + 0.999923 * (_ctx_1024t + 0.3 * jax.random.normal(jax.random.fold_in(_rk, 611), (4, 2048, 512), jnp.float32))
        return (x, ctx_1024, _lenS2)
    x, ctx_1024, _lenS2 = _rec_inputs()

    def _L0_xattn_setup():
        import jax, jax.numpy as jnp
        import numpy as np
        DIM, HEADS, HEAD_DIM = (512, 16, 64)
        B, L, S = (4, 1024, 1024)
        EPS = 1e-05
        NEG_INF = -1000000000.0

        def rms_norm(x, w):
            var = jnp.mean(jnp.square(x), axis=-1, keepdims=True)
            return x * jax.lax.rsqrt(var + EPS) * w
        key = jax.random.key(seed)
        ks = jax.random.split(key, 9)
        hd = HEADS * HEAD_DIM
        scale = 1.0 / np.sqrt(DIM)
        return {'q': jax.random.normal(ks[0], (B, L, DIM), dtype=jnp.float32), 'kv': jax.random.normal(ks[1], (B, S, DIM), dtype=jnp.float32), 'x_seqlens': jax.random.randint(ks[2], (B,), 1, S + 1, dtype=jnp.int32), 'Wq': jax.random.normal(ks[3], (DIM, hd), dtype=jnp.float32) * scale, 'Wk': jax.random.normal(ks[4], (DIM, hd), dtype=jnp.float32) * scale, 'Wv': jax.random.normal(ks[5], (DIM, hd), dtype=jnp.float32) * scale, 'Wo': jax.random.normal(ks[6], (hd, DIM), dtype=jnp.float32) * (1.0 / np.sqrt(hd)), 'q_norm_w': jnp.ones((HEAD_DIM,), dtype=jnp.float32), 'k_norm_w': jnp.ones((HEAD_DIM,), dtype=jnp.float32)}
    _L0_xattn_all = _L0_xattn_setup()
    _L0_xattn_in = {k: v for k, v in _L0_xattn_all.items() if k in ('Wq', 'Wk', 'Wv', 'Wo', 'q_norm_w', 'k_norm_w')}
    del _L0_xattn_all

    def _L0_attn_setup():
        import jax, jax.numpy as jnp
        import numpy as np
        B, S, D, H, DH = (4, 1024, 512, 16, 64)
        key = jax.random.key(seed)
        k1, k2, k3, k4, k5 = jax.random.split(key, 5)
        scale = 1.0 / np.sqrt(D)
        return {'x': jax.random.normal(k1, (B, S, D), dtype=jnp.float32), 'w_qkv': jax.random.normal(k2, (D, 3, H, DH), dtype=jnp.float32) * scale, 'b_qkv': jax.random.normal(k3, (3, H, DH), dtype=jnp.float32) * 0.02, 'w_out': jax.random.normal(k4, (H, DH, D), dtype=jnp.float32) * (1.0 / np.sqrt(H * DH)), 'b_out': jax.random.normal(k5, (D,), dtype=jnp.float32) * 0.02}
    _L0_attn_all = _L0_attn_setup()
    _L0_attn_in = {k: v for k, v in _L0_attn_all.items() if k in ('w_qkv', 'b_qkv', 'w_out', 'b_out')}
    del _L0_attn_all

    def _L0_ffn_setup():
        import jax, jax.numpy as jnp
        import numpy as np
        BLOCK = 32
        W_BITS = 4
        ACT_BITS = 16

        def act_qdq(x):
            qmax = 2.0 ** (ACT_BITS - 1) - 1.0
            scale = jnp.maximum(jnp.max(jnp.abs(x)) / qmax, 1e-12)
            return jnp.clip(jnp.round(x / scale), -qmax - 1.0, qmax) * scale

        def fixed_qdq_u16(x):
            scale = 1.0 / 65536.0
            return jnp.clip(jnp.round(x / scale), 0.0, 65535.0) * scale

        def lpbq_dequant(w):
            O, I = w.shape
            qmax = 2.0 ** (W_BITS - 1) - 1.0
            wb = w.reshape(O, I // BLOCK, BLOCK)
            s = jnp.maximum(jnp.max(jnp.abs(wb), axis=-1, keepdims=True) / qmax, 1e-12)
            wq = jnp.clip(jnp.round(wb / s), -qmax - 1.0, qmax) * s
            return wq.reshape(O, I)
        key = jax.random.key(seed)
        k1, k2, k3, k4 = jax.random.split(key, 4)
        B, S, H, I = (2, 2048, 512, 1536)
        x = jax.random.normal(k1, (B, S, H), jnp.float32)
        w_gate = jax.random.normal(k2, (I, H), jnp.float32) * 0.02
        w_up = jax.random.normal(k3, (I, H), jnp.float32) * 0.02
        w_down = jax.random.normal(k4, (H, I), jnp.float32) * 0.02
        return {'x': x, 'w_gate': w_gate, 'w_up': w_up, 'w_down': w_down}
    _L0_ffn_all = _L0_ffn_setup()
    _L0_ffn_in = {k: v for k, v in _L0_ffn_all.items() if k in ('w_gate', 'w_up', 'w_down')}
    del _L0_ffn_all
    return {'x': x, 'ctx_1024': ctx_1024, '_lenS2': _lenS2, 'L0_xattn_Wq': _L0_xattn_in['Wq'], 'L0_xattn_Wk': _L0_xattn_in['Wk'], 'L0_xattn_Wv': _L0_xattn_in['Wv'], 'L0_xattn_Wo': _L0_xattn_in['Wo'], 'L0_xattn_q_norm_w': _L0_xattn_in['q_norm_w'], 'L0_xattn_k_norm_w': _L0_xattn_in['k_norm_w'], 'L0_attn_w_qkv': _L0_attn_in['w_qkv'], 'L0_attn_b_qkv': _L0_attn_in['b_qkv'], 'L0_attn_w_out': _L0_attn_in['w_out'], 'L0_attn_b_out': _L0_attn_in['b_out'], 'L0_ffn_w_gate': _L0_ffn_in['w_gate'], 'L0_ffn_w_up': _L0_ffn_in['w_up'], 'L0_ffn_w_down': _L0_ffn_in['w_down']}

def reference(x, ctx_1024, _lenS2, L0_xattn_Wq, L0_xattn_Wk, L0_xattn_Wv, L0_xattn_Wo, L0_xattn_q_norm_w, L0_xattn_k_norm_w, L0_attn_w_qkv, L0_attn_b_qkv, L0_attn_w_out, L0_attn_b_out, L0_ffn_w_gate, L0_ffn_w_up, L0_ffn_w_down):
    import jax
    import jax.numpy as jnp

    def _L0_xattn_ref(q, kv, x_seqlens, Wq, Wk, Wv, Wo, q_norm_w, k_norm_w):
        import jax, jax.numpy as jnp
        import numpy as np
        DIM, HEADS, HEAD_DIM = (512, 16, 64)
        B, L, S = (4, 1024, 1024)
        EPS = 1e-05
        NEG_INF = -1000000000.0

        def rms_norm(x, w):
            var = jnp.mean(jnp.square(x), axis=-1, keepdims=True)
            return x * jax.lax.rsqrt(var + EPS) * w
        b, l, _ = q.shape
        s = kv.shape[1]
        qh = (q @ Wq).reshape(b, l, HEADS, HEAD_DIM).transpose(0, 2, 1, 3)
        kh = (kv @ Wk).reshape(b, s, HEADS, HEAD_DIM).transpose(0, 2, 1, 3)
        vh = (kv @ Wv).reshape(b, s, HEADS, HEAD_DIM).transpose(0, 2, 1, 3)
        qh = rms_norm(qh, q_norm_w)
        kh = rms_norm(kh, k_norm_w)
        mask = (jnp.arange(s, dtype=jnp.int32)[None, :] < x_seqlens[:, None])[:, None, None, :]
        scores = jnp.einsum('bhld,bhsd->bhls', qh, kh) * (1.0 / np.sqrt(HEAD_DIM))
        scores = jnp.where(mask, scores, NEG_INF)
        attn = jax.nn.softmax(scores, axis=-1)
        o = jnp.einsum('bhls,bhsd->bhld', attn, vh)
        o = o.transpose(0, 2, 1, 3).reshape(b, l, HEADS * HEAD_DIM)
        return o @ Wo

    def _L0_attn_ref(x, w_qkv, b_qkv, w_out, b_out):
        import jax, jax.numpy as jnp
        import numpy as np
        B, S, D, H, DH = (4, 1024, 512, 16, 64)
        qkv = jnp.einsum('bsd,dthe->bsthe', x, w_qkv) + b_qkv
        q, k, v = (qkv[:, :, 0], qkv[:, :, 1], qkv[:, :, 2])
        head_dim = q.shape[-1]
        scores = jnp.einsum('bqhe,bkhe->bhqk', q, k) / jnp.sqrt(jnp.float32(head_dim))
        seq = scores.shape[-1]
        causal = (jnp.arange(seq)[:, None] >= jnp.arange(seq)[None, :]).astype(scores.dtype)
        scores = scores - 1000000000.0 * (1.0 - causal)
        weights = jax.nn.softmax(scores, axis=-1)
        answers = jnp.einsum('bhqk,bkhe->bqhe', weights, v)
        out = jnp.einsum('bqhe,hed->bqd', answers, w_out) + b_out
        return out

    def _L0_ffn_ref(x, w_gate, w_up, w_down):
        import jax, jax.numpy as jnp
        import numpy as np
        BLOCK = 32
        W_BITS = 4
        ACT_BITS = 16

        def act_qdq(x):
            qmax = 2.0 ** (ACT_BITS - 1) - 1.0
            scale = jnp.maximum(jnp.max(jnp.abs(x)) / qmax, 1e-12)
            return jnp.clip(jnp.round(x / scale), -qmax - 1.0, qmax) * scale

        def fixed_qdq_u16(x):
            scale = 1.0 / 65536.0
            return jnp.clip(jnp.round(x / scale), 0.0, 65535.0) * scale

        def lpbq_dequant(w):
            O, I = w.shape
            qmax = 2.0 ** (W_BITS - 1) - 1.0
            wb = w.reshape(O, I // BLOCK, BLOCK)
            s = jnp.maximum(jnp.max(jnp.abs(wb), axis=-1, keepdims=True) / qmax, 1e-12)
            wq = jnp.clip(jnp.round(wb / s), -qmax - 1.0, qmax) * s
            return wq.reshape(O, I)
        x = act_qdq(x)
        up = act_qdq(x @ lpbq_dequant(w_up).T)
        gate = act_qdq(x @ lpbq_dequant(w_gate).T)
        sig = fixed_qdq_u16(jax.nn.sigmoid(gate))
        gate = act_qdq(gate * sig)
        o = act_qdq(gate * up)
        return o @ lpbq_dequant(w_down).T
    x = x + _L0_xattn_ref(_layernorm(x, axis=-1), ctx_1024, _lenS2, L0_xattn_Wq, L0_xattn_Wk, L0_xattn_Wv, L0_xattn_Wo, L0_xattn_q_norm_w, L0_xattn_k_norm_w)
    x = x + _L0_attn_ref(_layernorm(x, axis=-1), L0_attn_w_qkv, L0_attn_b_qkv, L0_attn_w_out, L0_attn_b_out)
    x = x + _L0_ffn_ref(_layernorm(x, axis=-1), L0_ffn_w_gate, L0_ffn_w_up, L0_ffn_w_down)
    return x

_drawn_inputs = setup_inputs


def setup_inputs(seed=0):
    import zlib

    import numpy as np

    out = dict(_drawn_inputs(seed))
    spreads = {'L0_xattn_q_norm_w': (1.0, 0.2), 'L0_xattn_k_norm_w': (1.0, 0.572)}
    factors = {'L0_attn_b_qkv': 3.488, 'L0_attn_b_out': 3.584}
    for name, (base, spread) in spreads.items():
        noise = np.random.default_rng([zlib.crc32(name.encode()), seed]).standard_normal(out[name].shape)
        drawn = base * np.exp(spread * noise) if base else spread * noise
        out[name] = jnp.asarray(drawn.astype(out[name].dtype))
    for name, factor in factors.items():
        out[name] = (out[name] * factor).astype(out[name].dtype)
    return out
```

```python
from contextlib import ExitStack

import concourse.bass as bass
from concourse import mybir

F32 = mybir.dt.float32
F32R = mybir.dt.float32r
F16 = mybir.dt.float16
I32 = mybir.dt.int32
ALU = mybir.AluOpType
ACT = mybir.ActivationFunctionType
AX_X = mybir.AxisListType.X
ABSMAX = bass.bass_isa.ReduceOp.absmax

P = 128
B = 4
D = 512
KD = D // P
S = 2048
HEADS, HD = 16, 64
E = HEADS * HD
HH = 8
HALVES = HEADS // HH
CHUNK = 512
TILES = CHUNK // P
CHUNKS = S // CHUNK
WINDOWS = HALVES * B * CHUNKS
UNITS = HALVES * B
SLOTS = 2 * TILES
ALL_HEADS = WINDOWS * HH
VW = HD + 1
FF = 1536
KF = FF // P
BLOCK = 32
LN_EPS = 1e-5
RMS_EPS = 1e-5
RAWS = 2
Q_UP, K_UP, V_UP, P_UP = 32.0, 1024.0, 16.0, 4096.0
LN_P_UP = 8.317766166719343
S_SCALE = 1.0 / (Q_UP * K_UP * 8.0)
NEG = -1e9 / S_SCALE
LOWEST = -3e38


def wait(eng, semaphore, value):
    if not isinstance(value, int) or value > 0:
        eng.wait_ge(semaphore, value)


def program(nc, x, ctx_t, lens, wq, wk, wv, wo, q_norm, k_norm, w_qkv, b_qkv, w_out, b_out,
            w_gate, w_up, w_down, out):
    with ExitStack() as whole:
        def sb(name, shape, dt, ctx=whole):
            return ctx.enter_context(nc.sbuf_tensor(name, shape, dt))

        def sems(ctx, names):
            handles = [nc.alloc_semaphore(n) for n in names.split()]

            def give_back():
                nc.clear_and_free_semaphores(handles)
                nc.all_engine_barrier()

            ctx.callback(give_back)
            return handles

        bank = [whole.enter_context(nc.psum_tensor(f"bank{i}", [P, 512], F32)) for i in range(8)]

        resid = sb("resid", [P, B, D], F32)
        ident = sb("ident", [P, P], F32)
        ident16 = sb("ident16", [P, P], F16)
        half_neg = sb("half_neg", [P, 64], F32)
        cross = whole.enter_context(ExitStack())
        o_acc = sb("o_acc", [P, UNITS, HH, VW], F32, cross)
        stage_q = cross.enter_context(ExitStack())
        wk_hi, wk_lo = (sb(n, [P, KD, E], F32R, stage_q) for n in ("wk_hi", "wk_lo"))
        wv_hi, wv_lo = (sb(n, [P, KD, E], F32R, stage_q) for n in ("wv_hi", "wv_lo"))
        q_st = sb("q_st", [P, UNITS, 2, HH, P], F16, stage_q)

        prologue(nc, sems, sb, bank, locals())
        cross_attention(nc, sems, sb, bank, locals())
        stage_q.close()
        with ExitStack() as attn:
            w_qkv_hi, w_qkv_lo = (sb(n, [P, KD, 3 * E], F32R, attn) for n in ("w_qkv_hi", "w_qkv_lo"))
            output_projection(nc, sems, sb, bank, locals(), "cross_out", o_acc, wo, None, (w_qkv, w_qkv_hi, w_qkv_lo))
            self_attention(nc, sems, sb, bank, locals(), w_qkv_hi, w_qkv_lo, o_acc)
        output_projection(nc, sems, sb, bank, locals(), "self_out", o_acc, w_out, b_out)
        cross.close()
        feed_forward(nc, sems, sb, bank, locals(), out)


def prologue(nc, sems, sb, bank, g):
    with ExitStack() as c:
        resid, ident, ident16, half_neg = g["resid"], g["ident"], g["ident16"], g["half_neg"]
        w_hi = [None, g["wk_hi"], g["wv_hi"]]
        w_lo = [None, g["wk_lo"], g["wv_lo"]]
        w_hi[0], w_lo[0] = (sb(n, [P, KD, E], F32R, c) for n in ("wq_hi", "wq_lo"))
        raw = [sb(f"w_raw{i}", [P, E], F32, c) for i in range(RAWS)]
        stats = sb("stats", [P, B, 6], F32, c)
        mean_var = sb("mean_var", [P, B, 2], F32, c)
        rstd = sb("rstd", [P, B], F32, c)
        var_eps = sb("var_eps", [P, B], F32, c)
        xn = sb("xn", [P, B, D], F32, c)
        xt_hi, xt_lo = (sb(n, [P, KD, B * P], F32R, c) for n in ("xt_hi", "xt_lo"))
        qk_norm = sb("qk_norm", [P, 2, HD], F32, c)
        norm_w = sb("norm_w", [P, HD], F32, c)
        q_sq = sb("q_sq", [P, HH * HD], F32, c)
        q_raw = [sb(f"q_raw{i}", [P, HH * HD], F32, c) for i in range(2)]
        q_ss, q_ms, q_rinv = (sb(n, [P, UNITS, HH], F32, c) for n in ("q_ss", "q_ms", "q_rinv"))
        q_n = [sb(f"q_n{i}", [P, HH, HD], F32, c) for i in range(2)]
        q_w = [sb(f"q_w{i}", [P, HH, HD], F32, c) for i in range(2)]
        stack = [sb(f"q_stack{i}", [P, HH, 3, HD], F16, c) for i in range(2)]
        x_in, norm_in = sems(c, "x_in norm_in")
        w_in = sems(c, " ".join(f"w_in{i}" for i in range(RAWS)))
        consts, stat, agg, v_eps, rs, x_n, x_tr, x_hi, x_lo = sems(
            c, "consts stat agg v_eps rs x_n x_tr x_hi x_lo")
        wh_done, wl_done, wnorm = sems(c, "wh_done wl_done wnorm")
        qp_done, sq_done, raw_done, ss_done, ms_done, rinv_done, qn_done, qw_done = sems(
            c, "qp_done sq_done raw_done ss_done ms_done rinv_done qn_done qw_done")
        hi_done, hi2_done, lo_done, tr_a, tr_b, st_a, st_b = sems(
            c, "hi_done hi2_done lo_done tr_a tr_b st_a st_b")
        q_st = g["q_st"]
        t_a, t_b = (bank[4 + i][:, :].bitcast(F16) for i in range(2))
        block = c.enter_context(nc.Block())

        def unit(n):
            return n // HALVES, n % HALVES, (n % HALVES) * B + n // HALVES

        @block.sync
        def _(sp):
            for b in range(B):
                sp.dma_start(resid[:, b, :], g["x"][b]).then_inc(x_in, 16)
            for i, n in enumerate(("q_norm", "k_norm")):
                sp.dma_start(qk_norm[:, i, :], g[n].partition_broadcast(P)).then_inc(norm_in, 16)
            for j in range(3 * KD):
                wait(sp, wl_done, j - RAWS + 1)
                sp.dma_start(raw[j % RAWS][:, :], g[("wq", "wk", "wv")[j // KD]].rearrange(
                    "(k p) n -> p k n", p=P)[:, j % KD, :]).then_inc(w_in[j % RAWS], 16)

        @block.gpsimd
        def _(pool):
            nc.gpsimd.memset(ident[:, :], 0.0).then_inc(consts, 1)
            nc.gpsimd.memset(ident16[:, :], 0.0).then_inc(consts, 1)
            nc.gpsimd.memset(half_neg[:, :], -0.5).then_inc(consts, 1)
            pool.wait_ge(consts, 3)
            for t in (ident, ident16):
                nc.gpsimd.affine_select(out=t[:, :], in_=t[:, :], compare_op=ALU.not_equal, fill=1.0, base=0,
                                        pattern=[[-1, P]], channel_multiplier=1).then_inc(consts, 1)
            pool.wait_ge(agg, B)
            nc.gpsimd.tensor_scalar(var_eps[:, :], mean_var[:, :, 1], LN_EPS, None, ALU.add).then_inc(v_eps, 1)
            pool.wait_ge(v_eps, 1)
            nc.gpsimd.tensor_tensor(rstd[:, :], var_eps[:, :], half_neg[:, 0:B], ALU.pow).then_inc(rs, 1)
            pool.wait_ge(wnorm, 1)
            for n in range(UNITS + 1):
                if n < UNITS:
                    pool.wait_ge(ss_done, n + 1)
                    nc.gpsimd.tensor_scalar(q_ms[:, n, :], q_ss[:, n, :], 1.0 / HD, RMS_EPS, ALU.mult,
                                            ALU.add).then_inc(ms_done, 1)
                    pool.wait_ge(ms_done, n + 1)
                    nc.gpsimd.tensor_tensor(q_rinv[:, n, :], q_ms[:, n, :], half_neg[:, 0:HH],
                                            ALU.pow).then_inc(rinv_done, 1)
                if n >= 1:
                    m = n - 1
                    pool.wait_ge(qn_done, m + 1)
                    wait(pool, lo_done, m - 1)
                    nc.gpsimd.tensor_tensor(q_w[m % 2][:, :, :], q_n[m % 2][:, :, :],
                                            norm_w[:, :].unsqueeze(1).to_broadcast([P, HH, HD]),
                                            ALU.mult).then_inc(qw_done, 1)

        @block.tensor
        def _(pe):
            pe.wait_ge(consts, 5)
            for b in range(B):
                pe.wait_ge(x_n, b + 1)
                for k in range(KD):
                    mm = nc.tensor.transpose(bank[b][:, k * P:(k + 1) * P], xn[:, b, k * P:(k + 1) * P], ident[:, :])
                mm.then_inc(x_tr, 1)
            for n in range(UNITS + 2):
                if n < UNITS:
                    b, half, _ = unit(n)
                    if n == 0:
                        pe.wait_ge(wl_done, KD)
                        pe.wait_ge(x_lo, B)
                    wait(pe, raw_done, n - 3)
                    project(nc, bank[n % 4][:, :], [xt_hi[:, k, b * P:(b + 1) * P] for k in range(KD)],
                            [xt_lo[:, k, b * P:(b + 1) * P] for k in range(KD)],
                            [w_hi[0][:, k, half * 512:(half + 1) * 512] for k in range(KD)],
                            [w_lo[0][:, k, half * 512:(half + 1) * 512] for k in range(KD)]).then_inc(qp_done, 1)
                if n >= 2:
                    m = n - 2
                    pe.wait_ge(lo_done, m + 1)
                    pe.wait_ge(hi2_done, m + 1)
                    wait(pe, st_a, m)
                    for h in range(HH):
                        mm = nc.tensor.transpose(t_a[:, h * P:(h + 1) * P],
                                                 stack[m % 2][:, h, 0:2, :].rearrange("p a d -> p (a d)"), ident16[:, :])
                    mm.then_inc(tr_a, 1)
                    wait(pe, st_b, m)
                    for h in range(HH):
                        mm = nc.tensor.transpose(t_b[:, h * P:(h + 1) * P],
                                                 stack[m % 2][:, h, 1:3, :].rearrange("p a d -> p (a d)"), ident16[:, :])
                    mm.then_inc(tr_b, 1)

        @block.scalar
        def _(act):
            def weights_hi(pieces):
                for j in pieces:
                    i = j // KD
                    act.wait_ge(w_in[j % RAWS], 16 * (j // RAWS + 1))
                    nc.scalar.activation(w_hi[i][:, j % KD, :], raw[j % RAWS][:, :], ACT.Copy).then_inc(wh_done, 1)

            def finish(m):
                act.wait_ge(qw_done, m + 1)
                wait(act, tr_b, m - 1)
                nc.scalar.activation(stack[m % 2][:, :, 0, :], q_w[m % 2][:, :, :], ACT.Copy).then_inc(hi_done, 1)

            def keep(m):
                act.wait_ge(tr_b, m + 1)
                nc.scalar.activation(q_st[:, unit(m)[2], 1, :, :].rearrange("p h q -> p (h q)"), t_b[:, :],
                                     ACT.Copy).then_inc(st_b, 1)

            weights_hi(range(KD))
            for b in range(B):
                act.wait_ge(x_tr, b + 1)
                nc.scalar.activation(xt_hi[:, :, b * P:(b + 1) * P], bank[b][:, :].rearrange("p (k q) -> p k q", k=KD),
                                     ACT.Copy).then_inc(x_hi, 1)
            for n in range(UNITS + 3):
                if n < UNITS:
                    act.wait_ge(qp_done, n + 1)
                    wait(act, ss_done, n)
                    nc.scalar.activation(q_sq[:, :], bank[n % 4][:, :], ACT.Square).then_inc(sq_done, 1)
                    wait(act, qn_done, n - 1)
                    nc.scalar.activation(q_raw[n % 2][:, :], bank[n % 4][:, :], ACT.Copy).then_inc(raw_done, 1)
                if 1 <= n <= UNITS:
                    finish(n - 1)
                if n >= 3:
                    keep(n - 3)
                if n < 2 * KD:
                    weights_hi([KD + n])

        @block.vector
        def _(dve):
            for b in range(B):
                dve.wait_ge(x_in, 16 * B)
                nc.vector.bn_stats(stats[:, b, :], resid[:, b, :]).then_inc(stat, 1)
            for b in range(B):
                dve.wait_ge(stat, b + 1)
                nc.vector.bn_aggr(mean_var[:, b, :], stats[:, b, :]).then_inc(agg, 1)
            dve.wait_ge(rs, 1)
            for b in range(B):
                nc.vector.tensor_scalar(xn[:, b, :], resid[:, b, :], mean_var[:, b, 0:1], rstd[:, b:b + 1],
                                        ALU.subtract, ALU.mult).then_inc(x_n, 1)
            dve.wait_ge(norm_in, 32)
            nc.vector.scalar_tensor_tensor(norm_w[:, :], qk_norm[:, 0, :], Q_UP, qk_norm[:, 1, :], ALU.mult,
                                           ALU.mult).then_inc(wnorm, 1)

            def weights_lo(pieces):
                for j in pieces:
                    i = j // KD
                    dve.wait_ge(wh_done, j + 1)
                    nc.vector.tensor_tensor(w_lo[i][:, j % KD, :], raw[j % RAWS][:, :],
                                            w_hi[i][:, j % KD, :].bitcast(F32), ALU.subtract).then_inc(wl_done, 1)

            def normed(m):
                dve.wait_ge(rinv_done, m + 1)
                dve.wait_ge(raw_done, m + 1)
                wait(dve, qw_done, m - 1)
                nc.vector.tensor_tensor(q_n[m % 2][:, :, :], q_raw[m % 2][:, :].rearrange("p (h d) -> p h d", h=HH),
                                        q_rinv[:, m, :].unsqueeze(2).to_broadcast([P, HH, HD]),
                                        ALU.mult).then_inc(qn_done, 1)

            def parts(m):
                dve.wait_ge(hi_done, m + 1)
                wait(dve, tr_b, m - 1)
                nc.vector.tensor_copy(stack[m % 2][:, :, 2, :], stack[m % 2][:, :, 0, :]).then_inc(hi2_done, 1)
                nc.vector.tensor_tensor(stack[m % 2][:, :, 1, :], q_w[m % 2][:, :, :], stack[m % 2][:, :, 0, :],
                                        ALU.subtract).then_inc(lo_done, 1)

            def keep(m):
                dve.wait_ge(tr_a, m + 1)
                nc.vector.tensor_copy(q_st[:, unit(m)[2], 0, :, :].rearrange("p h q -> p (h q)"),
                                      t_a[:, :]).then_inc(st_a, 1)

            weights_lo(range(KD))
            for b in range(B):
                dve.wait_ge(x_hi, b + 1)
                nc.vector.tensor_tensor(xt_lo[:, :, b * P:(b + 1) * P], bank[b][:, :].rearrange("p (k q) -> p k q", k=KD),
                                        xt_hi[:, :, b * P:(b + 1) * P].bitcast(F32), ALU.subtract).then_inc(x_lo, 1)
            for n in range(UNITS + 3):
                if n < UNITS:
                    dve.wait_ge(sq_done, n + 1)
                    nc.vector.tensor_reduce(q_ss[:, n, :], q_sq[:, :].rearrange("p (h d) -> p h d", h=HH), AX_X,
                                            ALU.add).then_inc(ss_done, 1)
                if n < UNITS:
                    normed(n)
                if 1 <= n <= UNITS:
                    parts(n - 1)
                if n >= 3:
                    keep(n - 3)
                if n < 2 * KD:
                    weights_lo([KD + n])


def project(nc, to, x_hi, x_lo, w_hi, w_lo):
    n = len(x_hi)
    for k in range(n):
        nc.tensor.matmul(to, x_hi[k], w_hi[k], start=(k == 0), stop=False)
        nc.tensor.matmul(to, x_hi[k], w_lo[k], start=False, stop=False)
        mm = nc.tensor.matmul(to, x_lo[k], w_hi[k], start=False, stop=(k == n - 1))
    return mm


def cross_attention(nc, sems, sb, bank, g):
    with ExitStack() as c:
        q_st, o_acc, ident, ident16, half_neg = (g[n] for n in ("q_st", "o_acc", "ident", "ident16", "half_neg"))
        ctx_raw = [sb(f"ctx_raw{i}", [P, KD, P], F32, c) for i in range(2)]
        ctx_hi = [sb(f"ctx_hi{i}", [P, KD, P], F32R, c) for i in range(TILES)]
        ctx_lo = [sb(f"ctx_lo{i}", [P, KD, P], F32R, c) for i in range(TILES)]
        k_sq = sb("k_sq", [P, HH * HD], F32, c)
        k_raw = [sb(f"k_raw{i}", [P, HH * HD], F32, c) for i in range(2)]
        k_ss = sb("k_ss", [P, HH], F32, c)
        k_ms = [sb(f"k_ms{i}", [P, HH], F32, c) for i in range(2)]
        k_rinv = [sb(f"k_rinv{i}", [P, HH], F32, c) for i in range(2)]
        k_n = [sb(f"k_n{i}", [P, HH, HD], F32, c) for i in range(2)]
        k_lh = [sb(f"k_lh{i}", [P, HH, 2, HD], F16, c) for i in range(2)]
        kt = [sb(f"kt{i}", [P, HH, CHUNK], F16, c) for i in range(2)]
        v_hi = [sb(f"v_hi{i}", [P, TILES, HH, VW], F16, c) for i in range(2)]
        v_lo = [sb(f"v_lo{i}", [P, TILES, HH, VW], F16, c) for i in range(2)]
        probs = [sb(f"probs{i}", [P, CHUNK], F32, c) for i in range(4)]
        pt_hi = [sb(f"pt_hi{i}", [P, CHUNK], F16, c) for i in range(2)]
        pt_lo = [sb(f"pt_lo{i}", [P, CHUNK], F16, c) for i in range(2)]
        key_no = sb("key_no", [P, CHUNK], F32, c)
        mask = sb("mask", [P, CHUNK], F32, c)
        lens_i = sb("lens_i", [P, B], I32, c)
        lens_f = sb("lens_f", [P, B], F32, c)
        left = sb("left", [P, B, CHUNKS], F32, c)
        chunk_max = sb("chunk_max", [P, 4], F32, c)
        run_max = sb("run_max", [P, UNITS, HH], F32, c)
        new_max = [sb(f"new_max{i}", [P, 2], F32, c) for i in range(2)]
        neg_max = [sb(f"neg_max{i}", [P, 2], F32, c) for i in range(2)]
        max_step = [sb(f"max_step{i}", [P, 2], F32, c) for i in range(2)]
        alpha = [sb(f"alpha{i}", [P, 2], F32, c) for i in range(2)]

        ctx_in = sems(c, "ctx_in0 ctx_in1")
        lens_in, ready, lens_done, left_done = sems(c, "lens_in ready lens_done left_done")
        ctx_hi_done, ctx_lo_done, proj_done = sems(c, "ctx_hi_done ctx_lo_done proj_done")
        k_sq_done, k_raw_done, k_ss_done, k_ms_done, k_rinv_done, k_n_done, k_hi_done, k_lo_done, k_tr_done, kt_done = sems(
            c, "k_sq_done k_raw_done k_ss_done k_ms_done k_rinv_done k_n_done k_hi_done k_lo_done k_tr_done kt_done")
        v_hi_done, v_lo_done, mask_done = sems(c, "v_hi_done v_lo_done mask_done")
        s_done, s_max_done, new_max_done, neg_max_done, step_done, kept_done = sems(
            c, "s_done s_max_done new_max_done neg_max_done step_done kept_done")
        p_done, p_tr_done, pt_hi_done, pt_lo_done, pv_done, alpha_done, scaled_done, added_done = sems(
            c, "p_done p_tr_done pt_hi_done pt_lo_done pv_done alpha_done scaled_done added_done")
        scores, p_turn, k_turn, o_new = bank[4], bank[5], bank[6][:, :].bitcast(F16), bank[7]
        o_pair = [o_new[:, 2 * i * VW:2 * (i + 1) * VW] for i in range(2)]
        block = c.enter_context(nc.Block())

        def windows(eng, body, last):
            for w in range(2):
                for s in range(SLOTS):
                    body(w, w, s)
            with eng.Fori(0, (WINDOWS - 4) // 2) as i:
                for p in range(2):
                    for s in range(SLOTS):
                        body(2 * i + 2 + p, 2 + p, s)
            for w in range(WINDOWS - 2, WINDOWS + 2):
                for s in range(SLOTS):
                    if SLOTS * w + s <= last:
                        body(w, w, s)

        def k_tile(w, n, s, lag):
            at = s - lag
            if at < 0:
                at, w, n = at + SLOTS, w - 1, n - 1
            return (TILES * w + at, at) if 0 <= n < WINDOWS and at < TILES else None

        def v_tile(w, n, s, lag):
            at = s - lag
            if at < 0:
                at, w, n = at + SLOTS, w - 1, n - 1
            return (TILES * w + at - TILES, at - TILES, n % 2) if 0 <= n < WINDOWS and at >= TILES else None

        def head(w, n, s, lag):
            at, w, n = s - lag, w - 1, n - 1
            while at < 0:
                at, w, n = at + SLOTS, w - 1, n - 1
            return (HH * w + at, at, w, n % 2) if 0 <= n < WINDOWS else None

        def ctx_tile(w, n, s):
            t, w, n = (s - 5, w + 1, n + 1) if s >= 5 else (TILES - 1, w, n)
            return (TILES * w + t, t) if (s >= 5 or s == 0) and 1 <= n < WINDOWS else None

        @block.sync
        def _(sp):
            sp.dma_start(lens_i[:, :], g["lens"].partition_broadcast(P)).then_inc(lens_in, 16)

            def load(tile, t, w):
                wait(sp, ctx_lo_done, tile - 1)
                sp.dma_start(ctx_raw[t % 2][:, :, :], g["ctx_t"][w % (B * CHUNKS), t]).then_inc(ctx_in[t % 2], 16)

            for t in range(TILES):
                load(t, t, 0)
            with sp.Fori(1, WINDOWS) as w:
                for t in range(TILES):
                    load(TILES * w + t, t, w)

        @block.gpsimd
        def _(pool):
            nc.gpsimd.iota(key_no[:, :], [[1, CHUNK]], base=0, channel_multiplier=0,
                           allow_small_or_imprecise_dtypes=True).then_inc(ready, 1)
            for i in range(2):
                nc.gpsimd.memset(v_hi[i][:, :, :, HD:VW], 1.0).then_inc(ready, 1)
                nc.gpsimd.memset(v_lo[i][:, :, :, HD:VW], 0.0).then_inc(ready, 1)
            nc.gpsimd.memset(o_acc[:, :, :, :], 0.0).then_inc(ready, 1)
            nc.gpsimd.memset(run_max[:, :, :], LOWEST).then_inc(ready, 1)

            def ctx_low(tile, t):
                pool.wait_ge(ctx_hi_done, tile + 1)
                nc.gpsimd.tensor_tensor(ctx_lo[t][:, :, :], ctx_raw[t % 2][:, :, :], ctx_hi[t][:, :, :].bitcast(F32),
                                        ALU.subtract).then_inc(ctx_lo_done, 1)

            def body(w, n, s):
                if found := k_tile(w, n, s, 1):
                    tile, t = found
                    pool.wait_ge(k_ms_done, tile + 1)
                    wait(pool, k_n_done, tile - 1)
                    nc.gpsimd.tensor_tensor(k_rinv[t % 2][:, :], k_ms[t % 2][:, :], half_neg[:, 0:HH],
                                            ALU.pow).then_inc(k_rinv_done, 1)
                if found := k_tile(w, n, s, 3):
                    tile, t = found
                    pool.wait_ge(k_hi_done, tile + 1)
                    nc.gpsimd.tensor_tensor(k_lh[t % 2][:, :, 0, :], k_n[t % 2][:, :, :], k_lh[t % 2][:, :, 1, :],
                                            ALU.subtract).then_inc(k_lo_done, 1)
                if (found := head(w, n, s, 3)) and found[1] % 2 == 0:
                    no, h, cw, _ = found
                    p, pair = HH // 2 * cw + h // 2, h // 2
                    pool.wait_ge(alpha_done, p + 1)
                    wait(pool, added_done, p - 1)
                    if n <= 1:
                        pool.wait_ge(ready, 7)
                    o_at = o_acc[:, cw // CHUNKS, h:h + 2, :]
                    nc.gpsimd.tensor_tensor(o_at, o_at, alpha[pair % 2][:, :].unsqueeze(2).to_broadcast([P, 2, VW]),
                                            ALU.mult).then_inc(scaled_done, 1)
                if found := ctx_tile(w, n, s):
                    ctx_low(*found)

            for t in range(TILES):
                ctx_low(t, t)
            windows(pool, body, SLOTS * (WINDOWS + 1) + 2)

        @block.scalar
        def _(act):
            def ctx_high(tile, t, w, n):
                act.wait_ge(ctx_in[t % 2], 16 * (2 * w + t // 2 + 1))
                if n > 0:
                    act.wait_ge(proj_done, SLOTS * w - TILES + t + 1)
                nc.scalar.activation(ctx_hi[t][:, :, :], ctx_raw[t % 2][:, :, :], ACT.Copy).then_inc(ctx_hi_done, 1)

            def body(w, n, s):
                slot = SLOTS * w + s
                if found := head(w, n, s, 4):
                    no, h, cw, par = found
                    act.wait_ge(p_tr_done, no + 1)
                    wait(act, pv_done, no - 1)
                    nc.scalar.activation(pt_hi[h % 2][:, :], p_turn[:, :], ACT.Copy).then_inc(pt_hi_done, 1)
                if found := k_tile(w, n, s, 1):
                    tile, t = found
                    act.wait_ge(proj_done, slot)
                    wait(act, k_ss_done, tile)
                    nc.scalar.activation(k_sq[:, :], bank[t][:, :], ACT.Square).then_inc(k_sq_done, 1)
                    wait(act, k_n_done, tile - 1)
                    nc.scalar.activation(k_raw[t % 2][:, :], bank[t][:, :], ACT.Copy).then_inc(k_raw_done, 1)
                if found := v_tile(w, n, s, 1):
                    tile, t, par = found
                    act.wait_ge(proj_done, slot)
                    wait(act, pv_done, HH * (w - (2 if s == 0 else 1)))
                    nc.scalar.activation(v_hi[par][:, t, :, 0:HD], bank[t][:, :].rearrange("p (h d) -> p h d", h=HH),
                                         ACT.Copy, scale=V_UP).then_inc(v_hi_done, 1)
                if found := k_tile(w, n, s, 3):
                    tile, t = found
                    act.wait_ge(k_n_done, tile + 1)
                    wait(act, k_tr_done, tile - 1)
                    nc.scalar.activation(k_lh[t % 2][:, :, 1, :], k_n[t % 2][:, :, :], ACT.Copy).then_inc(k_hi_done, 1)
                if found := head(w, n, s, 2):
                    no, h, cw, par = found
                    p, pair = HH // 2 * cw + h // 2, h // 2
                    if h % 2 == 0:
                        act.wait_ge(step_done, p + 1)
                        wait(act, scaled_done, p - 1)
                        nc.scalar.activation(alpha[pair % 2][:, :], max_step[pair % 2][:, :], ACT.Exp,
                                             scale=S_SCALE).then_inc(alpha_done, 1)
                    act.wait_ge(neg_max_done, p + 1)
                    nc.scalar.activation(probs[h % 4][:, :], probs[h % 4][:, :], ACT.Exp, scale=S_SCALE,
                                         bias=neg_max[pair % 2][:, h % 2:h % 2 + 1]).then_inc(p_done, 1)
                if found := ctx_tile(w, n, s):
                    ctx_high(*found, w + (1 if s else 0), 1)

            for t in range(TILES):
                ctx_high(t, t, 0, 0)
            windows(act, body, SLOTS * (WINDOWS + 1) + 3)

        @block.vector
        def _(dve):
            dve.wait_ge(lens_in, 16)
            nc.vector.tensor_copy(lens_f[:, :], lens_i[:, :]).then_inc(lens_done, 1)
            dve.wait_ge(lens_done, 1)
            for k in range(CHUNKS):
                nc.vector.tensor_scalar(left[:, :, k], lens_f[:, :], float(-CHUNK * k), None, ALU.add).then_inc(left_done, 1)
            dve.wait_ge(left_done, CHUNKS)
            dve.wait_ge(ready, 7)

            def body(w, n, s):
                slot = SLOTS * w + s
                if found := head(w, n, s, 1):
                    dve.wait_ge(s_done, found[0] + 1)
                    dve.wait_ge(mask_done, found[2] + 1)
                    wait(dve, p_tr_done, found[0] - 3)
                if found := head(w, n, s, 4):
                    no, h, cw, par = found
                    dve.wait_ge(pt_hi_done, no + 1)
                    nc.vector.tensor_tensor(pt_lo[h % 2][:, :], p_turn[:, :], pt_hi[h % 2][:, :],
                                            ALU.subtract).then_inc(pt_lo_done, 1)
                if found := head(w, n, s, 1):
                    no, h, cw, par = found
                    p, pair = HH // 2 * cw + h // 2, h // 2
                    nc.vector.tensor_tensor_reduce(probs[h % 4][:, :], scores[:, :], mask[:, :], 1.0, LOWEST, ALU.add,
                                                   ALU.max, chunk_max[:, h % 4:h % 4 + 1]).then_inc(s_max_done, 1)
                    if h % 2 == 1:
                        u, two = cw // CHUNKS, slice(h - 1, h + 1)
                        dve.wait_ge(s_max_done, no + 1)
                        wait(dve, kept_done, p)
                        nc.vector.tensor_tensor(new_max[pair % 2][:, :], run_max[:, u, two],
                                                chunk_max[:, (h - 1) % 4:(h - 1) % 4 + 2], ALU.max).then_inc(new_max_done, 1)
                        dve.wait_ge(new_max_done, p + 1)
                        wait(dve, p_done, 2 * p - 2)
                        nc.vector.tensor_scalar(neg_max[pair % 2][:, :], new_max[pair % 2][:, :], -S_SCALE, LN_P_UP,
                                                ALU.mult, ALU.add).then_inc(neg_max_done, 1)
                        wait(dve, alpha_done, p - 1)
                        nc.vector.tensor_tensor(max_step[pair % 2][:, :], run_max[:, u, two], new_max[pair % 2][:, :],
                                                ALU.subtract).then_inc(step_done, 1)
                        dve.wait_ge(step_done, p + 1)
                        nc.vector.tensor_tensor(run_max[:, u, two], run_max[:, u, two], new_max[pair % 2][:, :],
                                                ALU.max).then_inc(kept_done, 1)
                if s == 0 and 1 <= n <= WINDOWS:
                    wait(dve, s_max_done, HH * (w - 1))
                    at = (w - 1) % (B * CHUNKS)
                    nc.vector.tensor_scalar(mask[:, :], key_no[:, :], left[:, :, :].rearrange("p b k -> p (b k)")[:, bass.ds(at, 1)],
                                            NEG, ALU.is_ge, ALU.mult).then_inc(mask_done, 1)
                if found := k_tile(w, n, s, 5):
                    tile, t = found
                    par = (n - (1 if s < 5 else 0)) % 2
                    dve.wait_ge(k_tr_done, tile + 1)
                    wait(dve, s_done, HH * (w - (2 if s < 5 else 1)))
                    nc.vector.tensor_copy(kt[par][:, :, t * P:(t + 1) * P],
                                          k_turn[:, :].rearrange("p (h q) -> p h q", h=HH)).then_inc(kt_done, 1)
                if (found := head(w, n, s, 5)) and found[1] % 2 == 1:
                    no, h, cw, par = found
                    p, pair = HH // 2 * cw + h // 2, h // 2
                    dve.wait_ge(pv_done, no + 1)
                    dve.wait_ge(scaled_done, p + 1)
                    o_at = o_acc[:, cw // CHUNKS, h - 1:h + 1, :]
                    nc.vector.tensor_tensor(o_at, o_at, o_pair[pair % 2].rearrange("p (h v) -> p h v", h=2),
                                            ALU.add).then_inc(added_done, 1)
                if found := k_tile(w, n, s, 1):
                    tile, t = found
                    dve.wait_ge(k_sq_done, tile + 1)
                    wait(dve, k_ms_done, tile)
                    nc.vector.tensor_reduce(k_ss[:, :], k_sq[:, :].rearrange("p (h d) -> p h d", h=HH), AX_X,
                                            ALU.add).then_inc(k_ss_done, 1)
                if found := v_tile(w, n, s, 1):
                    tile, t, par = found
                    dve.wait_ge(v_hi_done, tile + 1)
                    nc.vector.scalar_tensor_tensor(v_lo[par][:, t, :, 0:HD], bank[t][:, :].rearrange("p (h d) -> p h d", h=HH),
                                                   V_UP, v_hi[par][:, t, :, 0:HD], ALU.mult,
                                                   ALU.subtract).then_inc(v_lo_done, 1)
                if found := k_tile(w, n, s, 1):
                    tile, t = found
                    dve.wait_ge(k_ss_done, tile + 1)
                    wait(dve, k_rinv_done, tile - 1)
                    nc.vector.tensor_scalar(k_ms[t % 2][:, :], k_ss[:, :], K_UP ** -2 / HD, K_UP ** -2 * RMS_EPS,
                                            ALU.mult, ALU.add).then_inc(k_ms_done, 1)
                if found := k_tile(w, n, s, 2):
                    tile, t = found
                    dve.wait_ge(k_rinv_done, tile + 1)
                    dve.wait_ge(k_raw_done, tile + 1)
                    wait(dve, k_lo_done, tile - 1)
                    nc.vector.tensor_tensor(k_n[t % 2][:, :, :], k_raw[t % 2][:, :].rearrange("p (h d) -> p h d", h=HH),
                                            k_rinv[t % 2][:, :].unsqueeze(2).to_broadcast([P, HH, HD]),
                                            ALU.mult).then_inc(k_n_done, 1)

            windows(dve, body, SLOTS * (WINDOWS + 1) + 4)

        @block.tensor
        def _(pe):
            pe.wait_ge(ready, 7)

            def body(w, n, s):
                slot = SLOTS * w + s
                if n < WINDOWS:
                    t, half = s % TILES, w // (B * CHUNKS)
                    if s < TILES:
                        pe.wait_ge(ctx_lo_done, TILES * w + t + 1)
                        wait(pe, v_lo_done, TILES * (w - 1) + t + 1)
                        w_hi, w_lo = g["wk_hi"], g["wk_lo"]
                    else:
                        pe.wait_ge(k_raw_done, TILES * w + t + 1)
                        w_hi, w_lo = g["wv_hi"], g["wv_lo"]
                    project(nc, bank[t][:, :], [ctx_hi[t][:, k, :] for k in range(KD)],
                            [ctx_lo[t][:, k, :] for k in range(KD)],
                            [w_hi[:, k, bass.ds(half * 512, 512)] for k in range(KD)],
                            [w_lo[:, k, bass.ds(half * 512, 512)] for k in range(KD)]).then_inc(proj_done, 1)
                if found := head(w, n, s, 0):
                    no, h, cw, par = found
                    pe.wait_ge(kt_done, TILES * (cw + 1))
                    wait(pe, s_max_done, no)
                    for i in range(2):
                        mm = nc.tensor.matmul(scores[:, :], q_st[:, cw // CHUNKS, i, h, :], kt[par][:, h, :],
                                              start=(i == 0), stop=(i == 1))
                    mm.then_inc(s_done, 1)
                if found := head(w, n, s, 3):
                    no, h, cw, par = found
                    pe.wait_ge(p_done, no + 1)
                    wait(pe, pt_lo_done, no)
                    for k in range(TILES):
                        mm = nc.tensor.transpose(p_turn[:, k * P:(k + 1) * P], probs[h % 4][:, k * P:(k + 1) * P],
                                                 ident[:, :])
                    mm.then_inc(p_tr_done, 1)
                if found := k_tile(w, n, s, 4):
                    tile, t = found
                    pe.wait_ge(k_lo_done, tile + 1)
                    wait(pe, kt_done, tile)
                    for h in range(HH):
                        mm = nc.tensor.transpose(k_turn[:, h * P:(h + 1) * P],
                                                 k_lh[t % 2][:, h, :, :].rearrange("p a d -> p (a d)"), ident16[:, :])
                    mm.then_inc(k_tr_done, 1)
                if found := head(w, n, s, 4):
                    no, h, cw, par = found
                    pair = h // 2
                    pe.wait_ge(pt_lo_done, no + 1)
                    pe.wait_ge(v_lo_done, TILES * (cw + 1))
                    if h % 2 == 0:
                        wait(pe, added_done, HH // 2 * cw + pair)
                    to = o_pair[pair % 2][:, (h % 2) * VW:(h % 2 + 1) * VW]
                    for k in range(TILES):
                        at = slice(k * P, (k + 1) * P)
                        nc.tensor.matmul(to, pt_hi[h % 2][:, at], v_hi[par][:, k, h, :], start=(k == 0), stop=False)
                        nc.tensor.matmul(to, pt_hi[h % 2][:, at], v_lo[par][:, k, h, :], start=False, stop=False)
                        mm = nc.tensor.matmul(to, pt_lo[h % 2][:, at], v_hi[par][:, k, h, :], start=False,
                                              stop=(k == TILES - 1))
                    mm.then_inc(pv_done, 1)

            windows(pe, body, SLOTS * (WINDOWS + 1) + 3)


def layer_norm(nc, sems, sb, c, tag, resid, half_neg, banks):
    stats = sb(tag + "_stats", [P, B, 6], F32, c)
    mean_var = sb(tag + "_mean_var", [P, B, 2], F32, c)
    rstd = sb(tag + "_rstd", [P, B], F32, c)
    var_eps = sb(tag + "_var_eps", [P, B], F32, c)
    xn = sb(tag + "_xn", [P, B, D], F32, c)
    stat, agg, v_eps, rs, x_n = sems(c, " ".join(tag + "_" + n for n in "stat agg v_eps rs x_n".split()))

    def vector(dve):
        for b in range(B):
            nc.vector.bn_stats(stats[:, b, :], resid[:, b, :]).then_inc(stat, 1)
        for b in range(B):
            dve.wait_ge(stat, b + 1)
            nc.vector.bn_aggr(mean_var[:, b, :], stats[:, b, :]).then_inc(agg, 1)
        dve.wait_ge(rs, 1)
        for b in range(B):
            nc.vector.tensor_scalar(xn[:, b, :], resid[:, b, :], mean_var[:, b, 0:1], rstd[:, b:b + 1],
                                    ALU.subtract, ALU.mult).then_inc(x_n, 1)

    def gpsimd(pool):
        pool.wait_ge(agg, B)
        nc.gpsimd.tensor_scalar(var_eps[:, :], mean_var[:, :, 1], LN_EPS, None, ALU.add).then_inc(v_eps, 1)
        pool.wait_ge(v_eps, 1)
        nc.gpsimd.tensor_tensor(rstd[:, :], var_eps[:, :], half_neg[:, 0:B], ALU.pow).then_inc(rs, 1)

    return xn, vector, gpsimd, x_n


def turn_rows(nc, sems, sb, c, tag, rows, rows_done, ident, banks):
    xt_hi, xt_lo = (sb(tag + n, [P, KD, B * P], F32R, c) for n in ("_xt_hi", "_xt_lo"))
    x_tr, x_hi, x_lo = sems(c, " ".join(tag + n for n in ("_x_tr", "_x_hi", "_x_lo")))

    def tensor(pe):
        for b in range(B):
            pe.wait_ge(rows_done, b + 1)
            for k in range(KD):
                mm = nc.tensor.transpose(banks[b][:, k * P:(k + 1) * P], rows[:, b, k * P:(k + 1) * P], ident[:, :])
            mm.then_inc(x_tr, 1)

    def scalar(act):
        for b in range(B):
            act.wait_ge(x_tr, b + 1)
            nc.scalar.activation(xt_hi[:, :, b * P:(b + 1) * P], banks[b][:, :].rearrange("p (k q) -> p k q", k=KD),
                                 ACT.Copy).then_inc(x_hi, 1)

    def vector(dve):
        for b in range(B):
            dve.wait_ge(x_hi, b + 1)
            nc.vector.tensor_tensor(xt_lo[:, :, b * P:(b + 1) * P], banks[b][:, :].rearrange("p (k q) -> p k q", k=KD),
                                    xt_hi[:, :, b * P:(b + 1) * P].bitcast(F32), ALU.subtract).then_inc(x_lo, 1)

    return xt_hi, xt_lo, tensor, scalar, vector, x_lo


def output_projection(nc, sems, sb, bank, g, tag, o_acc, weights, bias, then_split=None):
    with ExitStack() as c:
        resid, ident = g["resid"], g["ident"]
        rec, rec_up = (sb(tag + n, [P, UNITS, HH], F32, c) for n in ("_rec", "_rec_up"))
        o_n = [sb(f"{tag}_o_n{i}", [P, HALVES, HH, HD], F32, c) for i in range(2)]
        ot_hi = [sb(f"{tag}_ot_hi{i}", [P, E // P, P], F32R, c) for i in range(2)]
        ot_lo = [sb(f"{tag}_ot_lo{i}", [P, E // P, P], F32R, c) for i in range(2)]
        w_hi, w_lo = (sb(tag + n, [P, E // P, D], F32R, c) for n in ("_w_hi", "_w_lo"))
        raws = 4
        raw = [sb(f"{tag}_raw{i}", [P, 2 * D], F32, c) for i in range(raws)]
        own = E // P // 2
        extra = then_split[0].shape[1] // (2 * D) * KD if then_split else 0
        if bias is not None:
            bias_rows = sb(tag + "_bias", [P, D], F32, c)
        w_in = sems(c, " ".join(f"{tag}_w_in{i}" for i in range(raws)))
        b_in, wh_done, wl_done, rec_done, rec_up_done, on_done, tr_done, oh_done, ol_done, y_done, r_done = sems(
            c, " ".join(tag + n for n in "_b_in _wh _wl _rec_d _rec_up_d _on _tr _oh _ol _y _r".split()))
        block = c.enter_context(nc.Block())

        def piece(j):
            if j < own:
                src = weights.rearrange("(k p) n -> p k n", p=P)[:, 2 * j:2 * j + 2, :]
                return src, w_hi[:, 2 * j:2 * j + 2, :], w_lo[:, 2 * j:2 * j + 2, :]
            k, n = (j - own) % KD, (j - own) // KD
            at = slice(2 * D * n, 2 * D * (n + 1))
            return then_split[0].rearrange("(k p) n -> p k n", p=P)[:, k, at], then_split[1][:, k, at], then_split[2][:, k, at]

        def shaped(j, t):
            return t[:, :].rearrange("p (k n) -> p k n", k=2) if j < own else t[:, :]

        @block.sync
        def _(sp):
            if bias is not None:
                sp.dma_start(bias_rows[:, :], bias.partition_broadcast(P)).then_inc(b_in, 16)
            for j in range(own + extra):
                wait(sp, wl_done, j - raws + 1)
                sp.dma_start(shaped(j, raw[j % raws]), piece(j)[0]).then_inc(w_in[j % raws], 16)

        @block.scalar
        def _(act):
            def high(j):
                act.wait_ge(w_in[j % raws], 16 * (j // raws + 1))
                nc.scalar.activation(piece(j)[1], shaped(j, raw[j % raws]), ACT.Copy).then_inc(wh_done, 1)

            for j in range(own):
                high(j)
            for b in range(B):
                for i in range(2):
                    act.wait_ge(tr_done, 2 * b + i + 1)
                    if b >= 2:
                        act.wait_ge(y_done, b - 1)
                    nc.scalar.activation(ot_hi[b % 2][:, 4 * i:4 * i + 4, :],
                                         bank[2 * (b % 2) + i][:, :].rearrange("p (k q) -> p k q", k=4),
                                         ACT.Copy).then_inc(oh_done, 1)
            for j in range(own, own + extra):
                high(j)

        @block.vector
        def _(dve):
            def low(j):
                dve.wait_ge(wh_done, j + 1)
                nc.vector.tensor_tensor(piece(j)[2], shaped(j, raw[j % raws]), piece(j)[1].bitcast(F32),
                                        ALU.subtract).then_inc(wl_done, 1)

            def normed(b):
                wait(dve, tr_done, 2 * (b - 1))
                for half in range(HALVES):
                    u = half * B + b
                    nc.vector.tensor_tensor(o_n[b % 2][:, half, :, :], o_acc[:, u, :, 0:HD],
                                            rec_up[:, u, :].unsqueeze(2).to_broadcast([P, HH, HD]),
                                            ALU.mult).then_inc(on_done, 1)

            nc.vector.reciprocal(rec[:, :, :], o_acc[:, :, :, HD]).then_inc(rec_done, 1)
            dve.wait_ge(rec_done, 1)
            nc.vector.tensor_scalar(rec_up[:, :, :], rec[:, :, :], 1.0 / V_UP, None, ALU.mult).then_inc(rec_up_done, 1)
            dve.wait_ge(rec_up_done, 1)
            normed(0)
            for j in range(own):
                low(j)
            if bias is not None:
                dve.wait_ge(b_in, 16)
                for b in range(B):
                    nc.vector.tensor_tensor(resid[:, b, :], resid[:, b, :], bias_rows[:, :], ALU.add).then_inc(r_done, 1)
            for b in range(B):
                if b + 1 < B:
                    normed(b + 1)
                for i in range(2):
                    dve.wait_ge(oh_done, 2 * b + i + 1)
                    nc.vector.tensor_tensor(ot_lo[b % 2][:, 4 * i:4 * i + 4, :],
                                            bank[2 * (b % 2) + i][:, :].rearrange("p (k q) -> p k q", k=4),
                                            ot_hi[b % 2][:, 4 * i:4 * i + 4, :].bitcast(F32),
                                            ALU.subtract).then_inc(ol_done, 1)
                if b >= 1:
                    add(nc, dve, b - 1, y_done, resid, bank, r_done, bias)
            add(nc, dve, B - 1, y_done, resid, bank, r_done, bias)
            for j in range(own, own + extra):
                low(j)

        @block.tensor
        def _(pe):
            for b in range(B + 1):
                if b < B:
                    pe.wait_ge(on_done, 2 * (b + 1))
                    wait(pe, ol_done, 2 * (b - 1))
                    for i in range(2):
                        for k in range(4):
                            at = 4 * i + k
                            mm = nc.tensor.transpose(
                                bank[2 * (b % 2) + i][:, k * P:(k + 1) * P],
                                o_n[b % 2][:, :, :, :].rearrange("p a h d -> p (a h d)")[:, at * P:(at + 1) * P], ident[:, :])
                        mm.then_inc(tr_done, 1)
                if b >= 1:
                    m = b - 1
                    if m == 0:
                        pe.wait_ge(wl_done, own)
                    pe.wait_ge(ol_done, 2 * (m + 1))
                    n = E // P
                    project(nc, bank[4 + m][:, :], [ot_hi[m % 2][:, k, :] for k in range(n)],
                            [ot_lo[m % 2][:, k, :] for k in range(n)], [w_hi[:, k, :] for k in range(n)],
                            [w_lo[:, k, :] for k in range(n)]).then_inc(y_done, 1)


def add(nc, dve, b, y_done, resid, bank, r_done, bias):
    dve.wait_ge(y_done, b + 1)
    if bias is not None:
        dve.wait_ge(r_done, b + 1)
    nc.vector.tensor_tensor(resid[:, b, :], resid[:, b, :], bank[4 + b][:, :], ALU.add).then_inc(r_done, 1)


def self_attention(nc, sems, sb, bank, g, w_hi, w_lo, o_self):
    with ExitStack() as c:
        resid, ident, ident16 = g["resid"], g["ident"], g["ident16"]
        xn, ln_vector, ln_pool, x_n = layer_norm(nc, sems, sb, c, "self", resid, g["half_neg"], bank)
        xt_hi, xt_lo, turn_pe, turn_act, turn_dve, x_lo = turn_rows(nc, sems, sb, c, "self", xn, x_n, ident, bank)
        bias_rows = sb("self_bias", [P, 3, HALVES, HH * HD], F32, c)
        causal = sb("causal", [P, P], F32, c)
        ln_up = sb("ln_up", [P, 1], F32, c)
        biased = [sb(f"biased{i}", [P, HH, HD], F32, c) for i in range(3)]
        stack_q = [sb(f"stack_q{i}", [P, HH, 3, HD], F16, c) for i in range(2)]
        stack_k = [sb(f"stack_k{i}", [P, HH, 2, HD], F16, c) for i in range(2)]
        v_hi = [sb(f"self_v_hi{i}", [P, HH, VW], F16, c) for i in range(4)]
        v_lo = [sb(f"self_v_lo{i}", [P, HH, VW], F16, c) for i in range(4)]
        qt_a, qt_b, kt = ([sb(f"{n}{i}", [P, HH, P], F16, c) for i in range(2)] for n in ("qt_a", "qt_b", "self_kt"))
        probs = [sb(f"self_probs{i}", [P, HH, P], F32, c) for i in range(2)]
        row_max = [sb(f"row_max{i}", [P, HH], F32, c) for i in range(2)]
        pt_hi, pt_lo = (sb(n, [P, HH, P], F16, c) for n in ("self_pt_hi", "self_pt_lo"))
        b_in, ready, qkv_done, biased_done, hi_done, dup_done, lo_done = sems(
            c, "self_b_in self_ready qkv_done biased_done self_hi self_dup self_lo")
        qa_tr, qb_tr, k_tr, qa_kept, qb_kept, k_kept, s_done, masked, max_done, less_max, p_done = sems(
            c, "qa_tr qb_tr self_k_tr qa_kept qb_kept self_k_kept self_s masked self_max less_max self_p")
        p_tr, ph_done, pl_done, pv_done, o_done = sems(c, "self_p_tr self_ph self_pl self_pv self_o")
        turn_a, turn_b = bank[3], bank[6]
        a16, b16 = turn_a[:, :].bitcast(F16), turn_b[:, :].bitcast(F16)
        UP = V_UP
        scale = 1.0 / (UP * UP * 8.0)
        block = c.enter_context(nc.Block())

        @block.sync
        def _(sp):
            sp.dma_start(bias_rows[:, :, :, :].rearrange("p t a n -> p (t a n)"),
                         g["b_qkv"].partition_broadcast(P)).then_inc(b_in, 16)

        @block.gpsimd
        def _(pool):
            nc.gpsimd.memset(causal[:, :], 0.0).then_inc(ready, 1)
            nc.gpsimd.memset(ln_up[:, :], LN_P_UP).then_inc(ready, 1)
            for i in range(4):
                nc.gpsimd.memset(v_hi[i][:, :, HD:VW], 1.0).then_inc(ready, 1)
                nc.gpsimd.memset(v_lo[i][:, :, HD:VW], 0.0).then_inc(ready, 1)
            pool.wait_ge(ready, 10)
            nc.gpsimd.affine_select(out=causal[:, :], in_=causal[:, :], compare_op=ALU.is_ge, fill=-1e9 / scale, base=0,
                                    pattern=[[-1, P]], channel_multiplier=1).then_inc(ready, 1)
            ln_pool(pool)

        @block.tensor
        def _(pe):
            turn_pe(pe)
            for n in range(UNITS + 3):
                if n < UNITS:
                    b, half = n // HALVES, n % HALVES
                    if n == 0:
                        pe.wait_ge(x_lo, B)
                    for t in range(3):
                        wait(pe, biased_done, 3 * (n - 1) + t + 1)
                        at = slice((t * HALVES + half) * 512, (t * HALVES + half + 1) * 512)
                        project(nc, bank[t][:, :], [xt_hi[:, k, b * P:(b + 1) * P] for k in range(KD)],
                                [xt_lo[:, k, b * P:(b + 1) * P] for k in range(KD)],
                                [w_hi[:, k, at] for k in range(KD)], [w_lo[:, k, at] for k in range(KD)]).then_inc(qkv_done, 1)
                if 1 <= n <= UNITS:
                    m = n - 1
                    pe.wait_ge(lo_done, 3 * m + 2)
                    pe.wait_ge(dup_done, m + 1)
                    wait(pe, pl_done, 2 * (m - 2))
                    wait(pe, k_kept, m)
                    wait(pe, qb_kept, m)
                    for h in range(HH):
                        mm = nc.tensor.transpose(a16[:, h * P:(h + 1) * P],
                                                 stack_q[m % 2][:, h, 0:2, :].rearrange("p a d -> p (a d)"), ident16[:, :])
                    mm.then_inc(qa_tr, 1)
                    for h in range(HH):
                        mm = nc.tensor.transpose(b16[:, h * P:(h + 1) * P],
                                                 stack_q[m % 2][:, h, 1:3, :].rearrange("p a d -> p (a d)"), ident16[:, :])
                    mm.then_inc(qb_tr, 1)
                    pe.wait_ge(qa_kept, m + 1)
                    for h in range(HH):
                        mm = nc.tensor.transpose(a16[:, h * P:(h + 1) * P],
                                                 stack_k[m % 2][:, h, :, :].rearrange("p a d -> p (a d)"), ident16[:, :])
                    mm.then_inc(k_tr, 1)
                if 2 <= n <= UNITS + 1:
                    m = n - 2
                    pe.wait_ge(k_kept, m + 1)
                    pe.wait_ge(qb_kept, m + 1)
                    for h in range(HH):
                        if h % 4 == 0:
                            wait(pe, masked, 2 * (m - 1) + h // 4 + 1)
                        to = bank[4 + h // 4][:, (h % 4) * P:(h % 4 + 1) * P]
                        nc.tensor.matmul(to, qt_a[m % 2][:, h, :], kt[m % 2][:, h, :], start=True, stop=False)
                        mm = nc.tensor.matmul(to, qt_b[m % 2][:, h, :], kt[m % 2][:, h, :], start=False, stop=True)
                        if h % 4 == 3:
                            mm.then_inc(s_done, 1)
                if n >= 3:
                    m = n - 3
                    pe.wait_ge(p_done, m + 1)
                    for i, to in enumerate((turn_b, turn_a)):
                        last = min(n, UNITS)
                        pe.wait_ge(qb_kept if i == 0 else k_kept, last)
                        for k in range(4):
                            mm = nc.tensor.transpose(to[:, k * P:(k + 1) * P], probs[m % 2][:, 4 * i + k, :], ident[:, :])
                        mm.then_inc(p_tr, 1)
                    for i in range(2):
                        pe.wait_ge(pl_done, 2 * m + i + 1)
                        wait(pe, o_done, 2 * m + i)
                        for h in range(4 * i, 4 * i + 4):
                            to = bank[7][:, (h % 4) * VW:(h % 4 + 1) * VW]
                            nc.tensor.matmul(to, pt_hi[:, h, :], v_hi[m % 4][:, h, :], start=True, stop=False)
                            nc.tensor.matmul(to, pt_hi[:, h, :], v_lo[m % 4][:, h, :], start=False, stop=False)
                            mm = nc.tensor.matmul(to, pt_lo[:, h, :], v_hi[m % 4][:, h, :], start=False, stop=True)
                        mm.then_inc(pv_done, 1)

        @block.scalar
        def _(act):
            turn_act(act)
            act.wait_ge(ready, 11)
            for n in range(UNITS + 3):
                if n < UNITS:
                    for t, to in enumerate((stack_q[n % 2][:, :, 0, :], stack_k[n % 2][:, :, 1, :], v_hi[n % 4][:, :, 0:HD])):
                        act.wait_ge(biased_done, 3 * n + t + 1)
                        if t == 0:
                            wait(act, k_tr, n - 1)
                            wait(act, pv_done, 2 * (n - 3))
                        nc.scalar.activation(to, biased[t][:, :, :], ACT.Copy, scale=UP).then_inc(hi_done, 1)
                if 1 <= n <= UNITS:
                    m = n - 1
                    act.wait_ge(qb_tr, m + 1)
                    wait(act, s_done, 2 * (m - 1))
                    nc.scalar.activation(qt_b[m % 2][:, :, :].rearrange("p h q -> p (h q)"), b16[:, :],
                                         ACT.Copy).then_inc(qb_kept, 1)
                if 2 <= n <= UNITS + 1:
                    m = n - 2
                    act.wait_ge(less_max, m + 1)
                    nc.scalar.activation(probs[m % 2][:, :, :], probs[m % 2][:, :, :], ACT.Exp, scale=scale,
                                         bias=ln_up[:, 0:1]).then_inc(p_done, 1)
                if n >= 3:
                    m = n - 3
                    for i, src in enumerate((turn_b, turn_a)):
                        act.wait_ge(p_tr, 2 * m + i + 1)
                        wait(act, pv_done, 2 * m)
                        nc.scalar.activation(pt_hi[:, 4 * i:4 * i + 4, :].rearrange("p h q -> p (h q)"), src[:, :],
                                             ACT.Copy).then_inc(ph_done, 1)

        @block.vector
        def _(dve):
            ln_vector(dve)
            turn_dve(dve)
            dve.wait_ge(b_in, 16)
            dve.wait_ge(ready, 11)
            for n in range(UNITS + 3):
                if n < UNITS:
                    half = n % HALVES
                    for t in range(3):
                        dve.wait_ge(qkv_done, 3 * n + t + 1)
                        wait(dve, lo_done, 3 * (n - 1) + t + 1)
                        nc.vector.tensor_tensor(biased[t][:, :, :].rearrange("p h d -> p (h d)"), bank[t][:, :],
                                                bias_rows[:, t, half, :], ALU.add).then_inc(biased_done, 1)
                    for t, (to, hi) in enumerate(((stack_q[n % 2][:, :, 1, :], stack_q[n % 2][:, :, 0, :]),
                                                  (stack_k[n % 2][:, :, 0, :], stack_k[n % 2][:, :, 1, :]),
                                                  (v_lo[n % 4][:, :, 0:HD], v_hi[n % 4][:, :, 0:HD]))):
                        dve.wait_ge(hi_done, 3 * n + t + 1)
                        nc.vector.scalar_tensor_tensor(to, biased[t][:, :, :], UP, hi, ALU.mult,
                                                       ALU.subtract).then_inc(lo_done, 1)
                        if t == 0:
                            nc.vector.tensor_copy(stack_q[n % 2][:, :, 2, :], hi).then_inc(dup_done, 1)
                if 1 <= n <= UNITS:
                    m = n - 1
                    dve.wait_ge(qa_tr, m + 1)
                    wait(dve, s_done, 2 * (m - 1))
                    nc.vector.tensor_copy(qt_a[m % 2][:, :, :].rearrange("p h q -> p (h q)"), a16[:, :]).then_inc(qa_kept, 1)
                    dve.wait_ge(k_tr, m + 1)
                    nc.vector.tensor_copy(kt[m % 2][:, :, :].rearrange("p h q -> p (h q)"), a16[:, :]).then_inc(k_kept, 1)
                if 2 <= n <= UNITS + 1:
                    m = n - 2
                    for i in range(2):
                        dve.wait_ge(s_done, 2 * m + i + 1)
                        wait(dve, p_tr, 2 * (m - 1))
                        nc.vector.tensor_tensor(probs[m % 2][:, 4 * i:4 * i + 4, :],
                                                bank[4 + i][:, :].rearrange("p (h q) -> p h q", h=4),
                                                causal[:, :].unsqueeze(1).to_broadcast([P, 4, P]), ALU.add).then_inc(masked, 1)
                    dve.wait_ge(masked, 2 * (m + 1))
                    nc.vector.tensor_reduce(row_max[m % 2][:, :], probs[m % 2][:, :, :], AX_X, ALU.max).then_inc(max_done, 1)
                    dve.wait_ge(max_done, m + 1)
                    nc.vector.tensor_tensor(probs[m % 2][:, :, :], probs[m % 2][:, :, :],
                                            row_max[m % 2][:, :].unsqueeze(2).to_broadcast([P, HH, P]),
                                            ALU.subtract).then_inc(less_max, 1)
                if n >= 3:
                    m = n - 3
                    for i, src in enumerate((turn_b, turn_a)):
                        dve.wait_ge(ph_done, 2 * m + i + 1)
                        nc.vector.tensor_tensor(pt_lo[:, 4 * i:4 * i + 4, :].rearrange("p h q -> p (h q)"), src[:, :],
                                                pt_hi[:, 4 * i:4 * i + 4, :].rearrange("p h q -> p (h q)"),
                                                ALU.subtract).then_inc(pl_done, 1)
                    u = (m % HALVES) * B + m // HALVES
                    for i in range(2):
                        dve.wait_ge(pv_done, 2 * m + i + 1)
                        nc.vector.tensor_copy(o_self[:, u, 4 * i:4 * i + 4, :],
                                              bank[7][:, 0:4 * VW].rearrange("p (h v) -> p h v", h=4)).then_inc(o_done, 1)


QMAX = 32767.0
MIN_SCALE = 1e-12
ROUND = 1.5 * 2.0 ** 23


def feed_forward(nc, sems, sb, bank, g, out):
    I16, U16 = mybir.dt.int16, mybir.dt.uint16
    with ExitStack() as c:
        resid, ident = g["resid"], g["ident"]
        up_raw = sb("up_raw", [P, KF, B * P], F32, c)
        gate_raw = sb("gate_raw", [P, KF, B * P], F32, c)
        wd_hi, wd_lo = (sb(n, [P, KF, D], F32R, c) for n in ("wd_hi", "wd_lo"))
        top2 = sb("top2", [P, 2], F32, c)
        x_scale = sb("x_scale", [P, 1], F32, c)
        ffn_in(nc, sems, sb, bank, g, up_raw, gate_raw, wd_hi, wd_lo, top2, x_scale)
        ffn_out(nc, sems, sb, bank, g, up_raw, gate_raw, wd_hi, wd_lo, top2, x_scale, out)


def scale_of(nc, dve, top, times, to, inverse, tmp, done, at):
    nc.vector.tensor_scalar(tmp, top, times, 1.0 / QMAX, ALU.mult, ALU.mult).then_inc(done, 1)
    dve.wait_ge(done, at + 1)
    nc.vector.tensor_scalar(to, tmp, MIN_SCALE, None, ALU.max).then_inc(done, 1)
    dve.wait_ge(done, at + 2)
    nc.vector.reciprocal(inverse, to).then_inc(done, 1)
    dve.wait_ge(done, at + 3)
    return at + 3


def ffn_in(nc, sems, sb, bank, g, up_raw, gate_raw, wd_hi, wd_lo, top2, x_scale):
    I16 = mybir.dt.int16
    NB = D // BLOCK
    PIECES = 3 * KF
    with ExitStack() as c:
        resid, ident = g["resid"], g["ident"]
        xn, ln_vector, ln_pool, x_n = layer_norm(nc, sems, sb, c, "ffn", resid, g["half_neg"], bank)
        x_top, x_gtop, x_tmp, x_inv = (sb(n, [P, 1], F32, c) for n in ("x_top", "x_gtop", "x_tmp", "x_inv"))
        xi = sb("xi", [P, B, D], I16, c)
        xf = sb("xf", [P, B, D], F32, c)
        rows_done, top_done, all_done, sc_done, xi_done = sems(c, "rows_done top_done all_done sc_done xi_done")
        xt_hi, xt_lo, turn_pe, turn_act, turn_dve, x_lo = turn_rows(nc, sems, sb, c, "ffn", xf, rows_done, ident, bank)
        raws = 4
        raw = [sb(f"ffn_raw{i}", [P, NB, BLOCK], F32, c) for i in range(raws)]
        w_top = [sb(f"w_top{i}", [P, NB], F32, c) for i in range(2)]
        w_sc = [sb(f"w_sc{i}", [P, NB], F32, c) for i in range(2)]
        w_inv = [sb(f"w_inv{i}", [P, NB], F32, c) for i in range(2)]
        w_div = [sb(f"w_div{i}", [P, NB, BLOCK], F32, c) for i in range(2)]
        w_int = [sb(f"w_int{i}", [P, NB, BLOCK], F32, c) for i in range(2)]
        w_deq = [sb(f"w_deq{i}", [P, NB, BLOCK], F32, c) for i in range(2)]
        wt_hi = [sb(f"wt_hi{i}", [P, KD, P], F32R, c) for i in range(2)]
        wt_lo = [sb(f"wt_lo{i}", [P, KD, P], F32R, c) for i in range(2)]
        tops = sb("tops", [P, 2, KF], F32, c)
        w_in = sems(c, " ".join(f"ffn_w_in{i}" for i in range(raws)))
        wtop_done, wsc_done, winv_done, wdiv_done, wint_done, wdeq_done, wtr_done, whi_done, wlo_done = sems(
            c, "wtop_done wsc_done winv_done wdiv_done wint_done wdeq_done wtr_done whi_done wlo_done")
        y_done, kept_done, tops_done, mine_done, both_done = sems(c, "ffn_y ffn_kept tops_done mine_done both_done")
        top_mine = sb("top_mine", [P, 2], F32, c)
        block = c.enter_context(nc.Block())
        LIN = 2 * KF

        def source(j):
            if j < LIN:
                return (g["w_up"], g["w_gate"])[j // KF][(j % KF) * P:(j % KF + 1) * P, :]
            ot, ci = (j - LIN) // 3, (j - LIN) % 3
            return g["w_down"][ot * P:(ot + 1) * P, ci * D:(ci + 1) * D]

        def parts(j):
            if j < LIN:
                return wt_hi[j % 2][:, :, :], wt_lo[j % 2][:, :, :]
            ot, ci = (j - LIN) // 3, (j - LIN) % 3
            at = (slice(None), slice(KD * ci, KD * (ci + 1)), slice(ot * P, (ot + 1) * P))
            return wd_hi[at], wd_lo[at]

        @block.sync
        def _(sp):
            for j in range(PIECES):
                wait(sp, wdiv_done, j - raws + 1)
                sp.dma_start(raw[j % raws][:, :, :].rearrange("p a i -> p (a i)"), source(j)).then_inc(w_in[j % raws], 16)

        @block.gpsimd
        def _(pool):
            def divided(j):
                pool.wait_ge(winv_done, j + 1)
                wait(pool, wint_done, j - 1)
                nc.gpsimd.tensor_tensor(w_div[j % 2][:, :, :], raw[j % raws][:, :, :],
                                        w_inv[j % 2][:, :].unsqueeze(2).to_broadcast([P, NB, BLOCK]),
                                        ALU.mult).then_inc(wdiv_done, 1)

            def dequantised(j):
                pool.wait_ge(wint_done, j + 1)
                wait(pool, wtr_done, j - 1)
                nc.gpsimd.tensor_tensor(w_deq[j % 2][:, :, :], w_int[j % 2][:, :, :],
                                        w_sc[j % 2][:, :].unsqueeze(2).to_broadcast([P, NB, BLOCK]),
                                        ALU.mult).then_inc(wdeq_done, 1)

            ln_pool(pool)
            pool.wait_ge(top_done, 1)
            nc.gpsimd.partition_all_reduce(x_gtop[:, :], x_top[:, :], P, ABSMAX).then_inc(all_done, 1)
            for j in range(PIECES + 1):
                if j < PIECES:
                    divided(j)
                if j >= 1:
                    dequantised(j - 1)
                if j == LIN + 5:
                    pool.wait_ge(mine_done, 1)
                    nc.gpsimd.partition_all_reduce(top2[:, :], top_mine[:, :], P, ABSMAX).then_inc(both_done, 1)

        @block.vector
        def _(dve):
            ln_vector(dve)
            dve.wait_ge(x_n, B)
            nc.vector.tensor_reduce(x_top[:, :], xn[:, :, :].rearrange("p b d -> p (b d)"), AX_X, ALU.max,
                                    apply_absolute_value=True).then_inc(top_done, 1)
            dve.wait_ge(all_done, 1)
            scale_of(nc, dve, x_gtop[:, :], 1.0, x_scale[:, :], x_inv[:, :], x_tmp[:, :], sc_done, 0)
            for b in range(B):
                nc.vector.tensor_scalar(xi[:, b, :], xn[:, b, :], x_inv[:, 0:1], None, ALU.mult).then_inc(xi_done, 1)
            for b in range(B):
                dve.wait_ge(xi_done, b + 1)
                nc.vector.tensor_copy(xf[:, b, :], xi[:, b, :]).then_inc(rows_done, 1)
            turn_dve(dve)

            def tops_of(j):
                dve.wait_ge(w_in[j % raws], 16 * (j // raws + 1))
                nc.vector.tensor_reduce(w_top[j % 2][:, :], raw[j % raws][:, :, :], AX_X, ALU.max,
                                        apply_absolute_value=True).then_inc(wtop_done, 1)
                dve.wait_ge(wtop_done, j + 1)
                wait(dve, wdeq_done, j - 1)
                nc.vector.tensor_scalar(w_sc[j % 2][:, :], w_top[j % 2][:, :], 1.0 / 7.0, MIN_SCALE, ALU.mult,
                                        ALU.max).then_inc(wsc_done, 1)
                dve.wait_ge(wsc_done, j + 1)
                wait(dve, wdiv_done, j - 1)
                nc.vector.reciprocal(w_inv[j % 2][:, :], w_sc[j % 2][:, :]).then_inc(winv_done, 1)

            def rounded(j):
                dve.wait_ge(wdiv_done, j + 1)
                nc.vector.tensor_scalar(w_int[j % 2][:, :, :], w_div[j % 2][:, :, :], ROUND, ROUND, ALU.add,
                                        ALU.subtract).then_inc(wint_done, 1)

            def low(j):
                dve.wait_ge(whi_done, j + 1)
                hi, lo = parts(j)
                nc.vector.tensor_tensor(lo, bank[4 + j % 2][:, :].rearrange("p (k q) -> p k q", k=KD), hi.bitcast(F32),
                                        ALU.subtract).then_inc(wlo_done, 1)

            def top_of(j):
                dve.wait_ge(kept_done, j + 1)
                src = (up_raw, gate_raw)[j // KF][:, j % KF, :]
                nc.vector.tensor_reduce(tops[:, j // KF, j % KF:j % KF + 1], src, AX_X, ALU.max,
                                        apply_absolute_value=True).then_inc(tops_done, 1)
                if j == LIN - 1:
                    dve.wait_ge(tops_done, LIN)
                    nc.vector.tensor_reduce(top_mine[:, :], tops[:, :, :], AX_X, ALU.max).then_inc(mine_done, 1)

            for j in range(PIECES + 4):
                if j < PIECES:
                    tops_of(j)
                if 1 <= j <= PIECES:
                    rounded(j - 1)
                if 3 <= j <= PIECES + 2:
                    low(j - 3)
                if 4 <= j < LIN + 4:
                    top_of(j - 4)

        @block.scalar
        def _(act):
            turn_act(act)

            def high(j):
                act.wait_ge(wtr_done, j + 1)
                if j < LIN:
                    wait(act, y_done, j - 1)
                nc.scalar.activation(parts(j)[0], bank[4 + j % 2][:, :].rearrange("p (k q) -> p k q", k=KD),
                                     ACT.Copy).then_inc(whi_done, 1)

            for j in range(PIECES + 1):
                if j < PIECES:
                    high(j)
                if 1 <= j <= LIN:
                    m = j - 1
                    act.wait_ge(y_done, m + 1)
                    nc.scalar.activation((up_raw, gate_raw)[m // KF][:, m % KF, :], bank[m % 4][:, :],
                                         ACT.Copy).then_inc(kept_done, 1)

        @block.tensor
        def _(pe):
            turn_pe(pe)
            for j in range(PIECES + 1):
                if j < PIECES:
                    pe.wait_ge(wdeq_done, j + 1)
                    wait(pe, wlo_done, j - 1)
                    for k in range(KD):
                        mm = nc.tensor.transpose(bank[4 + j % 2][:, k * P:(k + 1) * P],
                                                 w_deq[j % 2][:, :, :].rearrange("p a i -> p (a i)")[:, k * P:(k + 1) * P],
                                                 ident[:, :])
                    mm.then_inc(wtr_done, 1)
                if 1 <= j <= LIN:
                    m = j - 1
                    if m == 0:
                        pe.wait_ge(x_lo, B)
                    pe.wait_ge(wlo_done, m + 1)
                    wait(pe, kept_done, m - 3)
                    project(nc, bank[m % 4][:, :], [wt_hi[m % 2][:, k, :] for k in range(KD)],
                            [wt_lo[m % 2][:, k, :] for k in range(KD)], [xt_hi[:, k, :] for k in range(KD)],
                            [xt_lo[:, k, :] for k in range(KD)]).then_inc(y_done, 1)


def ffn_out(nc, sems, sb, bank, g, up_raw, gate_raw, wd_hi, wd_lo, top2, x_scale, out):
    I16, U16 = mybir.dt.int16, mybir.dt.uint16
    UNIT = 1.0 / 65536.0
    with ExitStack() as c:
        resid = g["resid"]
        up_i, gate_i = (sb(n, [P, KF, B * P], I16, c) for n in ("up_i", "gate_i"))
        sig = [sb(f"sig{i}", [P, B * P], F32, c) for i in range(2)]
        sig_i = [sb(f"sig_i{i}", [P, B * P], U16, c) for i in range(2)]
        o_hi = [sb(f"o_hi{i}", [P, B * P], F32R, c) for i in range(3)]
        o_lo = [sb(f"o_lo{i}", [P, B * P], F32R, c) for i in range(3)]
        y = sb("y_rows", [P, B, D], F32, c)
        tmp2, scale2, inv2, raw_inv2 = (sb(n, [P, 2], F32, c) for n in ("tmp2", "scale2", "inv2", "raw_inv2"))
        tops3, tops4 = (sb(n, [P, KF], F32, c) for n in ("tops3", "tops4"))
        top3, gtop3, tmp3, scale3, inv3, raw_inv3 = (sb(n, [P, 1], F32, c) for n in
                                                     ("top3", "gtop3", "tmp3", "scale3", "inv3", "raw_inv3"))
        top4, gtop4, tmp4, scale4, inv4, raw_inv4, both_sc = (
            sb(n, [P, 1], F32, c) for n in ("top4", "gtop4", "tmp4", "scale4", "inv4", "raw_inv4", "both_sc"))
        sc_done, inv_done, up_done, gate_done, sig_done, sigi_done, act_done, t3_done, m3_done, g3_done = sems(
            c, "o_sc o_inv up_done gate_done sig_done sigi_done act_done t3_done m3_done g3_done")
        inv3_done, gi_done, prod_done, t4_done, m4_done, g4_done, inv4_done, oi_done, oh_done, ol_done, down_done, y_done, sent = sems(
            c, "inv3_done gi_done prod_done t4_done m4_done g4_done inv4_done oi_done oh_done ol_done down_done y_done sent")
        block = c.enter_context(nc.Block())

        @block.sync
        def _(sp):
            for b in range(B):
                sp.wait_ge(y_done, b + 1)
                sp.dma_start(out[b], y[:, b, :]).then_inc(sent, 16)
            sp.wait_ge(sent, 16 * B)

        @block.gpsimd
        def _(pool):
            pool.wait_ge(m3_done, 1)
            nc.gpsimd.partition_all_reduce(gtop3[:, :], top3[:, :], P, ABSMAX).then_inc(g3_done, 1)
            pool.wait_ge(m4_done, 1)
            nc.gpsimd.partition_all_reduce(gtop4[:, :], top4[:, :], P, ABSMAX).then_inc(g4_done, 1)

        @block.vector
        def _(dve):
            at = scale_of(nc, dve, top2[:, :], x_scale[:, 0:1], scale2[:, :], inv2[:, :], tmp2[:, :], sc_done, 0)
            nc.vector.tensor_scalar(raw_inv2[:, :], inv2[:, :], x_scale[:, 0:1], None, ALU.mult).then_inc(inv_done, 1)
            dve.wait_ge(inv_done, 1)

            def gate_int(k):
                nc.vector.tensor_scalar(gate_i[:, k, :], gate_raw[:, k, :], raw_inv2[:, 1:2], None,
                                        ALU.mult).then_inc(gate_done, 1)

            gate_int(0)
            for k in range(KF):
                if k + 1 < KF:
                    gate_int(k + 1)
                dve.wait_ge(sig_done, k + 1)
                nc.vector.tensor_scalar(sig_i[k % 2][:, :], sig[k % 2][:, :], 65536.0, None, ALU.mult).then_inc(sigi_done, 1)
                dve.wait_ge(sigi_done, k + 1)
                nc.vector.scalar_tensor_tensor(gate_raw[:, k, :], gate_i[:, k, :], scale2[:, 1:2], sig_i[k % 2][:, :],
                                               ALU.mult, ALU.mult).then_inc(act_done, 1)
                dve.wait_ge(act_done, k + 1)
                nc.vector.tensor_reduce(tops3[:, k:k + 1], gate_raw[:, k, :], AX_X, ALU.max,
                                        apply_absolute_value=True).then_inc(t3_done, 1)
            dve.wait_ge(t3_done, KF)
            nc.vector.tensor_reduce(top3[:, :], tops3[:, :], AX_X, ALU.max).then_inc(m3_done, 1)
            dve.wait_ge(g3_done, 1)
            at = scale_of(nc, dve, gtop3[:, :], UNIT, scale3[:, :], inv3[:, :], tmp3[:, :], sc_done, at)
            nc.vector.tensor_scalar(raw_inv3[:, :], inv3[:, :], UNIT, None, ALU.mult).then_inc(inv3_done, 1)
            dve.wait_ge(up_done, KF)
            for k in range(KF):
                dve.wait_ge(gi_done, k + 1)
                nc.vector.tensor_tensor(gate_raw[:, k, :], gate_i[:, k, :], up_i[:, k, :], ALU.mult).then_inc(prod_done, 1)
                dve.wait_ge(prod_done, k + 1)
                nc.vector.tensor_reduce(tops4[:, k:k + 1], gate_raw[:, k, :], AX_X, ALU.max,
                                        apply_absolute_value=True).then_inc(t4_done, 1)
            dve.wait_ge(t4_done, KF)
            nc.vector.tensor_reduce(top4[:, :], tops4[:, :], AX_X, ALU.max).then_inc(m4_done, 1)
            nc.vector.tensor_scalar(both_sc[:, :], scale3[:, :], scale2[:, 0:1], None, ALU.mult).then_inc(m4_done, 1)
            dve.wait_ge(m4_done, 2)
            dve.wait_ge(g4_done, 1)
            at = scale_of(nc, dve, gtop4[:, :], both_sc[:, 0:1], scale4[:, :], inv4[:, :], tmp4[:, :], sc_done, at)
            nc.vector.tensor_scalar(raw_inv4[:, :], inv4[:, :], both_sc[:, 0:1], None, ALU.mult).then_inc(inv4_done, 1)
            for k in range(KF):
                dve.wait_ge(oi_done, k + 1)
                wait(dve, down_done, k - 2)
                nc.vector.tensor_copy(o_hi[k % 3][:, :], up_i[:, k, :]).then_inc(oh_done, 1)
                dve.wait_ge(oh_done, k + 1)
                nc.vector.tensor_tensor(o_lo[k % 3][:, :], up_i[:, k, :], o_hi[k % 3][:, :].bitcast(F32),
                                        ALU.subtract).then_inc(ol_done, 1)
            for b in range(B):
                dve.wait_ge(down_done, KF)
                nc.vector.scalar_tensor_tensor(y[:, b, :], bank[b][:, :], scale4[:, 0:1], resid[:, b, :], ALU.mult,
                                               ALU.add).then_inc(y_done, 1)

        @block.scalar
        def _(act):
            act.wait_ge(inv_done, 1)
            for k in range(KF):
                act.wait_ge(gate_done, k + 1)
                wait(act, sigi_done, k - 1)
                nc.scalar.activation(sig[k % 2][:, :], gate_i[:, k, :], ACT.Sigmoid, scale=scale2[:, 1:2]).then_inc(sig_done, 1)
                nc.scalar.activation(up_i[:, k, :], up_raw[:, k, :], ACT.Copy, scale=raw_inv2[:, 0:1]).then_inc(up_done, 1)
            act.wait_ge(inv3_done, 1)
            for k in range(KF):
                nc.scalar.activation(gate_i[:, k, :], gate_raw[:, k, :], ACT.Copy, scale=raw_inv3[:, 0:1]).then_inc(gi_done, 1)
            act.wait_ge(inv4_done, 1)
            for k in range(KF):
                nc.scalar.activation(up_i[:, k, :], gate_raw[:, k, :], ACT.Copy, scale=raw_inv4[:, 0:1]).then_inc(oi_done, 1)

        @block.tensor
        def _(pe):
            for k in range(KF):
                pe.wait_ge(ol_done, k + 1)
                for b in range(B):
                    at = slice(b * P, (b + 1) * P)
                    nc.tensor.matmul(bank[b][:, :], o_hi[k % 3][:, at], wd_hi[:, k, :], start=(k == 0), stop=False)
                    nc.tensor.matmul(bank[b][:, :], o_hi[k % 3][:, at], wd_lo[:, k, :], start=False, stop=False)
                    mm = nc.tensor.matmul(bank[b][:, :], o_lo[k % 3][:, at], wd_hi[:, k, :], start=False, stop=(k == KF - 1))
                mm.then_inc(down_done, 1)


_OUTS = [((4, 128, 512), "float32")]


def kernel(**inputs):
    import numpy as _np
    import concourse.bacc as _bacc
    from concourse import mybir as _mybir
    from concourse.bass_utils import run_bass_kernel_spmd as _run

    def whole(name):
        return _np.ascontiguousarray(inputs[name])

    context = whole("ctx_1024").reshape(B, CHUNKS, TILES, P, KD, P).transpose(0, 1, 2, 5, 4, 3)
    laid = {
        "x": whole("x"),
        "ctx_t": _np.ascontiguousarray(context.reshape(B * CHUNKS, TILES, P, KD, P)),
        "lens": whole("_lenS2"),
        "wq": whole("L0_xattn_Wq"), "wk": whole("L0_xattn_Wk"), "wv": whole("L0_xattn_Wv"), "wo": whole("L0_xattn_Wo"),
        "q_norm": whole("L0_xattn_q_norm_w"), "k_norm": whole("L0_xattn_k_norm_w"),
        "w_qkv": whole("L0_attn_w_qkv").reshape(D, 3 * E), "b_qkv": whole("L0_attn_b_qkv").reshape(3 * E),
        "w_out": whole("L0_attn_w_out").reshape(E, D), "b_out": whole("L0_attn_b_out"),
        "w_gate": whole("L0_ffn_w_gate"), "w_up": whole("L0_ffn_w_up"), "w_down": whole("L0_ffn_w_down"),
    }
    nc = _bacc.Bacc("TRN2", target_bir_lowering=False, num_devices=1)
    args = [nc.dram_tensor(f"in_{n}_dram", a.shape, _mybir.dt.from_np(a.dtype), kind="ExternalInput").ap()
            for n, a in laid.items()]
    for i, (shape, dtype) in enumerate(_OUTS):
        args.append(nc.dram_tensor(f"out_{i}_dram", shape, _mybir.dt.from_np(_np.dtype(dtype)), kind="ExternalOutput").ap())
    program(nc, *args)
    r = _run(nc, [{f"in_{n}_dram": a for n, a in laid.items()}], core_ids=[0])
    return r.results[0]["out_0_dram"]
```

```python
from contextlib import ExitStack

import concourse.bass as bass
from concourse import mybir

F32 = mybir.dt.float32
F32R = mybir.dt.float32r
F16 = mybir.dt.float16
I32 = mybir.dt.int32
ALU = mybir.AluOpType
ACT = mybir.ActivationFunctionType
AX_X = mybir.AxisListType.X
ABSMAX = bass.bass_isa.ReduceOp.absmax

P = 128
B = 4
D = 512
KD = D // P
S = 2048
HEADS, HD = 16, 64
E = HEADS * HD
HH = 8
HALVES = HEADS // HH
CHUNK = 512
TILES = CHUNK // P
CHUNKS = S // CHUNK
WINDOWS = HALVES * B * CHUNKS
UNITS = HALVES * B
SLOTS = 2 * TILES
ALL_HEADS = WINDOWS * HH
VW = HD + 1
FF = 1536
KF = FF // P
BLOCK = 32
LN_EPS = 1e-5
RMS_EPS = 1e-5
RAWS = 4
Q_UP, K_UP, V_UP, P_UP = 32.0, 1024.0, 16.0, 4096.0
LN_P_UP = 8.317766166719343
S_SCALE = 1.0 / (Q_UP * K_UP * 8.0)
NEG = -1e9 / S_SCALE
LOWEST = -3e38


def wait(eng, semaphore, value):
    if not isinstance(value, int) or value > 0:
        eng.wait_ge(semaphore, value)


def program(nc, x, ctx_t, lens, wq, wk, wv, wo, q_norm, k_norm, w_qkv, b_qkv, w_out, b_out,
            w_gate, w_up, w_down, out):
    with ExitStack() as whole:
        def sb(name, shape, dt, ctx=whole):
            return ctx.enter_context(nc.sbuf_tensor(name, shape, dt))

        def sems(ctx, names):
            handles = [nc.alloc_semaphore(n) for n in names.split()]

            def give_back():
                nc.clear_and_free_semaphores(handles)
                nc.all_engine_barrier()

            ctx.callback(give_back)
            return handles

        bank = [whole.enter_context(nc.psum_tensor(f"bank{i}", [P, 512], F32)) for i in range(8)]

        resid = sb("resid", [P, B, D], F32)
        ident = sb("ident", [P, P], F32)
        ident16 = sb("ident16", [P, P], F16)
        half_neg = sb("half_neg", [P, 64], F32)
        cross = whole.enter_context(ExitStack())
        o_acc = sb("o_acc", [P, UNITS, HH, VW], F32, cross)
        stage_q = cross.enter_context(ExitStack())
        wk_hi, wk_lo = (sb(n, [P, KD, E], F32R, stage_q) for n in ("wk_hi", "wk_lo"))
        wv_hi, wv_lo = (sb(n, [P, KD, E], F32R, stage_q) for n in ("wv_hi", "wv_lo"))
        q_st = sb("q_st", [P, UNITS, 2, HH, P], F16, stage_q)

        prologue(nc, sems, sb, bank, locals())
        cross_attention(nc, sems, sb, bank, locals())
        stage_q.close()
        with ExitStack() as attn:
            w_qkv_hi, w_qkv_lo = (sb(n, [P, KD, 3 * E], F32R, attn) for n in ("w_qkv_hi", "w_qkv_lo"))
            output_projection(nc, sems, sb, bank, locals(), "cross_out", o_acc, wo, None, (w_qkv, w_qkv_hi, w_qkv_lo))
            self_attention(nc, sems, sb, bank, locals(), w_qkv_hi, w_qkv_lo, o_acc)
        output_projection(nc, sems, sb, bank, locals(), "self_out", o_acc, w_out, b_out)
        cross.close()
        feed_forward(nc, sems, sb, bank, locals(), out)


def prologue(nc, sems, sb, bank, g):
    with ExitStack() as c:
        resid, ident, ident16, half_neg = g["resid"], g["ident"], g["ident16"], g["half_neg"]
        w_hi = [None, g["wk_hi"], g["wv_hi"]]
        w_lo = [None, g["wk_lo"], g["wv_lo"]]
        w_hi[0], w_lo[0] = (sb(n, [P, KD, E], F32R, c) for n in ("wq_hi", "wq_lo"))
        raw = [sb(f"w_raw{i}", [P, E], F32, c) for i in range(RAWS)]
        stats = sb("stats", [P, B, 6], F32, c)
        mean_var = sb("mean_var", [P, B, 2], F32, c)
        rstd = sb("rstd", [P, B], F32, c)
        var_eps = sb("var_eps", [P, B], F32, c)
        xn = sb("xn", [P, B, D], F32, c)
        xt_hi, xt_lo = (sb(n, [P, KD, B * P], F32R, c) for n in ("xt_hi", "xt_lo"))
        qk_norm = sb("qk_norm", [P, 2, HD], F32, c)
        norm_w = sb("norm_w", [P, HD], F32, c)
        q_sq = sb("q_sq", [P, HH * HD], F32, c)
        q_raw = [sb(f"q_raw{i}", [P, HH * HD], F32, c) for i in range(2)]
        q_ss, q_ms, q_rinv = (sb(n, [P, UNITS, HH], F32, c) for n in ("q_ss", "q_ms", "q_rinv"))
        q_n, q_w = ([xn[:, 2 * j + i, :].rearrange("p (h d) -> p h d", h=HH) for i in range(2)] for j in range(2))
        stack = [sb(f"q_stack{i}", [P, HH, 3, HD], F16, c) for i in range(2)]
        x_in, norm_in = sems(c, "x_in norm_in")
        w_in = sems(c, " ".join(f"w_in{i}" for i in range(RAWS)))
        consts, stat, agg, v_eps, rs, x_n, x_tr, x_hi, x_lo = sems(
            c, "consts stat agg v_eps rs x_n x_tr x_hi x_lo")
        wh_done, wl_done, wnorm, zeroed = sems(c, "wh_done wl_done wnorm zeroed")
        qp_done, sq_done, raw_done, ss_done, ms_done, rinv_done, qn_done, qw_done = sems(
            c, "qp_done sq_done raw_done ss_done ms_done rinv_done qn_done qw_done")
        hi_done, hi2_done, lo_done, tr_a, tr_b, st_a, st_b = sems(
            c, "hi_done hi2_done lo_done tr_a tr_b st_a st_b")
        q_st = g["q_st"]
        t_a, t_b = (bank[4 + i][:, :].bitcast(F16) for i in range(2))
        block = c.enter_context(nc.Block())

        def unit(n):
            return n // HALVES, n % HALVES, (n % HALVES) * B + n // HALVES

        @block.sync
        def _(sp):
            for b in range(B):
                sp.dma_start(resid[:, b, :], g["x"][b]).then_inc(x_in, 16)
            for i, n in enumerate(("q_norm", "k_norm")):
                sp.dma_start(qk_norm[:, i, :], g[n].partition_broadcast(P)).then_inc(norm_in, 16)
            for j in range(3 * KD):
                wait(sp, wl_done, j - RAWS + 1)
                sp.dma_start(raw[j % RAWS][:, :], g[("wq", "wk", "wv")[j // KD]].rearrange(
                    "(k p) n -> p k n", p=P)[:, j % KD, :]).then_inc(w_in[j % RAWS], 16)

        @block.gpsimd
        def _(pool):
            nc.gpsimd.memset(ident[:, :], 0.0).then_inc(consts, 1)
            nc.gpsimd.memset(ident16[:, :], 0.0).then_inc(consts, 1)
            nc.gpsimd.memset(half_neg[:, :], -0.5).then_inc(consts, 1)
            nc.gpsimd.memset(g["o_acc"][:, :, :, :], 0.0).then_inc(zeroed, 1)
            pool.wait_ge(consts, 3)
            for t in (ident, ident16):
                nc.gpsimd.affine_select(out=t[:, :], in_=t[:, :], compare_op=ALU.not_equal, fill=1.0, base=0,
                                        pattern=[[-1, P]], channel_multiplier=1).then_inc(consts, 1)
            pool.wait_ge(agg, B)
            nc.gpsimd.tensor_scalar(var_eps[:, :], mean_var[:, :, 1], LN_EPS, None, ALU.add).then_inc(v_eps, 1)
            pool.wait_ge(v_eps, 1)
            nc.gpsimd.tensor_tensor(rstd[:, :], var_eps[:, :], half_neg[:, 0:B], ALU.pow).then_inc(rs, 1)
            pool.wait_ge(wnorm, 1)
            for n in range(UNITS + 2):
                if n < UNITS:
                    pool.wait_ge(ss_done, n + 1)
                    nc.gpsimd.tensor_scalar(q_ms[:, n, :], q_ss[:, n, :], 1.0 / HD, RMS_EPS, ALU.mult,
                                            ALU.add).then_inc(ms_done, 1)
                    pool.wait_ge(ms_done, n + 1)
                    nc.gpsimd.tensor_tensor(q_rinv[:, n, :], q_ms[:, n, :], half_neg[:, 0:HH],
                                            ALU.pow).then_inc(rinv_done, 1)
                if n >= 2:
                    m = n - 2
                    pool.wait_ge(qn_done, m + 1)
                    wait(pool, lo_done, m - 1)
                    nc.gpsimd.tensor_tensor(q_w[m % 2][:, :, :], q_n[m % 2][:, :, :],
                                            norm_w[:, :].unsqueeze(1).to_broadcast([P, HH, HD]),
                                            ALU.mult).then_inc(qw_done, 1)

        @block.tensor
        def _(pe):
            pe.wait_ge(consts, 5)
            for b in range(B):
                pe.wait_ge(x_n, b + 1)
                for k in range(KD):
                    mm = nc.tensor.transpose(bank[b][:, k * P:(k + 1) * P], xn[:, b, k * P:(k + 1) * P], ident[:, :])
                mm.then_inc(x_tr, 1)
            for n in range(UNITS + 4):
                if n < UNITS:
                    b, half, _ = unit(n)
                    if n == 0:
                        pe.wait_ge(wl_done, KD)
                        pe.wait_ge(x_lo, B)
                    wait(pe, raw_done, n - 3)
                    project(nc, bank[n % 4][:, :], [xt_hi[:, k, b * P:(b + 1) * P] for k in range(KD)],
                            [xt_lo[:, k, b * P:(b + 1) * P] for k in range(KD)],
                            [w_hi[0][:, k, half * 512:(half + 1) * 512] for k in range(KD)],
                            [w_lo[0][:, k, half * 512:(half + 1) * 512] for k in range(KD)]).then_inc(qp_done, 1)
                if n >= 4:
                    m = n - 4
                    pe.wait_ge(lo_done, m + 1)
                    pe.wait_ge(hi2_done, m + 1)
                    wait(pe, st_a, m)
                    for h in range(HH):
                        mm = nc.tensor.transpose(t_a[:, h * P:(h + 1) * P],
                                                 stack[m % 2][:, h, 0:2, :].rearrange("p a d -> p (a d)"), ident16[:, :])
                    mm.then_inc(tr_a, 1)
                    wait(pe, st_b, m)
                    for h in range(HH):
                        mm = nc.tensor.transpose(t_b[:, h * P:(h + 1) * P],
                                                 stack[m % 2][:, h, 1:3, :].rearrange("p a d -> p (a d)"), ident16[:, :])
                    mm.then_inc(tr_b, 1)

        @block.scalar
        def _(act):
            def weights_hi(pieces):
                for j in pieces:
                    i = j // KD
                    act.wait_ge(w_in[j % RAWS], 16 * (j // RAWS + 1))
                    nc.scalar.activation(w_hi[i][:, j % KD, :], raw[j % RAWS][:, :], ACT.Copy).then_inc(wh_done, 1)

            def finish(m):
                act.wait_ge(qw_done, m + 1)
                wait(act, tr_b, m - 1)
                nc.scalar.activation(stack[m % 2][:, :, 0, :], q_w[m % 2][:, :, :], ACT.Copy).then_inc(hi_done, 1)

            def keep(m):
                act.wait_ge(tr_b, m + 1)
                nc.scalar.activation(q_st[:, unit(m)[2], 1, :, :].rearrange("p h q -> p (h q)"), t_b[:, :],
                                     ACT.Copy).then_inc(st_b, 1)

            weights_hi(range(KD))
            for b in range(B):
                act.wait_ge(x_tr, b + 1)
                nc.scalar.activation(xt_hi[:, :, b * P:(b + 1) * P], bank[b][:, :].rearrange("p (k q) -> p k q", k=KD),
                                     ACT.Copy).then_inc(x_hi, 1)
            for n in range(UNITS + 5):
                if n >= 5:
                    keep(n - 5)
                if n < UNITS:
                    act.wait_ge(qp_done, n + 1)
                    wait(act, ss_done, n)
                    nc.scalar.activation(q_sq[:, :], bank[n % 4][:, :], ACT.Square).then_inc(sq_done, 1)
                    wait(act, qn_done, n - 1)
                    nc.scalar.activation(q_raw[n % 2][:, :], bank[n % 4][:, :], ACT.Copy).then_inc(raw_done, 1)
                if 3 <= n <= UNITS + 2:
                    finish(n - 3)
                if n < 2 * KD:
                    weights_hi([KD + n])

        @block.vector
        def _(dve):
            for b in range(B):
                dve.wait_ge(x_in, 16 * B)
                nc.vector.bn_stats(stats[:, b, :], resid[:, b, :]).then_inc(stat, 1)
            for b in range(B):
                dve.wait_ge(stat, b + 1)
                nc.vector.bn_aggr(mean_var[:, b, :], stats[:, b, :]).then_inc(agg, 1)
            dve.wait_ge(rs, 1)
            for b in range(B):
                nc.vector.tensor_scalar(xn[:, b, :], resid[:, b, :], mean_var[:, b, 0:1], rstd[:, b:b + 1],
                                        ALU.subtract, ALU.mult).then_inc(x_n, 1)
            dve.wait_ge(norm_in, 32)
            nc.vector.scalar_tensor_tensor(norm_w[:, :], qk_norm[:, 0, :], Q_UP, qk_norm[:, 1, :], ALU.mult,
                                           ALU.mult).then_inc(wnorm, 1)

            def weights_lo(pieces):
                for j in pieces:
                    i = j // KD
                    dve.wait_ge(wh_done, j + 1)
                    nc.vector.tensor_tensor(w_lo[i][:, j % KD, :], raw[j % RAWS][:, :],
                                            w_hi[i][:, j % KD, :].bitcast(F32), ALU.subtract).then_inc(wl_done, 1)

            def normed(m):
                dve.wait_ge(rinv_done, m + 1)
                dve.wait_ge(raw_done, m + 1)
                wait(dve, qw_done, m - 1)
                nc.vector.tensor_tensor(q_n[m % 2][:, :, :], q_raw[m % 2][:, :].rearrange("p (h d) -> p h d", h=HH),
                                        q_rinv[:, m, :].unsqueeze(2).to_broadcast([P, HH, HD]),
                                        ALU.mult).then_inc(qn_done, 1)

            def parts(m):
                dve.wait_ge(hi_done, m + 1)
                wait(dve, tr_b, m - 1)
                nc.vector.tensor_copy(stack[m % 2][:, :, 2, :], stack[m % 2][:, :, 0, :]).then_inc(hi2_done, 1)
                nc.vector.tensor_tensor(stack[m % 2][:, :, 1, :], q_w[m % 2][:, :, :], stack[m % 2][:, :, 0, :],
                                        ALU.subtract).then_inc(lo_done, 1)

            def keep(m):
                dve.wait_ge(tr_a, m + 1)
                nc.vector.tensor_copy(q_st[:, unit(m)[2], 0, :, :].rearrange("p h q -> p (h q)"),
                                      t_a[:, :]).then_inc(st_a, 1)

            weights_lo(range(KD))
            for b in range(B):
                dve.wait_ge(x_hi, b + 1)
                nc.vector.tensor_tensor(xt_lo[:, :, b * P:(b + 1) * P], bank[b][:, :].rearrange("p (k q) -> p k q", k=KD),
                                        xt_hi[:, :, b * P:(b + 1) * P].bitcast(F32), ALU.subtract).then_inc(x_lo, 1)
            for n in range(UNITS + 5):
                if n >= 5:
                    keep(n - 5)
                if 1 <= n <= UNITS:
                    normed(n - 1)
                if n < UNITS:
                    dve.wait_ge(sq_done, n + 1)
                    nc.vector.tensor_reduce(q_ss[:, n, :], q_sq[:, :].rearrange("p (h d) -> p h d", h=HH), AX_X,
                                            ALU.add).then_inc(ss_done, 1)
                if n < 2 * KD:
                    weights_lo([KD + n])
                if 3 <= n <= UNITS + 2:
                    parts(n - 3)


def project(nc, to, x_hi, x_lo, w_hi, w_lo):
    n = len(x_hi)
    for k in range(n):
        nc.tensor.matmul(to, x_hi[k], w_hi[k], start=(k == 0), stop=False)
        nc.tensor.matmul(to, x_hi[k], w_lo[k], start=False, stop=False)
        mm = nc.tensor.matmul(to, x_lo[k], w_hi[k], start=False, stop=(k == n - 1))
    return mm


def cross_attention(nc, sems, sb, bank, g):
    with ExitStack() as c:
        q_st, o_acc, ident, ident16, half_neg = (g[n] for n in ("q_st", "o_acc", "ident", "ident16", "half_neg"))
        ctx_raw = [sb(f"ctx_raw{i}", [P, KD, P], F32, c) for i in range(2)]
        ctx_hi = [sb(f"ctx_hi{i}", [P, KD, P], F32R, c) for i in range(TILES)]
        ctx_lo = [sb(f"ctx_lo{i}", [P, KD, P], F32R, c) for i in range(TILES)]
        k_sq = sb("k_sq", [P, HH * HD], F32, c)
        k_raw = [sb(f"k_raw{i}", [P, HH * HD], F32, c) for i in range(2)]
        k_ss = sb("k_ss", [P, HH], F32, c)
        k_ms = [sb(f"k_ms{i}", [P, HH], F32, c) for i in range(2)]
        k_rinv = [sb(f"k_rinv{i}", [P, HH], F32, c) for i in range(2)]
        k_n = [sb(f"k_n{i}", [P, HH, HD], F32, c) for i in range(2)]
        k_lh = [sb(f"k_lh{i}", [P, HH, 2, HD], F16, c) for i in range(2)]
        kt = [sb(f"kt{i}", [P, HH, CHUNK], F16, c) for i in range(2)]
        v_hi = [sb(f"v_hi{i}", [P, TILES, HH, VW], F16, c) for i in range(2)]
        v_lo = [sb(f"v_lo{i}", [P, TILES, HH, VW], F16, c) for i in range(2)]
        probs = [sb(f"probs{i}", [P, CHUNK], F32, c) for i in range(4)]
        pt_hi = [sb(f"pt_hi{i}", [P, CHUNK], F16, c) for i in range(2)]
        pt_lo = [sb(f"pt_lo{i}", [P, CHUNK], F16, c) for i in range(2)]
        key_no = sb("key_no", [P, CHUNK], F32, c)
        mask = sb("mask", [P, CHUNK], F32, c)
        lens_i = sb("lens_i", [P, B], I32, c)
        lens_f = sb("lens_f", [P, B], F32, c)
        left = sb("left", [P, B, CHUNKS], F32, c)
        chunk_max = sb("chunk_max", [P, 4], F32, c)
        run_max = sb("run_max", [P, UNITS, HH], F32, c)
        new_max = [sb(f"new_max{i}", [P, 2], F32, c) for i in range(2)]
        neg_max = [sb(f"neg_max{i}", [P, 2], F32, c) for i in range(2)]
        max_step = [sb(f"max_step{i}", [P, 2], F32, c) for i in range(2)]
        alpha = [sb(f"alpha{i}", [P, 2], F32, c) for i in range(2)]

        ctx_in = sems(c, "ctx_in0 ctx_in1")
        lens_in, ready, lens_done, left_done = sems(c, "lens_in ready lens_done left_done")
        ctx_hi_done, ctx_lo_done, proj_done = sems(c, "ctx_hi_done ctx_lo_done proj_done")
        k_sq_done, k_raw_done, k_ss_done, k_ms_done, k_rinv_done, k_n_done, k_hi_done, k_lo_done, k_tr_done, kt_done = sems(
            c, "k_sq_done k_raw_done k_ss_done k_ms_done k_rinv_done k_n_done k_hi_done k_lo_done k_tr_done kt_done")
        v_hi_done, v_lo_done, mask_done = sems(c, "v_hi_done v_lo_done mask_done")
        s_done, s_max_done, new_max_done, neg_max_done, step_done, kept_done = sems(
            c, "s_done s_max_done new_max_done neg_max_done step_done kept_done")
        p_done, p_tr_done, pt_hi_done, pt_lo_done, pv_done, alpha_done, scaled_done, added_done = sems(
            c, "p_done p_tr_done pt_hi_done pt_lo_done pv_done alpha_done scaled_done added_done")
        scores, p_turn, k_turn, o_new = bank[4], bank[5], bank[6][:, :].bitcast(F16), bank[7]
        o_pair = [o_new[:, 2 * i * VW:2 * (i + 1) * VW] for i in range(2)]
        block = c.enter_context(nc.Block())

        def windows(eng, body, last):
            for w in range(3):
                for s in range(SLOTS):
                    body(w, w, s)
            with eng.Fori(0, (WINDOWS - 4) // 2) as i:
                for p in range(2):
                    for s in range(SLOTS):
                        body(2 * i + 3 + p, 3 + p, s)
            for w in range(WINDOWS - 1, WINDOWS + 2):
                for s in range(SLOTS):
                    if SLOTS * w + s <= last:
                        body(w, w, s)

        def k_tile(w, n, s, lag):
            at = s - lag
            if at < 0:
                at, w, n = at + SLOTS, w - 1, n - 1
            return (TILES * w + at, at) if 0 <= n < WINDOWS and at < TILES else None

        def v_tile(w, n, s, lag):
            at = s - lag
            if at < 0:
                at, w, n = at + SLOTS, w - 1, n - 1
            return (TILES * w + at - TILES, at - TILES, n % 2) if 0 <= n < WINDOWS and at >= TILES else None

        def head(w, n, s, lag):
            at, w, n = s - lag, w - 1, n - 1
            while at < 0:
                at, w, n = at + SLOTS, w - 1, n - 1
            return (HH * w + at, at, w, n % 2) if 0 <= n < WINDOWS else None

        def ctx_tile(w, n, s):
            t, w, n = (s - 5, w + 1, n + 1) if s >= 5 else (TILES - 1, w, n)
            return (TILES * w + t, t) if (s >= 5 or s == 0) and 1 <= n < WINDOWS else None

        @block.sync
        def _(sp):
            sp.dma_start(lens_i[:, :], g["lens"].partition_broadcast(P)).then_inc(lens_in, 16)

            def load(tile, t, w):
                wait(sp, ctx_lo_done, tile - 1)
                sp.dma_start(ctx_raw[t % 2][:, :, :], g["ctx_t"][w % (B * CHUNKS), t]).then_inc(ctx_in[t % 2], 16)

            for t in range(TILES):
                load(t, t, 0)
            with sp.Fori(1, WINDOWS) as w:
                for t in range(TILES):
                    load(TILES * w + t, t, w)

        @block.gpsimd
        def _(pool):
            nc.gpsimd.iota(key_no[:, :], [[1, CHUNK]], base=0, channel_multiplier=0,
                           allow_small_or_imprecise_dtypes=True).then_inc(ready, 1)
            for i in range(2):
                nc.gpsimd.memset(v_hi[i][:, :, :, HD:VW], 1.0).then_inc(ready, 1)
                nc.gpsimd.memset(v_lo[i][:, :, :, HD:VW], 0.0).then_inc(ready, 1)
            nc.gpsimd.memset(run_max[:, :, :], LOWEST).then_inc(ready, 1)

            def ctx_low(tile, t):
                pool.wait_ge(ctx_hi_done, tile + 1)
                nc.gpsimd.tensor_tensor(ctx_lo[t][:, :, :], ctx_raw[t % 2][:, :, :], ctx_hi[t][:, :, :].bitcast(F32),
                                        ALU.subtract).then_inc(ctx_lo_done, 1)

            def body(w, n, s):
                if found := k_tile(w, n, s, 1):
                    tile, t = found
                    pool.wait_ge(k_ms_done, tile + 1)
                    wait(pool, k_n_done, tile - 1)
                    nc.gpsimd.tensor_tensor(k_rinv[t % 2][:, :], k_ms[t % 2][:, :], half_neg[:, 0:HH],
                                            ALU.pow).then_inc(k_rinv_done, 1)
                if found := k_tile(w, n, s, 3):
                    tile, t = found
                    pool.wait_ge(k_hi_done, tile + 1)
                    nc.gpsimd.tensor_tensor(k_lh[t % 2][:, :, 0, :], k_n[t % 2][:, :, :], k_lh[t % 2][:, :, 1, :],
                                            ALU.subtract).then_inc(k_lo_done, 1)
                if (found := head(w, n, s, 3)) and found[1] % 2 == 0:
                    no, h, cw, _ = found
                    p, pair = HH // 2 * cw + h // 2, h // 2
                    pool.wait_ge(alpha_done, p + 1)
                    wait(pool, added_done, p - 1)
                    if n <= 1:
                        pool.wait_ge(ready, 6)
                    o_at = o_acc[:, cw // CHUNKS, h:h + 2, :]
                    nc.gpsimd.tensor_tensor(o_at, o_at, alpha[pair % 2][:, :].unsqueeze(2).to_broadcast([P, 2, VW]),
                                            ALU.mult).then_inc(scaled_done, 1)
                if found := ctx_tile(w, n, s):
                    ctx_low(*found)

            for t in range(TILES):
                ctx_low(t, t)
            windows(pool, body, SLOTS * (WINDOWS + 1) + 2)

        @block.scalar
        def _(act):
            def ctx_high(tile, t, w, n):
                act.wait_ge(ctx_in[t % 2], 16 * (2 * w + t // 2 + 1))
                if n > 0:
                    act.wait_ge(proj_done, SLOTS * w - TILES + t + 1)
                nc.scalar.activation(ctx_hi[t][:, :, :], ctx_raw[t % 2][:, :, :], ACT.Copy).then_inc(ctx_hi_done, 1)

            def body(w, n, s):
                slot = SLOTS * w + s
                if found := head(w, n, s, 4):
                    no, h, cw, par = found
                    act.wait_ge(p_tr_done, no + 1)
                    wait(act, pv_done, no - 1)
                    nc.scalar.activation(pt_hi[h % 2][:, :], p_turn[:, :], ACT.Copy).then_inc(pt_hi_done, 1)
                if found := k_tile(w, n, s, 1):
                    tile, t = found
                    act.wait_ge(proj_done, slot)
                    wait(act, k_ss_done, tile)
                    nc.scalar.activation(k_sq[:, :], bank[t][:, :], ACT.Square).then_inc(k_sq_done, 1)
                    wait(act, k_n_done, tile - 1)
                    nc.scalar.activation(k_raw[t % 2][:, :], bank[t][:, :], ACT.Copy).then_inc(k_raw_done, 1)
                if found := v_tile(w, n, s, 1):
                    tile, t, par = found
                    act.wait_ge(proj_done, slot)
                    wait(act, pv_done, HH * (w - (2 if s == 0 else 1)))
                    nc.scalar.activation(v_hi[par][:, t, :, 0:HD], bank[t][:, :].rearrange("p (h d) -> p h d", h=HH),
                                         ACT.Copy, scale=V_UP).then_inc(v_hi_done, 1)
                if found := k_tile(w, n, s, 3):
                    tile, t = found
                    act.wait_ge(k_n_done, tile + 1)
                    wait(act, k_tr_done, tile - 1)
                    nc.scalar.activation(k_lh[t % 2][:, :, 1, :], k_n[t % 2][:, :, :], ACT.Copy).then_inc(k_hi_done, 1)
                if found := head(w, n, s, 2):
                    no, h, cw, par = found
                    p, pair = HH // 2 * cw + h // 2, h // 2
                    if h % 2 == 0:
                        act.wait_ge(step_done, p + 1)
                        wait(act, scaled_done, p - 1)
                        nc.scalar.activation(alpha[pair % 2][:, :], max_step[pair % 2][:, :], ACT.Exp,
                                             scale=S_SCALE).then_inc(alpha_done, 1)
                    act.wait_ge(neg_max_done, p + 1)
                    nc.scalar.activation(probs[h % 4][:, :], probs[h % 4][:, :], ACT.Exp, scale=S_SCALE,
                                         bias=neg_max[pair % 2][:, h % 2:h % 2 + 1]).then_inc(p_done, 1)
                if found := ctx_tile(w, n, s):
                    ctx_high(*found, w + (1 if s else 0), 1)

            for t in range(TILES):
                ctx_high(t, t, 0, 0)
            windows(act, body, SLOTS * (WINDOWS + 1) + 3)

        @block.vector
        def _(dve):
            dve.wait_ge(lens_in, 16)
            nc.vector.tensor_copy(lens_f[:, :], lens_i[:, :]).then_inc(lens_done, 1)
            dve.wait_ge(lens_done, 1)
            for k in range(CHUNKS):
                nc.vector.tensor_scalar(left[:, :, k], lens_f[:, :], float(-CHUNK * k), None, ALU.add).then_inc(left_done, 1)
            dve.wait_ge(left_done, CHUNKS)
            dve.wait_ge(ready, 6)

            def body(w, n, s):
                slot = SLOTS * w + s
                if (found := head(w, n, s, 5)) and found[1] % 2 == 1:
                    no, h, cw, par = found
                    p, pair = HH // 2 * cw + h // 2, h // 2
                    dve.wait_ge(pv_done, no + 1)
                    dve.wait_ge(scaled_done, p + 1)
                    o_at = o_acc[:, cw // CHUNKS, h - 1:h + 1, :]
                    nc.vector.tensor_tensor(o_at, o_at, o_pair[pair % 2].rearrange("p (h v) -> p h v", h=2),
                                            ALU.add).then_inc(added_done, 1)
                if found := head(w, n, s, 1):
                    dve.wait_ge(s_done, found[0] + 1)
                    dve.wait_ge(mask_done, found[2] + 1)
                    wait(dve, p_tr_done, found[0] - 3)
                if found := head(w, n, s, 4):
                    no, h, cw, par = found
                    dve.wait_ge(pt_hi_done, no + 1)
                    nc.vector.tensor_tensor(pt_lo[h % 2][:, :], p_turn[:, :], pt_hi[h % 2][:, :],
                                            ALU.subtract).then_inc(pt_lo_done, 1)
                if found := head(w, n, s, 1):
                    no, h, cw, par = found
                    p, pair = HH // 2 * cw + h // 2, h // 2
                    nc.vector.tensor_tensor_reduce(probs[h % 4][:, :], scores[:, :], mask[:, :], 1.0, LOWEST, ALU.add,
                                                   ALU.max, chunk_max[:, h % 4:h % 4 + 1]).then_inc(s_max_done, 1)
                    if h % 2 == 1:
                        u, two = cw // CHUNKS, slice(h - 1, h + 1)
                        dve.wait_ge(s_max_done, no + 1)
                        wait(dve, kept_done, p)
                        nc.vector.tensor_tensor(new_max[pair % 2][:, :], run_max[:, u, two],
                                                chunk_max[:, (h - 1) % 4:(h - 1) % 4 + 2], ALU.max).then_inc(new_max_done, 1)
                        dve.wait_ge(new_max_done, p + 1)
                        wait(dve, p_done, 2 * p - 2)
                        nc.vector.tensor_scalar(neg_max[pair % 2][:, :], new_max[pair % 2][:, :], -S_SCALE, LN_P_UP,
                                                ALU.mult, ALU.add).then_inc(neg_max_done, 1)
                        wait(dve, alpha_done, p - 1)
                        nc.vector.tensor_tensor(max_step[pair % 2][:, :], run_max[:, u, two], new_max[pair % 2][:, :],
                                                ALU.subtract).then_inc(step_done, 1)
                        dve.wait_ge(step_done, p + 1)
                        nc.vector.tensor_tensor(run_max[:, u, two], run_max[:, u, two], new_max[pair % 2][:, :],
                                                ALU.max).then_inc(kept_done, 1)
                if s == 0 and 1 <= n <= WINDOWS:
                    wait(dve, s_max_done, HH * (w - 1))
                    at = (w - 1) % (B * CHUNKS)
                    nc.vector.tensor_scalar(mask[:, :], key_no[:, :], left[:, :, :].rearrange("p b k -> p (b k)")[:, bass.ds(at, 1)],
                                            NEG, ALU.is_ge, ALU.mult).then_inc(mask_done, 1)
                if found := k_tile(w, n, s, 5):
                    tile, t = found
                    par = (n - (1 if s < 5 else 0)) % 2
                    dve.wait_ge(k_tr_done, tile + 1)
                    wait(dve, s_done, HH * (w - (2 if s < 5 else 1)))
                    nc.vector.tensor_copy(kt[par][:, :, t * P:(t + 1) * P],
                                          k_turn[:, :].rearrange("p (h q) -> p h q", h=HH)).then_inc(kt_done, 1)
                if found := k_tile(w, n, s, 1):
                    tile, t = found
                    dve.wait_ge(k_sq_done, tile + 1)
                    wait(dve, k_ms_done, tile)
                    nc.vector.tensor_reduce(k_ss[:, :], k_sq[:, :].rearrange("p (h d) -> p h d", h=HH), AX_X,
                                            ALU.add).then_inc(k_ss_done, 1)
                if found := v_tile(w, n, s, 1):
                    tile, t, par = found
                    dve.wait_ge(v_hi_done, tile + 1)
                    nc.vector.scalar_tensor_tensor(v_lo[par][:, t, :, 0:HD], bank[t][:, :].rearrange("p (h d) -> p h d", h=HH),
                                                   V_UP, v_hi[par][:, t, :, 0:HD], ALU.mult,
                                                   ALU.subtract).then_inc(v_lo_done, 1)
                if found := k_tile(w, n, s, 1):
                    tile, t = found
                    dve.wait_ge(k_ss_done, tile + 1)
                    wait(dve, k_rinv_done, tile - 1)
                    nc.vector.tensor_scalar(k_ms[t % 2][:, :], k_ss[:, :], K_UP ** -2 / HD, K_UP ** -2 * RMS_EPS,
                                            ALU.mult, ALU.add).then_inc(k_ms_done, 1)
                if found := k_tile(w, n, s, 2):
                    tile, t = found
                    dve.wait_ge(k_rinv_done, tile + 1)
                    dve.wait_ge(k_raw_done, tile + 1)
                    wait(dve, k_lo_done, tile - 1)
                    nc.vector.tensor_tensor(k_n[t % 2][:, :, :], k_raw[t % 2][:, :].rearrange("p (h d) -> p h d", h=HH),
                                            k_rinv[t % 2][:, :].unsqueeze(2).to_broadcast([P, HH, HD]),
                                            ALU.mult).then_inc(k_n_done, 1)

            windows(dve, body, SLOTS * (WINDOWS + 1) + 4)

        @block.tensor
        def _(pe):
            pe.wait_ge(ready, 6)

            def body(w, n, s):
                slot = SLOTS * w + s
                if n < WINDOWS:
                    t, half = s % TILES, w // (B * CHUNKS)
                    if s < TILES:
                        pe.wait_ge(ctx_lo_done, TILES * w + t + 1)
                        wait(pe, v_lo_done, TILES * (w - 1) + t + 1)
                        w_hi, w_lo = g["wk_hi"], g["wk_lo"]
                    else:
                        pe.wait_ge(k_raw_done, TILES * w + t + 1)
                        w_hi, w_lo = g["wv_hi"], g["wv_lo"]
                    project(nc, bank[t][:, :], [ctx_hi[t][:, k, :] for k in range(KD)],
                            [ctx_lo[t][:, k, :] for k in range(KD)],
                            [w_hi[:, k, bass.ds(half * 512, 512)] for k in range(KD)],
                            [w_lo[:, k, bass.ds(half * 512, 512)] for k in range(KD)]).then_inc(proj_done, 1)
                if found := head(w, n, s, 3):
                    no, h, cw, par = found
                    pe.wait_ge(p_done, no + 1)
                    wait(pe, pt_lo_done, no)
                    for k in range(TILES):
                        mm = nc.tensor.transpose(p_turn[:, k * P:(k + 1) * P], probs[h % 4][:, k * P:(k + 1) * P],
                                                 ident[:, :])
                    mm.then_inc(p_tr_done, 1)
                if found := k_tile(w, n, s, 4):
                    tile, t = found
                    pe.wait_ge(k_lo_done, tile + 1)
                    wait(pe, kt_done, tile)
                    for h in range(HH):
                        mm = nc.tensor.transpose(k_turn[:, h * P:(h + 1) * P],
                                                 k_lh[t % 2][:, h, :, :].rearrange("p a d -> p (a d)"), ident16[:, :])
                    mm.then_inc(k_tr_done, 1)
                if found := head(w, n, s, 4):
                    no, h, cw, par = found
                    pair = h // 2
                    pe.wait_ge(pt_lo_done, no + 1)
                    pe.wait_ge(v_lo_done, TILES * (cw + 1))
                    if h % 2 == 0:
                        wait(pe, added_done, HH // 2 * cw + pair)
                    to = o_pair[pair % 2][:, (h % 2) * VW:(h % 2 + 1) * VW]
                    for k in range(TILES):
                        at = slice(k * P, (k + 1) * P)
                        nc.tensor.matmul(to, pt_hi[h % 2][:, at], v_hi[par][:, k, h, :], start=(k == 0), stop=False)
                        nc.tensor.matmul(to, pt_hi[h % 2][:, at], v_lo[par][:, k, h, :], start=False, stop=False)
                        mm = nc.tensor.matmul(to, pt_lo[h % 2][:, at], v_hi[par][:, k, h, :], start=False,
                                              stop=(k == TILES - 1))
                    mm.then_inc(pv_done, 1)
                if found := head(w, n, s, 0):
                    no, h, cw, par = found
                    pe.wait_ge(kt_done, TILES * (cw + 1))
                    wait(pe, s_max_done, no)
                    for i in range(2):
                        mm = nc.tensor.matmul(scores[:, :], q_st[:, cw // CHUNKS, i, h, :], kt[par][:, h, :],
                                              start=(i == 0), stop=(i == 1))
                    mm.then_inc(s_done, 1)

            windows(pe, body, SLOTS * (WINDOWS + 1) + 3)


def layer_norm(nc, sems, sb, c, tag, resid, half_neg, banks):
    stats = sb(tag + "_stats", [P, B, 6], F32, c)
    mean_var = sb(tag + "_mean_var", [P, B, 2], F32, c)
    rstd = sb(tag + "_rstd", [P, B], F32, c)
    var_eps = sb(tag + "_var_eps", [P, B], F32, c)
    xn = sb(tag + "_xn", [P, B, D], F32, c)
    stat, agg, v_eps, rs, x_n = sems(c, " ".join(tag + "_" + n for n in "stat agg v_eps rs x_n".split()))

    def vector(dve, meanwhile=None):
        for b in range(B):
            nc.vector.bn_stats(stats[:, b, :], resid[:, b, :]).then_inc(stat, 1)
        for b in range(B):
            dve.wait_ge(stat, b + 1)
            nc.vector.bn_aggr(mean_var[:, b, :], stats[:, b, :]).then_inc(agg, 1)
        if meanwhile:
            meanwhile()
        dve.wait_ge(rs, 1)
        for b in range(B):
            nc.vector.tensor_scalar(xn[:, b, :], resid[:, b, :], mean_var[:, b, 0:1], rstd[:, b:b + 1],
                                    ALU.subtract, ALU.mult).then_inc(x_n, 1)

    def gpsimd(pool):
        pool.wait_ge(agg, B)
        nc.gpsimd.tensor_scalar(var_eps[:, :], mean_var[:, :, 1], LN_EPS, None, ALU.add).then_inc(v_eps, 1)
        pool.wait_ge(v_eps, 1)
        nc.gpsimd.tensor_tensor(rstd[:, :], var_eps[:, :], half_neg[:, 0:B], ALU.pow).then_inc(rs, 1)

    return xn, vector, gpsimd, x_n


def turn_rows(nc, sems, sb, c, tag, rows, rows_done, ident, banks):
    xt_hi, xt_lo = (sb(tag + n, [P, KD, B * P], F32R, c) for n in ("_xt_hi", "_xt_lo"))
    x_tr, x_hi, x_lo = sems(c, " ".join(tag + n for n in ("_x_tr", "_x_hi", "_x_lo")))

    def tensor(pe):
        for b in range(B):
            pe.wait_ge(rows_done, b + 1)
            for k in range(KD):
                mm = nc.tensor.transpose(banks[b][:, k * P:(k + 1) * P], rows[:, b, k * P:(k + 1) * P], ident[:, :])
            mm.then_inc(x_tr, 1)

    def scalar(act):
        for b in range(B):
            act.wait_ge(x_tr, b + 1)
            nc.scalar.activation(xt_hi[:, :, b * P:(b + 1) * P], banks[b][:, :].rearrange("p (k q) -> p k q", k=KD),
                                 ACT.Copy).then_inc(x_hi, 1)

    def vector(dve):
        for b in range(B):
            dve.wait_ge(x_hi, b + 1)
            nc.vector.tensor_tensor(xt_lo[:, :, b * P:(b + 1) * P], banks[b][:, :].rearrange("p (k q) -> p k q", k=KD),
                                    xt_hi[:, :, b * P:(b + 1) * P].bitcast(F32), ALU.subtract).then_inc(x_lo, 1)

    return xt_hi, xt_lo, tensor, scalar, vector, x_lo


def output_projection(nc, sems, sb, bank, g, tag, o_acc, weights, bias, then_split=None):
    with ExitStack() as c:
        resid, ident = g["resid"], g["ident"]
        rec, rec_up = (sb(tag + n, [P, UNITS, HH], F32, c) for n in ("_rec", "_rec_up"))
        o_n = [sb(f"{tag}_o_n{i}", [P, HALVES, HH, HD], F32, c) for i in range(2)]
        ot_hi = [sb(f"{tag}_ot_hi{i}", [P, E // P, P], F32R, c) for i in range(2)]
        ot_lo = [sb(f"{tag}_ot_lo{i}", [P, E // P, P], F32R, c) for i in range(2)]
        w_hi, w_lo = (sb(tag + n, [P, E // P, D], F32R, c) for n in ("_w_hi", "_w_lo"))
        raws = 4
        raw = [sb(f"{tag}_raw{i}", [P, 2 * D], F32, c) for i in range(raws)]
        own = E // P // 2
        extra = then_split[0].shape[1] // (2 * D) * KD if then_split else 0
        if bias is not None:
            bias_rows = sb(tag + "_bias", [P, D], F32, c)
        w_in = sems(c, " ".join(f"{tag}_w_in{i}" for i in range(raws)))
        b_in, wh_done, wl_done, rec_done, rec_up_done, on_done, tr_done, oh_done, ol_done, y_done, r_done = sems(
            c, " ".join(tag + n for n in "_b_in _wh _wl _rec_d _rec_up_d _on _tr _oh _ol _y _r".split()))
        block = c.enter_context(nc.Block())

        def piece(j):
            if j < own:
                src = weights.rearrange("(k p) n -> p k n", p=P)[:, 2 * j:2 * j + 2, :]
                return src, w_hi[:, 2 * j:2 * j + 2, :], w_lo[:, 2 * j:2 * j + 2, :]
            k, n = (j - own) % KD, (j - own) // KD
            at = slice(2 * D * n, 2 * D * (n + 1))
            return then_split[0].rearrange("(k p) n -> p k n", p=P)[:, k, at], then_split[1][:, k, at], then_split[2][:, k, at]

        def shaped(j, t):
            return t[:, :].rearrange("p (k n) -> p k n", k=2) if j < own else t[:, :]

        @block.sync
        def _(sp):
            if bias is not None:
                sp.dma_start(bias_rows[:, :], bias.partition_broadcast(P)).then_inc(b_in, 16)
            for j in range(own + extra):
                wait(sp, wl_done, j - raws + 1)
                sp.dma_start(shaped(j, raw[j % raws]), piece(j)[0]).then_inc(w_in[j % raws], 16)

        @block.scalar
        def _(act):
            def high(j):
                act.wait_ge(w_in[j % raws], 16 * (j // raws + 1))
                nc.scalar.activation(piece(j)[1], shaped(j, raw[j % raws]), ACT.Copy).then_inc(wh_done, 1)

            for j in range(own):
                high(j)
            for b in range(B):
                for i in range(2):
                    act.wait_ge(tr_done, 2 * b + i + 1)
                    if b >= 2:
                        act.wait_ge(y_done, b - 1)
                    nc.scalar.activation(ot_hi[b % 2][:, 4 * i:4 * i + 4, :],
                                         bank[2 * (b % 2) + i][:, :].rearrange("p (k q) -> p k q", k=4),
                                         ACT.Copy).then_inc(oh_done, 1)
                for j in range(own + extra * b // B, own + extra * (b + 1) // B):
                    high(j)

        @block.vector
        def _(dve):
            def low(j):
                dve.wait_ge(wh_done, j + 1)
                nc.vector.tensor_tensor(piece(j)[2], shaped(j, raw[j % raws]), piece(j)[1].bitcast(F32),
                                        ALU.subtract).then_inc(wl_done, 1)

            def normed(b):
                wait(dve, tr_done, 2 * (b - 1))
                for half in range(HALVES):
                    u = half * B + b
                    nc.vector.tensor_tensor(o_n[b % 2][:, half, :, :], o_acc[:, u, :, 0:HD],
                                            rec_up[:, u, :].unsqueeze(2).to_broadcast([P, HH, HD]),
                                            ALU.mult).then_inc(on_done, 1)

            nc.vector.reciprocal(rec[:, :, :], o_acc[:, :, :, HD]).then_inc(rec_done, 1)
            dve.wait_ge(rec_done, 1)
            nc.vector.tensor_scalar(rec_up[:, :, :], rec[:, :, :], 1.0 / V_UP, None, ALU.mult).then_inc(rec_up_done, 1)
            dve.wait_ge(rec_up_done, 1)
            normed(0)
            for j in range(own):
                low(j)
            if bias is not None:
                dve.wait_ge(b_in, 16)
                for b in range(B):
                    nc.vector.tensor_tensor(resid[:, b, :], resid[:, b, :], bias_rows[:, :], ALU.add).then_inc(r_done, 1)
            for b in range(B):
                if b + 1 < B:
                    normed(b + 1)
                if b >= 1:
                    for j in range(own + extra * (b - 1) // B, own + extra * b // B):
                        low(j)
                for i in range(2):
                    dve.wait_ge(oh_done, 2 * b + i + 1)
                    nc.vector.tensor_tensor(ot_lo[b % 2][:, 4 * i:4 * i + 4, :],
                                            bank[2 * (b % 2) + i][:, :].rearrange("p (k q) -> p k q", k=4),
                                            ot_hi[b % 2][:, 4 * i:4 * i + 4, :].bitcast(F32),
                                            ALU.subtract).then_inc(ol_done, 1)
                if b >= 1:
                    add(nc, dve, b - 1, y_done, resid, bank, r_done, bias)
            for j in range(own + extra * (B - 1) // B, own + extra):
                low(j)
            add(nc, dve, B - 1, y_done, resid, bank, r_done, bias)

        @block.tensor
        def _(pe):
            for b in range(B + 1):
                if b < B:
                    pe.wait_ge(on_done, 2 * (b + 1))
                    wait(pe, ol_done, 2 * (b - 1))
                    for i in range(2):
                        for k in range(4):
                            at = 4 * i + k
                            mm = nc.tensor.transpose(
                                bank[2 * (b % 2) + i][:, k * P:(k + 1) * P],
                                o_n[b % 2][:, :, :, :].rearrange("p a h d -> p (a h d)")[:, at * P:(at + 1) * P], ident[:, :])
                        mm.then_inc(tr_done, 1)
                if b >= 1:
                    m = b - 1
                    if m == 0:
                        pe.wait_ge(wl_done, own)
                    pe.wait_ge(ol_done, 2 * (m + 1))
                    n = E // P
                    project(nc, bank[4 + m][:, :], [ot_hi[m % 2][:, k, :] for k in range(n)],
                            [ot_lo[m % 2][:, k, :] for k in range(n)], [w_hi[:, k, :] for k in range(n)],
                            [w_lo[:, k, :] for k in range(n)]).then_inc(y_done, 1)


def add(nc, dve, b, y_done, resid, bank, r_done, bias):
    dve.wait_ge(y_done, b + 1)
    if bias is not None:
        dve.wait_ge(r_done, b + 1)
    nc.vector.tensor_tensor(resid[:, b, :], resid[:, b, :], bank[4 + b][:, :], ALU.add).then_inc(r_done, 1)


def self_attention(nc, sems, sb, bank, g, w_hi, w_lo, o_self):
    with ExitStack() as c:
        resid, ident, ident16 = g["resid"], g["ident"], g["ident16"]
        xn, ln_vector, ln_pool, x_n = layer_norm(nc, sems, sb, c, "self", resid, g["half_neg"], bank)
        xt_hi, xt_lo, turn_pe, turn_act, turn_dve, x_lo = turn_rows(nc, sems, sb, c, "self", xn, x_n, ident, bank)
        bias_rows = sb("self_bias", [P, 3, HALVES, HH * HD], F32, c)
        causal = sb("causal", [P, P], F32, c)
        ln_up = sb("ln_up", [P, 1], F32, c)
        biased = [sb(f"biased{i}", [P, HH, HD], F32, c) for i in range(3)]
        stack_q = [sb(f"stack_q{i}", [P, HH, 3, HD], F16, c) for i in range(2)]
        stack_k = [sb(f"stack_k{i}", [P, HH, 2, HD], F16, c) for i in range(2)]
        v_hi = [sb(f"self_v_hi{i}", [P, HH, VW], F16, c) for i in range(4)]
        v_lo = [sb(f"self_v_lo{i}", [P, HH, VW], F16, c) for i in range(4)]
        qt_a, qt_b, kt = ([sb(f"{n}{i}", [P, HH, P], F16, c) for i in range(2)] for n in ("qt_a", "qt_b", "self_kt"))
        probs = [sb(f"self_probs{i}", [P, HH, P], F32, c) for i in range(2)]
        row_max = [sb(f"row_max{i}", [P, HH], F32, c) for i in range(2)]
        pt_hi, pt_lo = (sb(n, [P, HH, P], F16, c) for n in ("self_pt_hi", "self_pt_lo"))
        b_in, ready, qkv_done, biased_done, hi_done, dup_done, lo_done = sems(
            c, "self_b_in self_ready qkv_done biased_done self_hi self_dup self_lo")
        qa_tr, qb_tr, k_tr, qa_kept, qb_kept, k_kept, s_done, masked, max_done, less_max, p_done = sems(
            c, "qa_tr qb_tr self_k_tr qa_kept qb_kept self_k_kept self_s masked self_max less_max self_p")
        p_tr, ph_done, pl_done, pv_done, o_done = sems(c, "self_p_tr self_ph self_pl self_pv self_o")
        turn_a, turn_b = bank[3], bank[6]
        a16, b16 = turn_a[:, :].bitcast(F16), turn_b[:, :].bitcast(F16)
        UP = V_UP
        scale = 1.0 / (UP * UP * 8.0)
        block = c.enter_context(nc.Block())

        @block.sync
        def _(sp):
            sp.dma_start(bias_rows[:, :, :, :].rearrange("p t a n -> p (t a n)"),
                         g["b_qkv"].partition_broadcast(P)).then_inc(b_in, 16)

        @block.gpsimd
        def _(pool):
            nc.gpsimd.memset(causal[:, :], 0.0).then_inc(ready, 1)
            nc.gpsimd.memset(ln_up[:, :], LN_P_UP).then_inc(ready, 1)
            for i in range(4):
                nc.gpsimd.memset(v_hi[i][:, :, HD:VW], 1.0).then_inc(ready, 1)
                nc.gpsimd.memset(v_lo[i][:, :, HD:VW], 0.0).then_inc(ready, 1)
            pool.wait_ge(ready, 10)
            nc.gpsimd.affine_select(out=causal[:, :], in_=causal[:, :], compare_op=ALU.is_ge, fill=-1e9 / scale, base=0,
                                    pattern=[[-1, P]], channel_multiplier=1).then_inc(ready, 1)
            ln_pool(pool)
            for m in range(UNITS):
                pool.wait_ge(max_done, m + 1)
                nc.gpsimd.tensor_tensor(probs[m % 2][:, :, :], probs[m % 2][:, :, :],
                                        row_max[m % 2][:, :].unsqueeze(2).to_broadcast([P, HH, P]),
                                        ALU.subtract).then_inc(less_max, 1)

        @block.tensor
        def _(pe):
            turn_pe(pe)

            def projected(n, t):
                if n >= UNITS:
                    return
                b, half = n // HALVES, n % HALVES
                if n == 0:
                    pe.wait_ge(x_lo, B)
                wait(pe, biased_done, 3 * (n - 1) + t + 1)
                at = slice((t * HALVES + half) * 512, (t * HALVES + half + 1) * 512)
                project(nc, bank[t][:, :], [xt_hi[:, k, b * P:(b + 1) * P] for k in range(KD)],
                        [xt_lo[:, k, b * P:(b + 1) * P] for k in range(KD)],
                        [w_hi[:, k, at] for k in range(KD)], [w_lo[:, k, at] for k in range(KD)]).then_inc(qkv_done, 1)

            def turned(to, stack, first):
                for h in range(HH):
                    mm = nc.tensor.transpose(to[:, h * P:(h + 1) * P],
                                             stack[:, h, first:first + 2, :].rearrange("p a d -> p (a d)"), ident16[:, :])
                return mm

            def queries_turned(m):
                pe.wait_ge(lo_done, 3 * m + 1)
                pe.wait_ge(dup_done, m + 1)
                wait(pe, pl_done, 2 * (m - 1))
                wait(pe, k_kept, m)
                wait(pe, qb_kept, m)
                turned(a16, stack_q[m % 2], 0).then_inc(qa_tr, 1)
                turned(b16, stack_q[m % 2], 1).then_inc(qb_tr, 1)

            def keys_turned(m):
                pe.wait_ge(lo_done, 3 * m + 2)
                pe.wait_ge(qa_kept, m + 1)
                turned(a16, stack_k[m % 2], 0).then_inc(k_tr, 1)

            def scored(m):
                pe.wait_ge(k_kept, m + 1)
                pe.wait_ge(qb_kept, m + 1)
                for h in range(HH):
                    if h % 4 == 0:
                        wait(pe, masked, 2 * (m - 1) + h // 4 + 1)
                    to = bank[4 + h // 4][:, (h % 4) * P:(h % 4 + 1) * P]
                    nc.tensor.matmul(to, qt_a[m % 2][:, h, :], kt[m % 2][:, h, :], start=True, stop=False)
                    mm = nc.tensor.matmul(to, qt_b[m % 2][:, h, :], kt[m % 2][:, h, :], start=False, stop=True)
                    if h % 4 == 3:
                        mm.then_inc(s_done, 1)

            def weights_turned(m):
                pe.wait_ge(p_done, m + 1)
                last = min(m + 2, UNITS)
                for i, (to, kept) in enumerate(((turn_b, qb_kept), (turn_a, k_kept))):
                    pe.wait_ge(kept, last)
                    wait(pe, pl_done, 2 * (m - 1) + i + 1)
                    for k in range(4):
                        mm = nc.tensor.transpose(to[:, k * P:(k + 1) * P], probs[m % 2][:, 4 * i + k, :], ident[:, :])
                    mm.then_inc(p_tr, 1)

            def valued(m):
                pe.wait_ge(lo_done, 3 * (m + 1))
                for i in range(2):
                    pe.wait_ge(pl_done, 2 * m + i + 1)
                    wait(pe, o_done, 2 * m + i)
                    for h in range(4 * i, 4 * i + 4):
                        to = bank[7][:, (h % 4) * VW:(h % 4 + 1) * VW]
                        nc.tensor.matmul(to, pt_hi[:, h, :], v_hi[m % 4][:, h, :], start=True, stop=False)
                        nc.tensor.matmul(to, pt_hi[:, h, :], v_lo[m % 4][:, h, :], start=False, stop=False)
                        mm = nc.tensor.matmul(to, pt_lo[:, h, :], v_hi[m % 4][:, h, :], start=False, stop=True)
                    mm.then_inc(pv_done, 1)

            for n in range(UNITS + 3):
                if n >= 3:
                    weights_turned(n - 3)
                projected(n, 0)
                if n >= 3:
                    valued(n - 3)
                if 1 <= n <= UNITS:
                    queries_turned(n - 1)
                projected(n, 1)
                if 1 <= n <= UNITS:
                    keys_turned(n - 1)
                projected(n, 2)
                if 1 <= n <= UNITS:
                    scored(n - 1)

        @block.scalar
        def _(act):
            turn_act(act)
            act.wait_ge(ready, 11)

            def high(n, t):
                if n >= UNITS:
                    return
                to = (stack_q[n % 2][:, :, 0, :], stack_k[n % 2][:, :, 1, :], v_hi[n % 4][:, :, 0:HD])[t]
                act.wait_ge(biased_done, 3 * n + t + 1)
                if t == 0:
                    wait(act, k_tr, n - 1)
                    wait(act, pv_done, 2 * (n - 3))
                nc.scalar.activation(to, biased[t][:, :, :], ACT.Copy, scale=UP).then_inc(hi_done, 1)

            for n in range(UNITS + 3):
                if n >= 3:
                    m = n - 3
                    for i, src in enumerate((turn_b, turn_a)):
                        act.wait_ge(p_tr, 2 * m + i + 1)
                        wait(act, pv_done, 2 * m)
                        nc.scalar.activation(pt_hi[:, 4 * i:4 * i + 4, :].rearrange("p h q -> p (h q)"), src[:, :],
                                             ACT.Copy).then_inc(ph_done, 1)
                high(n, 0)
                if 1 <= n <= UNITS:
                    m = n - 1
                    act.wait_ge(qb_tr, m + 1)
                    wait(act, s_done, 2 * (m - 1))
                    nc.scalar.activation(qt_b[m % 2][:, :, :].rearrange("p h q -> p (h q)"), b16[:, :],
                                         ACT.Copy).then_inc(qb_kept, 1)
                high(n, 1)
                if 2 <= n <= UNITS + 1:
                    m = n - 2
                    act.wait_ge(less_max, m + 1)
                    nc.scalar.activation(probs[m % 2][:, :, :], probs[m % 2][:, :, :], ACT.Exp, scale=scale,
                                         bias=ln_up[:, 0:1]).then_inc(p_done, 1)
                high(n, 2)

        @block.vector
        def _(dve):
            ln_vector(dve)
            turn_dve(dve)
            dve.wait_ge(b_in, 16)
            dve.wait_ge(ready, 11)

            def with_bias(n, t):
                if n >= UNITS:
                    return
                dve.wait_ge(qkv_done, 3 * n + t + 1)
                wait(dve, lo_done, 3 * (n - 1) + t + 1)
                nc.vector.tensor_tensor(biased[t][:, :, :].rearrange("p h d -> p (h d)"), bank[t][:, :],
                                        bias_rows[:, t, n % HALVES, :], ALU.add).then_inc(biased_done, 1)

            def low(n, t):
                if not 0 <= n < UNITS:
                    return
                to, hi = ((stack_q[n % 2][:, :, 1, :], stack_q[n % 2][:, :, 0, :]),
                          (stack_k[n % 2][:, :, 0, :], stack_k[n % 2][:, :, 1, :]),
                          (v_lo[n % 4][:, :, 0:HD], v_hi[n % 4][:, :, 0:HD]))[t]
                dve.wait_ge(hi_done, 3 * n + t + 1)
                nc.vector.scalar_tensor_tensor(to, biased[t][:, :, :], UP, hi, ALU.mult, ALU.subtract).then_inc(lo_done, 1)
                if t == 0:
                    nc.vector.tensor_copy(stack_q[n % 2][:, :, 2, :], hi).then_inc(dup_done, 1)

            for n in range(UNITS + 3):
                low(n - 1, 2)
                if 2 <= n <= UNITS + 1:
                    m = n - 2
                    for i in range(2):
                        dve.wait_ge(s_done, 2 * m + i + 1)
                        wait(dve, p_tr, 2 * (m - 1))
                        nc.vector.tensor_tensor(probs[m % 2][:, 4 * i:4 * i + 4, :],
                                                bank[4 + i][:, :].rearrange("p (h q) -> p h q", h=4),
                                                causal[:, :].unsqueeze(1).to_broadcast([P, 4, P]), ALU.add).then_inc(masked, 1)
                if n >= 3:
                    m = n - 3
                    for i, src in enumerate((turn_b, turn_a)):
                        dve.wait_ge(ph_done, 2 * m + i + 1)
                        nc.vector.tensor_tensor(pt_lo[:, 4 * i:4 * i + 4, :].rearrange("p h q -> p (h q)"), src[:, :],
                                                pt_hi[:, 4 * i:4 * i + 4, :].rearrange("p h q -> p (h q)"),
                                                ALU.subtract).then_inc(pl_done, 1)
                if 2 <= n <= UNITS + 1:
                    m = n - 2
                    dve.wait_ge(masked, 2 * (m + 1))
                    wait(dve, less_max, m - 1)
                    nc.vector.tensor_reduce(row_max[m % 2][:, :], probs[m % 2][:, :, :], AX_X, ALU.max).then_inc(max_done, 1)
                with_bias(n, 0)
                if n >= 3:
                    m = n - 3
                    u = (m % HALVES) * B + m // HALVES
                    for i in range(2):
                        dve.wait_ge(pv_done, 2 * m + i + 1)
                        nc.vector.tensor_copy(o_self[:, u, 4 * i:4 * i + 4, :],
                                              bank[7][:, 0:4 * VW].rearrange("p (h v) -> p h v", h=4)).then_inc(o_done, 1)
                if 1 <= n <= UNITS:
                    m = n - 1
                    dve.wait_ge(qa_tr, m + 1)
                    wait(dve, s_done, 2 * (m - 1))
                    nc.vector.tensor_copy(qt_a[m % 2][:, :, :].rearrange("p h q -> p (h q)"), a16[:, :]).then_inc(qa_kept, 1)
                low(n, 0)
                with_bias(n, 1)
                if 1 <= n <= UNITS:
                    m = n - 1
                    dve.wait_ge(k_tr, m + 1)
                    nc.vector.tensor_copy(kt[m % 2][:, :, :].rearrange("p h q -> p (h q)"), a16[:, :]).then_inc(k_kept, 1)
                low(n, 1)
                with_bias(n, 2)


QMAX = 32767.0
MIN_SCALE = 1e-12
ROUND = 1.5 * 2.0 ** 23


def feed_forward(nc, sems, sb, bank, g, out):
    I16, U16 = mybir.dt.int16, mybir.dt.uint16
    with ExitStack() as c:
        resid, ident = g["resid"], g["ident"]
        up_raw = sb("up_raw", [P, KF, B * P], F32, c)
        gate_raw = sb("gate_raw", [P, KF, B * P], F32, c)
        wd_hi, wd_lo = (sb(n, [P, KF, D], F32R, c) for n in ("wd_hi", "wd_lo"))
        top2 = sb("top2", [P, 2], F32, c)
        x_scale = sb("x_scale", [P, 1], F32, c)
        ffn_in(nc, sems, sb, bank, g, up_raw, gate_raw, wd_hi, wd_lo, top2, x_scale)
        ffn_out(nc, sems, sb, bank, g, up_raw, gate_raw, wd_hi, wd_lo, top2, x_scale, out)


def scale_of(nc, dve, top, times, to, inverse, tmp, done, at):
    nc.vector.tensor_scalar(tmp, top, times, 1.0 / QMAX, ALU.mult, ALU.mult).then_inc(done, 1)
    dve.wait_ge(done, at + 1)
    nc.vector.tensor_scalar(to, tmp, MIN_SCALE, None, ALU.max).then_inc(done, 1)
    dve.wait_ge(done, at + 2)
    nc.vector.reciprocal(inverse, to).then_inc(done, 1)
    dve.wait_ge(done, at + 3)
    return at + 3


def ffn_in(nc, sems, sb, bank, g, up_raw, gate_raw, wd_hi, wd_lo, top2, x_scale):
    I16 = mybir.dt.int16
    NB = D // BLOCK
    PIECES = 3 * KF
    with ExitStack() as c:
        resid, ident = g["resid"], g["ident"]
        xn, ln_vector, ln_pool, x_n = layer_norm(nc, sems, sb, c, "ffn", resid, g["half_neg"], bank)
        x_top, x_gtop, x_tmp, x_inv = (sb(n, [P, 1], F32, c) for n in ("x_top", "x_gtop", "x_tmp", "x_inv"))
        xi = sb("xi", [P, B, D], I16, c)
        xf = sb("xf", [P, B, D], F32, c)
        rows_done, top_done, all_done, sc_done, xi_done = sems(c, "rows_done top_done all_done sc_done xi_done")
        xt_hi, xt_lo, turn_pe, turn_act, turn_dve, x_lo = turn_rows(nc, sems, sb, c, "ffn", xf, rows_done, ident, bank)
        raws = 4
        raw = [sb(f"ffn_raw{i}", [P, NB, BLOCK], F32, c) for i in range(raws)]
        w_top = [sb(f"w_top{i}", [P, NB], F32, c) for i in range(2)]
        w_sc = [sb(f"w_sc{i}", [P, NB], F32, c) for i in range(4)]
        w_inv = [sb(f"w_inv{i}", [P, NB], F32, c) for i in range(3)]
        w_div = [sb(f"w_div{i}", [P, NB, BLOCK], F32, c) for i in range(3)]
        w_int = [sb(f"w_int{i}", [P, NB, BLOCK], F32, c) for i in range(3)]
        w_int16 = sb("w_int16", [P, NB, BLOCK], I16, c)
        w_deq = [sb(f"w_deq{i}", [P, NB, BLOCK], F32, c) for i in range(3)]
        wt_hi = [sb(f"wt_hi{i}", [P, KD, P], F32R, c) for i in range(3)]
        wt_lo = [sb(f"wt_lo{i}", [P, KD, P], F32R, c) for i in range(3)]
        tops = sb("tops", [P, 2, KF], F32, c)
        w_in = sems(c, " ".join(f"ffn_w_in{i}" for i in range(raws)))
        wtop_done, wsc_done, winv_done, wdiv_done, wint_done, wdeq_done, wtr_done, whi_done, wlo_done = sems(
            c, "wtop_done wsc_done winv_done wdiv_done wint_done wdeq_done wtr_done whi_done wlo_done")
        down_int_done, down_deq_done = sems(c, "down_int_done down_deq_done")
        y_done, kept_done, tops_done, mine_done, both_done = sems(c, "ffn_y ffn_kept tops_done mine_done both_done")
        top_mine = sb("top_mine", [P, 2], F32, c)
        block = c.enter_context(nc.Block())
        LIN = 2 * KF

        def linear(j):
            return 2 * (j // 3) + j % 3 if j % 3 < 2 else None

        def source(j):
            if (m := linear(j)) is not None:
                return (g["w_up"], g["w_gate"])[m // KF][(m % KF) * P:(m % KF + 1) * P, :]
            ot, ci = j // 3 // 3, j // 3 % 3
            return g["w_down"][ot * P:(ot + 1) * P, ci * D:(ci + 1) * D]

        def parts(j):
            if (m := linear(j)) is not None:
                return wt_hi[m % 3][:, :, :], wt_lo[m % 3][:, :, :]
            ot, ci = j // 3 // 3, j // 3 % 3
            at = (slice(None), slice(KD * ci, KD * (ci + 1)), slice(ot * P, (ot + 1) * P))
            return wd_hi[at], wd_lo[at]

        def after_rounding(eng, j):
            if j >= 0:
                m = linear(j)
                eng.wait_ge(*((down_int_done, j // 3 + 1) if m is None else (wint_done, m + 1)))

        def after_scaling(eng, j):
            if j >= 0:
                m = linear(j)
                eng.wait_ge(*((down_deq_done, j // 3 + 1) if m is None else (wdeq_done, m + 1)))

        def scales(j):
            return w_sc[j % 4][:, :].unsqueeze(2).to_broadcast([P, NB, BLOCK])

        @block.sync
        def _(sp):
            for j in range(PIECES):
                wait(sp, wdiv_done, j - raws + 1)
                sp.dma_start(raw[j % raws][:, :, :].rearrange("p a i -> p (a i)"), source(j)).then_inc(w_in[j % raws], 16)

        @block.gpsimd
        def _(pool):
            def divided(j):
                pool.wait_ge(winv_done, j + 1)
                after_rounding(pool, j - 3)
                nc.gpsimd.tensor_tensor(w_div[j % 3][:, :, :], raw[j % raws][:, :, :],
                                        w_inv[j % 3][:, :].unsqueeze(2).to_broadcast([P, NB, BLOCK]),
                                        ALU.mult).then_inc(wdiv_done, 1)

            def dequantised(j):
                if linear(j) is not None:
                    after_rounding(pool, j)
                    wait(pool, wtr_done, j - 2)
                    nc.gpsimd.tensor_tensor(w_deq[j % 3][:, :, :], w_int[j % 3][:, :, :], scales(j),
                                            ALU.mult).then_inc(wdeq_done, 1)

            ln_pool(pool)
            divided(0)
            pool.wait_ge(top_done, 1)
            nc.gpsimd.partition_all_reduce(x_gtop[:, :], x_top[:, :], P, ABSMAX).then_inc(all_done, 1)
            for j in range(1, PIECES + 2):
                if j < PIECES:
                    divided(j)
                if j >= 2:
                    dequantised(j - 2)
            pool.wait_ge(mine_done, 1)
            nc.gpsimd.partition_all_reduce(top2[:, :], top_mine[:, :], P, ABSMAX).then_inc(both_done, 1)

        @block.vector
        def _(dve):
            def tops_of(j):
                dve.wait_ge(w_in[j % raws], 16 * (j // raws + 1))
                nc.vector.tensor_reduce(w_top[j % 2][:, :], raw[j % raws][:, :, :], AX_X, ALU.max,
                                        apply_absolute_value=True).then_inc(wtop_done, 1)

            def scale_for(j):
                dve.wait_ge(wtop_done, j + 1)
                after_scaling(dve, j - 4)
                nc.vector.tensor_scalar(w_sc[j % 4][:, :], w_top[j % 2][:, :], 1.0 / 7.0, MIN_SCALE, ALU.mult,
                                        ALU.max).then_inc(wsc_done, 1)

            def inverse_of(j):
                dve.wait_ge(wsc_done, j + 1)
                wait(dve, wdiv_done, j - 2)
                nc.vector.reciprocal(w_inv[j % 3][:, :], w_sc[j % 4][:, :]).then_inc(winv_done, 1)

            def rounded(j):
                if linear(j) is not None:
                    dve.wait_ge(wdiv_done, j + 1)
                    nc.vector.tensor_scalar(w_int[j % 3][:, :, :], w_div[j % 3][:, :, :], ROUND, ROUND, ALU.add,
                                            ALU.subtract).then_inc(wint_done, 1)
                else:
                    after_rounding(dve, j)
                    wait(dve, wtr_done, j - 2)
                    nc.vector.tensor_tensor(w_deq[j % 3][:, :, :], w_int16[:, :, :], scales(j),
                                            ALU.mult).then_inc(down_deq_done, 1)

            def low(j):
                dve.wait_ge(whi_done, j + 1)
                hi, lo = parts(j)
                nc.vector.tensor_tensor(lo, bank[4 + j % 4][:, :].rearrange("p (k q) -> p k q", k=KD), hi.bitcast(F32),
                                        ALU.subtract).then_inc(wlo_done, 1)

            def top_of(m):
                dve.wait_ge(kept_done, m + 1)
                src = (up_raw, gate_raw)[m // KF][:, m % KF, :]
                nc.vector.tensor_reduce(tops[:, m // KF, m % KF:m % KF + 1], src, AX_X, ALU.max,
                                        apply_absolute_value=True).then_inc(tops_done, 1)
                if m == LIN - 1:
                    dve.wait_ge(tops_done, LIN)
                    nc.vector.tensor_reduce(top_mine[:, :], tops[:, :, :], AX_X, ALU.max).then_inc(mine_done, 1)

            def prepared(j):
                tops_of(j)
                scale_for(j)
                inverse_of(j)

            ln_vector(dve, lambda: prepared(0))
            dve.wait_ge(x_n, B)
            nc.vector.tensor_reduce(x_top[:, :], xn[:, :, :].rearrange("p b d -> p (b d)"), AX_X, ALU.max,
                                    apply_absolute_value=True).then_inc(top_done, 1)
            prepared(1)
            rounded(0)
            dve.wait_ge(all_done, 1)
            scale_of(nc, dve, x_gtop[:, :], 1.0, x_scale[:, :], x_inv[:, :], x_tmp[:, :], sc_done, 0)
            for b in range(B):
                nc.vector.tensor_scalar(xi[:, b, :], xn[:, b, :], x_inv[:, 0:1], None, ALU.mult).then_inc(xi_done, 1)
            for b in range(B):
                dve.wait_ge(xi_done, b + 1)
                nc.vector.tensor_copy(xf[:, b, :], xi[:, b, :]).then_inc(rows_done, 1)
            prepared(2)
            turn_dve(dve)
            for j in range(3, PIECES + 8):
                if j < PIECES:
                    tops_of(j)
                if j <= PIECES + 1:
                    rounded(j - 2)
                if j < PIECES:
                    scale_for(j)
                if 4 <= j <= PIECES + 3:
                    low(j - 4)
                if j < PIECES:
                    inverse_of(j)
                if j >= 8 and linear(j - 8) is not None:
                    top_of(linear(j - 8))

        @block.scalar
        def _(act):
            turn_act(act)

            def down_rounded(j):
                act.wait_ge(wdiv_done, j + 1)
                wait(act, down_deq_done, j // 3)
                nc.scalar.activation(w_int16[:, :, :], w_div[j % 3][:, :, :], ACT.Copy).then_inc(down_int_done, 1)

            def high(j):
                act.wait_ge(wtr_done, j + 1)
                if (m := linear(j)) is not None:
                    wait(act, y_done, m - 2)
                nc.scalar.activation(parts(j)[0], bank[4 + j % 4][:, :].rearrange("p (k q) -> p k q", k=KD),
                                     ACT.Copy).then_inc(whi_done, 1)

            for j in range(PIECES + 2):
                if j < PIECES:
                    if linear(j + 1) is None:
                        down_rounded(j + 1)
                    high(j)
                if j >= 3 and (m := linear(j - 3)) is not None:
                    act.wait_ge(y_done, m + 1)
                    nc.scalar.activation((up_raw, gate_raw)[m // KF][:, m % KF, :], bank[m % 4][:, :],
                                         ACT.Copy).then_inc(kept_done, 1)

        @block.tensor
        def _(pe):
            turn_pe(pe)
            for j in range(PIECES + 1):
                if j < PIECES:
                    after_scaling(pe, j)
                    wait(pe, wlo_done, j - 3)
                    for k in range(KD):
                        mm = nc.tensor.transpose(bank[4 + j % 4][:, k * P:(k + 1) * P],
                                                 w_deq[j % 3][:, :, :].rearrange("p a i -> p (a i)")[:, k * P:(k + 1) * P],
                                                 ident[:, :])
                    mm.then_inc(wtr_done, 1)
                if j >= 2 and (m := linear(j - 2)) is not None:
                    if m == 0:
                        pe.wait_ge(x_lo, B)
                    pe.wait_ge(wlo_done, j - 1)
                    wait(pe, kept_done, m - 3)
                    project(nc, bank[m % 4][:, :], [wt_hi[m % 3][:, k, :] for k in range(KD)],
                            [wt_lo[m % 3][:, k, :] for k in range(KD)], [xt_hi[:, k, :] for k in range(KD)],
                            [xt_lo[:, k, :] for k in range(KD)]).then_inc(y_done, 1)


def ffn_out(nc, sems, sb, bank, g, up_raw, gate_raw, wd_hi, wd_lo, top2, x_scale, out):
    I16, U16 = mybir.dt.int16, mybir.dt.uint16
    UNIT = 1.0 / 65536.0
    with ExitStack() as c:
        resid = g["resid"]
        up_i, gate_i = (sb(n, [P, KF, B * P], I16, c) for n in ("up_i", "gate_i"))
        sig = [sb(f"sig{i}", [P, B * P], F32, c) for i in range(2)]
        sig_i = [sb(f"sig_i{i}", [P, B * P], U16, c) for i in range(2)]
        o_hi = [sb(f"o_hi{i}", [P, B * P], F32R, c) for i in range(3)]
        o_lo = [sb(f"o_lo{i}", [P, B * P], F32R, c) for i in range(3)]
        y = sb("y_rows", [P, B, D], F32, c)
        tmp2, scale2, inv2, raw_inv2 = (sb(n, [P, 2], F32, c) for n in ("tmp2", "scale2", "inv2", "raw_inv2"))
        tops3, tops4 = (sb(n, [P, KF], F32, c) for n in ("tops3", "tops4"))
        top3, gtop3, tmp3, scale3, inv3, raw_inv3 = (sb(n, [P, 1], F32, c) for n in
                                                     ("top3", "gtop3", "tmp3", "scale3", "inv3", "raw_inv3"))
        top4, gtop4, tmp4, scale4, inv4, raw_inv4, both_sc = (
            sb(n, [P, 1], F32, c) for n in ("top4", "gtop4", "tmp4", "scale4", "inv4", "raw_inv4", "both_sc"))
        pool_up_done, = sems(c, "pool_up_done")
        sc_done, inv_done, up_done, gate_done, sig_done, sigi_done, act_done, t3_done, m3_done, g3_done = sems(
            c, "o_sc o_inv up_done gate_done sig_done sigi_done act_done t3_done m3_done g3_done")
        inv3_done, gi_done, prod_done, t4_done, m4_done, g4_done, inv4_done, oi_done, oh_done, ol_done, down_done, y_done, sent = sems(
            c, "inv3_done gi_done prod_done t4_done m4_done g4_done inv4_done oi_done oh_done ol_done down_done y_done sent")
        block = c.enter_context(nc.Block())

        @block.sync
        def _(sp):
            for b in range(B):
                sp.wait_ge(y_done, b + 1)
                sp.dma_start(out[b], y[:, b, :]).then_inc(sent, 16)
            sp.wait_ge(sent, 16 * B)

        on_act = [k for k in range(KF) if k % 3 == 2]

        @block.gpsimd
        def _(pool):
            pool.wait_ge(inv_done, 1)
            for k in range(KF):
                if k not in on_act:
                    nc.gpsimd.tensor_scalar(up_i[:, k, :], up_raw[:, k, :], raw_inv2[:, 0:1], None,
                                            ALU.mult).then_inc(pool_up_done, 1)
            pool.wait_ge(m3_done, 1)
            nc.gpsimd.partition_all_reduce(gtop3[:, :], top3[:, :], P, ABSMAX).then_inc(g3_done, 1)
            pool.wait_ge(m4_done, 1)
            nc.gpsimd.partition_all_reduce(gtop4[:, :], top4[:, :], P, ABSMAX).then_inc(g4_done, 1)

        @block.vector
        def _(dve):
            at = scale_of(nc, dve, top2[:, :], x_scale[:, 0:1], scale2[:, :], inv2[:, :], tmp2[:, :], sc_done, 0)
            nc.vector.tensor_scalar(raw_inv2[:, :], inv2[:, :], x_scale[:, 0:1], None, ALU.mult).then_inc(inv_done, 1)
            def top_of_gate(k):
                dve.wait_ge(act_done, k + 1)
                nc.vector.tensor_reduce(tops3[:, k:k + 1], gate_raw[:, k, :], AX_X, ALU.max,
                                        apply_absolute_value=True).then_inc(t3_done, 1)

            for k in range(KF):
                dve.wait_ge(sig_done, k + 1)
                nc.vector.tensor_scalar(sig_i[k % 2][:, :], sig[k % 2][:, :], 65536.0, None, ALU.mult).then_inc(sigi_done, 1)
                if k >= 1:
                    top_of_gate(k - 1)
                dve.wait_ge(sigi_done, k + 1)
                nc.vector.scalar_tensor_tensor(gate_raw[:, k, :], gate_i[:, k, :], scale2[:, 1:2], sig_i[k % 2][:, :],
                                               ALU.mult, ALU.mult).then_inc(act_done, 1)
            top_of_gate(KF - 1)
            dve.wait_ge(t3_done, KF)
            nc.vector.tensor_reduce(top3[:, :], tops3[:, :], AX_X, ALU.max).then_inc(m3_done, 1)
            dve.wait_ge(g3_done, 1)
            at = scale_of(nc, dve, gtop3[:, :], UNIT, scale3[:, :], inv3[:, :], tmp3[:, :], sc_done, at)
            nc.vector.tensor_scalar(raw_inv3[:, :], inv3[:, :], UNIT, None, ALU.mult).then_inc(inv3_done, 1)
            dve.wait_ge(up_done, len(on_act))
            dve.wait_ge(pool_up_done, KF - len(on_act))

            def top_of_product(k):
                dve.wait_ge(prod_done, k + 1)
                nc.vector.tensor_reduce(tops4[:, k:k + 1], gate_raw[:, k, :], AX_X, ALU.max,
                                        apply_absolute_value=True).then_inc(t4_done, 1)

            for k in range(KF):
                dve.wait_ge(gi_done, k + 1)
                nc.vector.tensor_tensor(gate_raw[:, k, :], gate_i[:, k, :], up_i[:, k, :], ALU.mult).then_inc(prod_done, 1)
                if k >= 1:
                    top_of_product(k - 1)
            top_of_product(KF - 1)
            dve.wait_ge(t4_done, KF)
            nc.vector.tensor_reduce(top4[:, :], tops4[:, :], AX_X, ALU.max).then_inc(m4_done, 1)
            nc.vector.tensor_scalar(both_sc[:, :], scale3[:, :], scale2[:, 0:1], None, ALU.mult).then_inc(m4_done, 1)
            dve.wait_ge(m4_done, 2)
            dve.wait_ge(g4_done, 1)
            at = scale_of(nc, dve, gtop4[:, :], both_sc[:, 0:1], scale4[:, :], inv4[:, :], tmp4[:, :], sc_done, at)
            nc.vector.tensor_scalar(raw_inv4[:, :], inv4[:, :], both_sc[:, 0:1], None, ALU.mult).then_inc(inv4_done, 1)
            for k in range(KF):
                dve.wait_ge(oi_done, k + 1)
                wait(dve, down_done, k - 2)
                nc.vector.tensor_copy(o_hi[k % 3][:, :], up_i[:, k, :]).then_inc(oh_done, 1)
                dve.wait_ge(oh_done, k + 1)
                nc.vector.tensor_tensor(o_lo[k % 3][:, :], up_i[:, k, :], o_hi[k % 3][:, :].bitcast(F32),
                                        ALU.subtract).then_inc(ol_done, 1)
            for b in range(B):
                dve.wait_ge(down_done, KF + b)
                nc.vector.scalar_tensor_tensor(y[:, b, :], bank[b][:, :], scale4[:, 0:1], resid[:, b, :], ALU.mult,
                                               ALU.add).then_inc(y_done, 1)

        @block.scalar
        def _(act):
            act.wait_ge(inv_done, 1)

            def gate_int(k):
                nc.scalar.activation(gate_i[:, k, :], gate_raw[:, k, :], ACT.Copy, scale=raw_inv2[:, 1:2]).then_inc(gate_done, 1)

            gate_int(0)
            for k in range(KF):
                if k + 1 < KF:
                    gate_int(k + 1)
                act.wait_ge(gate_done, k + 1)
                wait(act, sigi_done, k - 1)
                nc.scalar.activation(sig[k % 2][:, :], gate_i[:, k, :], ACT.Sigmoid, scale=scale2[:, 1:2]).then_inc(sig_done, 1)
                if k in on_act:
                    nc.scalar.activation(up_i[:, k, :], up_raw[:, k, :], ACT.Copy, scale=raw_inv2[:, 0:1]).then_inc(up_done, 1)
            act.wait_ge(inv3_done, 1)
            for k in range(KF):
                nc.scalar.activation(gate_i[:, k, :], gate_raw[:, k, :], ACT.Copy, scale=raw_inv3[:, 0:1]).then_inc(gi_done, 1)
            act.wait_ge(inv4_done, 1)
            for k in range(KF):
                nc.scalar.activation(up_i[:, k, :], gate_raw[:, k, :], ACT.Copy, scale=raw_inv4[:, 0:1]).then_inc(oi_done, 1)

        @block.tensor
        def _(pe):
            for k in range(KF):
                pe.wait_ge(ol_done, k + 1)
                for b in range(B):
                    at = slice(b * P, (b + 1) * P)
                    nc.tensor.matmul(bank[b][:, :], o_hi[k % 3][:, at], wd_hi[:, k, :], start=(k == 0), stop=False)
                    nc.tensor.matmul(bank[b][:, :], o_hi[k % 3][:, at], wd_lo[:, k, :], start=False, stop=False)
                    mm = nc.tensor.matmul(bank[b][:, :], o_lo[k % 3][:, at], wd_hi[:, k, :], start=False, stop=(k == KF - 1))
                    if b == B - 1 or k == KF - 1:
                        mm.then_inc(down_done, 1)


_OUTS = [((4, 128, 512), "float32")]


def kernel(**inputs):
    import numpy as _np
    import concourse.bacc as _bacc
    from concourse import mybir as _mybir
    from concourse.bass_utils import run_bass_kernel_spmd as _run

    def whole(name):
        return _np.ascontiguousarray(inputs[name])

    context = whole("ctx_1024").reshape(B, CHUNKS, TILES, P, KD, P).transpose(0, 1, 2, 5, 4, 3)
    laid = {
        "x": whole("x"),
        "ctx_t": _np.ascontiguousarray(context.reshape(B * CHUNKS, TILES, P, KD, P)),
        "lens": whole("_lenS2"),
        "wq": whole("L0_xattn_Wq"), "wk": whole("L0_xattn_Wk"), "wv": whole("L0_xattn_Wv"), "wo": whole("L0_xattn_Wo"),
        "q_norm": whole("L0_xattn_q_norm_w"), "k_norm": whole("L0_xattn_k_norm_w"),
        "w_qkv": whole("L0_attn_w_qkv").reshape(D, 3 * E), "b_qkv": whole("L0_attn_b_qkv").reshape(3 * E),
        "w_out": whole("L0_attn_w_out").reshape(E, D), "b_out": whole("L0_attn_b_out"),
        "w_gate": whole("L0_ffn_w_gate"), "w_up": whole("L0_ffn_w_up"), "w_down": whole("L0_ffn_w_down"),
    }
    nc = _bacc.Bacc("TRN2", target_bir_lowering=False, num_devices=1)
    args = [nc.dram_tensor(f"in_{n}_dram", a.shape, _mybir.dt.from_np(a.dtype), kind="ExternalInput").ap()
            for n, a in laid.items()]
    for i, (shape, dtype) in enumerate(_OUTS):
        args.append(nc.dram_tensor(f"out_{i}_dram", shape, _mybir.dt.from_np(_np.dtype(dtype)), kind="ExternalOutput").ap())
    program(nc, *args)
    r = _run(nc, [{f"in_{n}_dram": a for n, a in laid.items()}], core_ids=[0])
    return r.results[0]["out_0_dram"]
```

```python
from contextlib import ExitStack

import concourse.bass as bass
from concourse import mybir

F32 = mybir.dt.float32
F32R = mybir.dt.float32r
F16 = mybir.dt.float16
I32 = mybir.dt.int32
ALU = mybir.AluOpType
ACT = mybir.ActivationFunctionType
AX_X = mybir.AxisListType.X
ABSMAX = bass.bass_isa.ReduceOp.absmax

P = 128
B = 4
D = 512
KD = D // P
S = 2048
HEADS, HD = 16, 64
E = HEADS * HD
HH = 8
HALVES = HEADS // HH
CHUNK = 512
TILES = CHUNK // P
CHUNKS = S // CHUNK
WINDOWS = HALVES * B * CHUNKS
UNITS = HALVES * B
SLOTS = 2 * TILES
VW = HD + 1
FF = 1536
KF = FF // P
BLOCK = 32
LN_EPS = 1e-5
RMS_EPS = 1e-5
RAWS = 4
Q_UP, K_UP, V_UP, P_UP = 32.0, 1024.0, 16.0, 4096.0
LN_P_UP = 8.317766166719343
S_SCALE = 1.0 / (Q_UP * K_UP * 8.0)
NEG = -1e30
LOWEST = -3e38


def wait(eng, semaphore, value):
    if not isinstance(value, int) or value > 0:
        eng.wait_ge(semaphore, value)


def program(nc, x, ctx_t, lens, wq, wk, wv, wo, q_norm, k_norm, w_qkv, b_qkv, w_out, b_out,
            w_gate, w_up, w_down, out):
    with ExitStack() as whole:
        of_stage = [None, []]

        def sb(name, shape, dt, ctx=whole):
            return ctx.enter_context(nc.sbuf_tensor(name, shape, dt))

        def sems(ctx, names):
            handles = [nc.alloc_semaphore(n) for n in names.split()]
            if ctx is not of_stage[0]:
                of_stage[:] = [ctx, []]

                def give_back(held=of_stage[1]):
                    nc.clear_and_free_semaphores(held)
                    nc.all_engine_barrier()

                ctx.callback(give_back)
            of_stage[1].extend(handles)
            return handles

        bank = [whole.enter_context(nc.psum_tensor(f"bank{i}", [P, 512], F32)) for i in range(8)]

        resid = sb("resid", [P, B, D], F32)
        ident = sb("ident", [P, P], F32)
        ident16 = sb("ident16", [P, P], F16)
        half_neg = sb("half_neg", [P, 64], F32)
        cross = whole.enter_context(ExitStack())
        o_acc = sb("o_acc", [P, UNITS, HH, VW], F32, cross)
        stage_q = cross.enter_context(ExitStack())
        wk_hi, wk_lo = (sb(n, [P, KD, E], F32R, stage_q) for n in ("wk_hi", "wk_lo"))
        wv_hi, wv_lo = (sb(n, [P, KD, E], F32R, stage_q) for n in ("wv_hi", "wv_lo"))
        q_st = sb("q_st", [P, UNITS, 2, HH, P], F16, stage_q)

        prologue(nc, sems, sb, bank, locals())
        cross_attention(nc, sems, sb, bank, locals())
        stage_q.close()
        with ExitStack() as attn:
            w_qkv_hi, w_qkv_lo = (sb(n, [P, KD, 3 * E], F32R, attn) for n in ("w_qkv_hi", "w_qkv_lo"))
            self_xn = sb("self_xn", [P, B, D], F32, attn)
            output_projection(nc, sems, sb, bank, locals(), "cross_out", o_acc, wo, None, self_xn, None,
                              (w_qkv, w_qkv_hi, w_qkv_lo))
            self_attention(nc, sems, sb, bank, locals(), self_xn, w_qkv_hi, w_qkv_lo, o_acc)
        wd_hi, wd_lo = (sb(n, [P, KF, D], F32R) for n in ("wd_hi", "wd_lo"))
        ffn_xn, x_tops = sb("ffn_xn", [P, B, D], F32), sb("x_tops", [P, B], F32)
        ffn_raw = [sb(f"ffn_raw{i}", [P, D // BLOCK, BLOCK], F32) for i in range(RAWS)]
        ffn_w_in = sems(whole, " ".join(f"ffn_w_in{i}" for i in range(RAWS)))

        def ffn_load(sp, j):
            source = (w_up, w_gate)[j // KF][(j % KF) * P:(j % KF + 1) * P, :]
            sp.dma_start(ffn_raw[j % RAWS][:, :, :].rearrange("p a i -> p (a i)"), source).then_inc(ffn_w_in[j % RAWS], 16)

        output_projection(nc, sems, sb, bank, locals(), "self_out", o_acc, w_out, b_out, ffn_xn, x_tops,
                          meanwhile=lambda c, banks: down_weights(nc, sems, sb, c, banks, ident, w_down, wd_hi, wd_lo),
                          prefetch=lambda sp: [ffn_load(sp, j) for j in range(RAWS)])
        feed_forward(nc, sems, sb, bank, locals(), ffn_xn, x_tops, wd_hi, wd_lo, out)


def prologue(nc, sems, sb, bank, g):
    with ExitStack() as c:
        resid, ident, ident16, half_neg = g["resid"], g["ident"], g["ident16"], g["half_neg"]
        w_hi = [None, g["wk_hi"], g["wv_hi"]]
        w_lo = [None, g["wk_lo"], g["wv_lo"]]
        w_hi[0], w_lo[0] = (sb(n, [P, KD, E], F32R, c) for n in ("wq_hi", "wq_lo"))
        raw = [sb(f"w_raw{i}", [P, E], F32, c) for i in range(RAWS)]
        stats = sb("stats", [P, B, 6], F32, c)
        mean_var = sb("mean_var", [P, B, 2], F32, c)
        rstd = sb("rstd", [P, B], F32, c)
        var_eps = sb("var_eps", [P, B], F32, c)
        xn = sb("xn", [P, B, D], F32, c)
        xt_hi, xt_lo = (sb(n, [P, KD, B * P], F32R, c) for n in ("xt_hi", "xt_lo"))
        qk_norm = sb("qk_norm", [P, 2, HD], F32, c)
        norm_w = sb("norm_w", [P, HD], F32, c)
        q_sq = sb("q_sq", [P, HH * HD], F32, c)
        q_raw = [sb(f"q_raw{i}", [P, HH * HD], F32, c) for i in range(2)]
        q_ss, q_ms, q_rinv = (sb(n, [P, UNITS, HH], F32, c) for n in ("q_ss", "q_ms", "q_rinv"))
        q_n, q_w = ([xn[:, 2 * j + i, :].rearrange("p (h d) -> p h d", h=HH) for i in range(2)] for j in range(2))
        stack = [sb(f"q_stack{i}", [P, HH, 3, HD], F16, c) for i in range(2)]
        x_in, norm_in = sems(c, "x_in norm_in")
        w_in = sems(c, " ".join(f"w_in{i}" for i in range(RAWS)))
        consts, stat, agg, v_eps, rs, x_n, x_tr, x_hi, x_lo = sems(
            c, "consts stat agg v_eps rs x_n x_tr x_hi x_lo")
        wh_done, wl_done, wnorm, zeroed = sems(c, "wh_done wl_done wnorm zeroed")
        qp_done, sq_done, raw_done, ss_done, ms_done, rinv_done, qn_done, qw_done = sems(
            c, "qp_done sq_done raw_done ss_done ms_done rinv_done qn_done qw_done")
        hi_done, hi2_done, lo_done, tr_a, tr_b, st_a, st_b = sems(
            c, "hi_done hi2_done lo_done tr_a tr_b st_a st_b")
        q_st = g["q_st"]
        t_a, t_b = (bank[4 + i][:, :].bitcast(F16) for i in range(2))
        block = c.enter_context(nc.Block())

        def unit(n):
            return n // HALVES, n % HALVES, (n % HALVES) * B + n // HALVES

        @block.sync
        def _(sp):
            for b in range(B):
                sp.dma_start(resid[:, b, :], g["x"][b]).then_inc(x_in, 16)
            for i, n in enumerate(("q_norm", "k_norm")):
                sp.dma_start(qk_norm[:, i, :], g[n].partition_broadcast(P)).then_inc(norm_in, 16)
            for j in range(3 * KD):
                wait(sp, wl_done, j - RAWS + 1)
                sp.dma_start(raw[j % RAWS][:, :], g[("wq", "wk", "wv")[j // KD]].rearrange(
                    "(k p) n -> p k n", p=P)[:, j % KD, :]).then_inc(w_in[j % RAWS], 16)

        @block.gpsimd
        def _(pool):
            nc.gpsimd.memset(ident[:, :], 0.0).then_inc(consts, 1)
            nc.gpsimd.memset(ident16[:, :], 0.0).then_inc(consts, 1)
            nc.gpsimd.memset(half_neg[:, :], -0.5).then_inc(consts, 1)
            nc.gpsimd.memset(g["o_acc"][:, :, :, :], 0.0).then_inc(zeroed, 1)
            pool.wait_ge(consts, 3)
            for t in (ident, ident16):
                nc.gpsimd.affine_select(out=t[:, :], in_=t[:, :], compare_op=ALU.not_equal, fill=1.0, base=0,
                                        pattern=[[-1, P]], channel_multiplier=1).then_inc(consts, 1)
            pool.wait_ge(agg, B)
            nc.gpsimd.tensor_scalar(var_eps[:, :], mean_var[:, :, 1], LN_EPS, None, ALU.add).then_inc(v_eps, 1)
            pool.wait_ge(v_eps, 1)
            nc.gpsimd.tensor_tensor(rstd[:, :], var_eps[:, :], half_neg[:, 0:B], ALU.pow).then_inc(rs, 1)
            pool.wait_ge(wnorm, 1)
            for n in range(UNITS + 1):
                if n < UNITS:
                    pool.wait_ge(ss_done, n + 1)
                    nc.gpsimd.tensor_scalar(q_ms[:, n, :], q_ss[:, n, :], 1.0 / HD, RMS_EPS, ALU.mult,
                                            ALU.add).then_inc(ms_done, 1)
                    pool.wait_ge(ms_done, n + 1)
                    nc.gpsimd.tensor_tensor(q_rinv[:, n, :], q_ms[:, n, :], half_neg[:, 0:HH],
                                            ALU.pow).then_inc(rinv_done, 1)
                if n >= 1:
                    m = n - 1
                    pool.wait_ge(qn_done, m + 1)
                    wait(pool, lo_done, m - 1)
                    nc.gpsimd.tensor_tensor(q_w[m % 2][:, :, :], q_n[m % 2][:, :, :],
                                            norm_w[:, :].unsqueeze(1).to_broadcast([P, HH, HD]),
                                            ALU.mult).then_inc(qw_done, 1)

        @block.tensor
        def _(pe):
            pe.wait_ge(consts, 5)
            for b in range(B):
                pe.wait_ge(x_n, b + 1)
                for k in range(KD):
                    mm = nc.tensor.transpose(bank[b][:, k * P:(k + 1) * P], xn[:, b, k * P:(k + 1) * P], ident[:, :])
                mm.then_inc(x_tr, 1)
            for n in range(UNITS + 3):
                if n < UNITS:
                    b, half, _ = unit(n)
                    pe.wait_ge(x_lo, min(n + 1, B))
                    wait(pe, raw_done, n - 3)
                    project(nc, bank[n % 4][:, :], [xt_hi[:, k, b * P:(b + 1) * P] for k in range(KD)],
                            [xt_lo[:, k, b * P:(b + 1) * P] for k in range(KD)],
                            [w_hi[0][:, k, half * 512:(half + 1) * 512] for k in range(KD)],
                            [w_lo[0][:, k, half * 512:(half + 1) * 512] for k in range(KD)],
                            (lambda k: pe.wait_ge(wl_done, k + 1)) if n == 0 else None).then_inc(qp_done, 1)
                if n >= 3:
                    m = n - 3
                    pe.wait_ge(lo_done, m + 1)
                    pe.wait_ge(hi2_done, m + 1)
                    wait(pe, st_a, m)
                    for h in range(HH):
                        mm = nc.tensor.transpose(t_a[:, h * P:(h + 1) * P],
                                                 stack[m % 2][:, h, 0:2, :].rearrange("p a d -> p (a d)"), ident16[:, :])
                    mm.then_inc(tr_a, 1)
                    wait(pe, st_b, m)
                    for h in range(HH):
                        mm = nc.tensor.transpose(t_b[:, h * P:(h + 1) * P],
                                                 stack[m % 2][:, h, 1:3, :].rearrange("p a d -> p (a d)"), ident16[:, :])
                    mm.then_inc(tr_b, 1)

        @block.scalar
        def _(act):
            def weights_hi(pieces):
                for j in pieces:
                    i = j // KD
                    act.wait_ge(w_in[j % RAWS], 16 * (j // RAWS + 1))
                    nc.scalar.activation(w_hi[i][:, j % KD, :], raw[j % RAWS][:, :], ACT.Copy).then_inc(wh_done, 1)

            def finish(m):
                act.wait_ge(qw_done, m + 1)
                wait(act, tr_b, m - 1)
                nc.scalar.activation(stack[m % 2][:, :, 0, :], q_w[m % 2][:, :, :], ACT.Copy).then_inc(hi_done, 1)

            def keep(m):
                act.wait_ge(tr_b, m + 1)
                nc.scalar.activation(q_st[:, unit(m)[2], 1, :, :].rearrange("p h q -> p (h q)"), t_b[:, :],
                                     ACT.Copy).then_inc(st_b, 1)

            weights_hi(range(KD))
            for b in range(B):
                act.wait_ge(x_tr, b + 1)
                nc.scalar.activation(xt_hi[:, :, b * P:(b + 1) * P], bank[b][:, :].rearrange("p (k q) -> p k q", k=KD),
                                     ACT.Copy).then_inc(x_hi, 1)
            for n in range(UNITS + 4):
                if n >= 4:
                    keep(n - 4)
                if n < UNITS:
                    act.wait_ge(qp_done, n + 1)
                    wait(act, ss_done, n)
                    nc.scalar.activation(q_sq[:, :], bank[n % 4][:, :], ACT.Square).then_inc(sq_done, 1)
                    wait(act, qn_done, n - 1)
                    nc.scalar.activation(q_raw[n % 2][:, :], bank[n % 4][:, :], ACT.Copy).then_inc(raw_done, 1)
                if 2 <= n <= UNITS + 1:
                    finish(n - 2)
                if n < 2 * KD:
                    weights_hi([KD + n])

        @block.vector
        def _(dve):
            for b in range(B):
                dve.wait_ge(x_in, 16 * B)
                nc.vector.bn_stats(stats[:, b, :], resid[:, b, :]).then_inc(stat, 1)
            for b in range(B):
                dve.wait_ge(stat, b + 1)
                nc.vector.bn_aggr(mean_var[:, b, :], stats[:, b, :]).then_inc(agg, 1)
            dve.wait_ge(rs, 1)
            for b in range(B):
                nc.vector.tensor_scalar(xn[:, b, :], resid[:, b, :], mean_var[:, b, 0:1], rstd[:, b:b + 1],
                                        ALU.subtract, ALU.mult).then_inc(x_n, 1)
            dve.wait_ge(norm_in, 32)
            nc.vector.scalar_tensor_tensor(norm_w[:, :], qk_norm[:, 0, :], Q_UP, qk_norm[:, 1, :], ALU.mult,
                                           ALU.mult).then_inc(wnorm, 1)

            def weights_lo(pieces):
                for j in pieces:
                    i = j // KD
                    dve.wait_ge(wh_done, j + 1)
                    nc.vector.tensor_tensor(w_lo[i][:, j % KD, :], raw[j % RAWS][:, :],
                                            w_hi[i][:, j % KD, :].bitcast(F32), ALU.subtract).then_inc(wl_done, 1)

            def normed(m):
                dve.wait_ge(rinv_done, m + 1)
                dve.wait_ge(raw_done, m + 1)
                wait(dve, qw_done, m - 1)
                nc.vector.tensor_tensor(q_n[m % 2][:, :, :], q_raw[m % 2][:, :].rearrange("p (h d) -> p h d", h=HH),
                                        q_rinv[:, m, :].unsqueeze(2).to_broadcast([P, HH, HD]),
                                        ALU.mult).then_inc(qn_done, 1)

            def parts(m):
                dve.wait_ge(hi_done, m + 1)
                wait(dve, tr_b, m - 1)
                nc.vector.tensor_copy(stack[m % 2][:, :, 2, :], stack[m % 2][:, :, 0, :]).then_inc(hi2_done, 1)
                nc.vector.tensor_tensor(stack[m % 2][:, :, 1, :], q_w[m % 2][:, :, :], stack[m % 2][:, :, 0, :],
                                        ALU.subtract).then_inc(lo_done, 1)

            def keep(m):
                dve.wait_ge(tr_a, m + 1)
                nc.vector.tensor_copy(q_st[:, unit(m)[2], 0, :, :].rearrange("p h q -> p (h q)"),
                                      t_a[:, :]).then_inc(st_a, 1)

            weights_lo(range(KD))
            for b in range(B):
                dve.wait_ge(x_hi, b + 1)
                nc.vector.tensor_tensor(xt_lo[:, :, b * P:(b + 1) * P], bank[b][:, :].rearrange("p (k q) -> p k q", k=KD),
                                        xt_hi[:, :, b * P:(b + 1) * P].bitcast(F32), ALU.subtract).then_inc(x_lo, 1)
            for n in range(UNITS + 4):
                if n >= 4:
                    keep(n - 4)
                if 1 <= n <= UNITS:
                    normed(n - 1)
                if n < UNITS:
                    dve.wait_ge(sq_done, n + 1)
                    nc.vector.tensor_reduce(q_ss[:, n, :], q_sq[:, :].rearrange("p (h d) -> p h d", h=HH), AX_X,
                                            ALU.add).then_inc(ss_done, 1)
                if n < 2 * KD:
                    weights_lo([KD + n])
                if 2 <= n <= UNITS + 1:
                    parts(n - 2)


def project(nc, to, x_hi, x_lo, w_hi, w_lo, between=None):
    n = len(x_hi)
    for k in range(n):
        if between:
            between(k)
        nc.tensor.matmul(to, x_hi[k], w_hi[k], start=(k == 0), stop=False)
        nc.tensor.matmul(to, x_hi[k], w_lo[k], start=False, stop=False)
        mm = nc.tensor.matmul(to, x_lo[k], w_hi[k], start=False, stop=(k == n - 1))
    return mm


def cross_attention(nc, sems, sb, bank, g):
    with ExitStack() as c:
        q_st, o_acc, ident, ident16, half_neg = (g[n] for n in ("q_st", "o_acc", "ident", "ident16", "half_neg"))
        ctx_raw = [sb(f"ctx_raw{i}", [P, KD, P], F32, c) for i in range(2)]
        ctx_hi = [sb(f"ctx_hi{i}", [P, KD, P], F32R, c) for i in range(TILES)]
        ctx_lo = [sb(f"ctx_lo{i}", [P, KD, P], F32R, c) for i in range(TILES)]
        k_sq = sb("k_sq", [P, HH * HD], F32, c)
        k_raw = [sb(f"k_raw{i}", [P, HH * HD], F32, c) for i in range(2)]
        k_ss = sb("k_ss", [P, HH], F32, c)
        k_ms = [sb(f"k_ms{i}", [P, HH], F32, c) for i in range(2)]
        k_rinv = [sb(f"k_rinv{i}", [P, HH], F32, c) for i in range(2)]
        k_n = [sb(f"k_n{i}", [P, HH, HD], F32, c) for i in range(2)]
        k_lh = [sb(f"k_lh{i}", [P, HH, 2, HD], F16, c) for i in range(2)]
        kt = [sb(f"kt{i}", [P, HH, CHUNK], F16, c) for i in range(2)]
        v_hi = [sb(f"v_hi{i}", [P, TILES, HH, VW], F16, c) for i in range(2)]
        v_lo = [sb(f"v_lo{i}", [P, TILES, HH, VW], F16, c) for i in range(2)]
        probs = [sb(f"probs{i}", [P, CHUNK], F32, c) for i in range(4)]
        pt_hi = [sb(f"pt_hi{i}", [P, CHUNK], F16, c) for i in range(2)]
        pt_lo = [sb(f"pt_lo{i}", [P, CHUNK], F16, c) for i in range(2)]
        key_no = sb("key_no", [P, CHUNK], F32, c)
        mask = sb("mask", [P, CHUNK], F32, c)
        lens_i = sb("lens_i", [P, B], I32, c)
        lens_f = sb("lens_f", [P, B], F32, c)
        left = sb("left", [P, B, CHUNKS], F32, c)
        chunk_max = sb("chunk_max", [P, 4], F32, c)
        run_max = sb("run_max", [P, UNITS, HH], F32, c)
        new_max = [sb(f"new_max{i}", [P, 2], F32, c) for i in range(2)]
        neg_max = [sb(f"neg_max{i}", [P, 2], F32, c) for i in range(2)]
        max_step = [sb(f"max_step{i}", [P, 2], F32, c) for i in range(2)]
        alpha = [sb(f"alpha{i}", [P, 2], F32, c) for i in range(2)]

        ctx_in = sems(c, "ctx_in0 ctx_in1")
        lens_in, ready, lens_done, left_done = sems(c, "lens_in ready lens_done left_done")
        ctx_hi_done, ctx_lo_done, proj_done = sems(c, "ctx_hi_done ctx_lo_done proj_done")
        k_sq_done, k_raw_done, k_ss_done, k_ms_done, k_rinv_done, k_n_done, k_hi_done, k_lo_done, k_tr_done, kt_done = sems(
            c, "k_sq_done k_raw_done k_ss_done k_ms_done k_rinv_done k_n_done k_hi_done k_lo_done k_tr_done kt_done")
        v_hi_done, v_lo_done, mask_done = sems(c, "v_hi_done v_lo_done mask_done")
        s_done, s_max_done, new_max_done, neg_max_done, step_done, kept_done = sems(
            c, "s_done s_max_done new_max_done neg_max_done step_done kept_done")
        p_done, p_tr_done, pt_hi_done, pt_lo_done, pv_done, alpha_done, scaled_done, added_done = sems(
            c, "p_done p_tr_done pt_hi_done pt_lo_done pv_done alpha_done scaled_done added_done")
        scores, p_turn, k_turn, o_new = bank[4], bank[5], bank[6][:, :].bitcast(F16), bank[7]
        o_pair = [o_new[:, 2 * i * VW:2 * (i + 1) * VW] for i in range(2)]
        block = c.enter_context(nc.Block())

        def windows(eng, body, last):
            for w in range(3):
                for s in range(SLOTS):
                    body(w, w, s)
            with eng.Fori(0, (WINDOWS - 4) // 2) as i:
                for p in range(2):
                    for s in range(SLOTS):
                        body(2 * i + 3 + p, 3 + p, s)
            for w in range(WINDOWS - 1, WINDOWS + 2):
                for s in range(SLOTS):
                    if SLOTS * w + s <= last:
                        body(w, w, s)

        def k_tile(w, n, s, lag):
            at = s - lag
            if at < 0:
                at, w, n = at + SLOTS, w - 1, n - 1
            return (TILES * w + at, at) if 0 <= n < WINDOWS and at < TILES else None

        def v_tile(w, n, s, lag):
            at = s - lag
            if at < 0:
                at, w, n = at + SLOTS, w - 1, n - 1
            return (TILES * w + at - TILES, at - TILES, n % 2) if 0 <= n < WINDOWS and at >= TILES else None

        def head(w, n, s, lag):
            at, w, n = s - lag, w - 1, n - 1
            while at < 0:
                at, w, n = at + SLOTS, w - 1, n - 1
            return (HH * w + at, at, w, n % 2) if 0 <= n < WINDOWS else None

        def ctx_tile(w, n, s):
            t, w, n = (s - 5, w + 1, n + 1) if s >= 5 else (TILES - 1, w, n)
            return (TILES * w + t, t) if (s >= 5 or s == 0) and 1 <= n < WINDOWS else None

        @block.sync
        def _(sp):
            sp.dma_start(lens_i[:, :], g["lens"].partition_broadcast(P)).then_inc(lens_in, 16)

            def load(tile, t, w):
                wait(sp, ctx_lo_done, tile - 1)
                sp.dma_start(ctx_raw[t % 2][:, :, :], g["ctx_t"][w % (B * CHUNKS), t]).then_inc(ctx_in[t % 2], 16)

            for t in range(TILES):
                load(t, t, 0)
            with sp.Fori(1, WINDOWS) as w:
                for t in range(TILES):
                    load(TILES * w + t, t, w)

        @block.gpsimd
        def _(pool):
            nc.gpsimd.iota(key_no[:, :], [[1, CHUNK]], base=0, channel_multiplier=0,
                           allow_small_or_imprecise_dtypes=True).then_inc(ready, 1)
            for i in range(2):
                nc.gpsimd.memset(v_hi[i][:, :, :, HD:VW], 1.0).then_inc(ready, 1)
                nc.gpsimd.memset(v_lo[i][:, :, :, HD:VW], 0.0).then_inc(ready, 1)
            nc.gpsimd.memset(run_max[:, :, :], LOWEST).then_inc(ready, 1)

            def ctx_low(tile, t):
                pool.wait_ge(ctx_hi_done, tile + 1)
                nc.gpsimd.tensor_tensor(ctx_lo[t][:, :, :], ctx_raw[t % 2][:, :, :], ctx_hi[t][:, :, :].bitcast(F32),
                                        ALU.subtract).then_inc(ctx_lo_done, 1)

            def body(w, n, s):
                if found := k_tile(w, n, s, 1):
                    tile, t = found
                    pool.wait_ge(k_ms_done, tile + 1)
                    wait(pool, k_n_done, tile - 1)
                    nc.gpsimd.tensor_tensor(k_rinv[t % 2][:, :], k_ms[t % 2][:, :], half_neg[:, 0:HH],
                                            ALU.pow).then_inc(k_rinv_done, 1)
                if found := k_tile(w, n, s, 3):
                    tile, t = found
                    pool.wait_ge(k_hi_done, tile + 1)
                    nc.gpsimd.tensor_tensor(k_lh[t % 2][:, :, 0, :], k_n[t % 2][:, :, :], k_lh[t % 2][:, :, 1, :],
                                            ALU.subtract).then_inc(k_lo_done, 1)
                if (found := head(w, n, s, 3)) and found[1] % 2 == 0:
                    no, h, cw, _ = found
                    p, pair = HH // 2 * cw + h // 2, h // 2
                    pool.wait_ge(alpha_done, p + 1)
                    wait(pool, added_done, p - 1)
                    if n <= 1:
                        pool.wait_ge(ready, 6)
                    o_at = o_acc[:, cw // CHUNKS, h:h + 2, :]
                    nc.gpsimd.tensor_tensor(o_at, o_at, alpha[pair % 2][:, :].unsqueeze(2).to_broadcast([P, 2, VW]),
                                            ALU.mult).then_inc(scaled_done, 1)
                if found := ctx_tile(w, n, s):
                    ctx_low(*found)

            for t in range(TILES):
                ctx_low(t, t)
            windows(pool, body, SLOTS * (WINDOWS + 1) + 2)

        @block.scalar
        def _(act):
            def ctx_high(tile, t, w, n):
                act.wait_ge(ctx_in[t % 2], 16 * (2 * w + t // 2 + 1))
                if n > 0:
                    act.wait_ge(proj_done, SLOTS * w - TILES + t + 1)
                nc.scalar.activation(ctx_hi[t][:, :, :], ctx_raw[t % 2][:, :, :], ACT.Copy).then_inc(ctx_hi_done, 1)

            def body(w, n, s):
                slot = SLOTS * w + s
                if found := head(w, n, s, 4):
                    no, h, cw, par = found
                    act.wait_ge(p_tr_done, no + 1)
                    wait(act, pv_done, no - 1)
                    nc.scalar.activation(pt_hi[h % 2][:, :], p_turn[:, :], ACT.Copy).then_inc(pt_hi_done, 1)
                if found := k_tile(w, n, s, 1):
                    tile, t = found
                    act.wait_ge(proj_done, slot)
                    wait(act, k_ss_done, tile)
                    nc.scalar.activation(k_sq[:, :], bank[t][:, :], ACT.Square).then_inc(k_sq_done, 1)
                    wait(act, k_n_done, tile - 1)
                    nc.scalar.activation(k_raw[t % 2][:, :], bank[t][:, :], ACT.Copy).then_inc(k_raw_done, 1)
                if found := v_tile(w, n, s, 1):
                    tile, t, par = found
                    act.wait_ge(proj_done, slot)
                    wait(act, pv_done, HH * (w - (2 if s == 0 else 1)))
                    nc.scalar.activation(v_hi[par][:, t, :, 0:HD], bank[t][:, :].rearrange("p (h d) -> p h d", h=HH),
                                         ACT.Copy, scale=V_UP).then_inc(v_hi_done, 1)
                if found := k_tile(w, n, s, 3):
                    tile, t = found
                    act.wait_ge(k_n_done, tile + 1)
                    wait(act, k_tr_done, tile - 1)
                    nc.scalar.activation(k_lh[t % 2][:, :, 1, :], k_n[t % 2][:, :, :], ACT.Copy).then_inc(k_hi_done, 1)
                if found := head(w, n, s, 2):
                    no, h, cw, par = found
                    p, pair = HH // 2 * cw + h // 2, h // 2
                    if h % 2 == 0:
                        act.wait_ge(step_done, p + 1)
                        wait(act, scaled_done, p - 1)
                        nc.scalar.activation(alpha[pair % 2][:, :], max_step[pair % 2][:, :], ACT.Exp,
                                             scale=S_SCALE).then_inc(alpha_done, 1)
                    act.wait_ge(neg_max_done, p + 1)
                    nc.scalar.activation(probs[h % 4][:, :], probs[h % 4][:, :], ACT.Exp, scale=S_SCALE,
                                         bias=neg_max[pair % 2][:, h % 2:h % 2 + 1]).then_inc(p_done, 1)
                if found := ctx_tile(w, n, s):
                    ctx_high(*found, w + (1 if s else 0), 1)

            for t in range(TILES):
                ctx_high(t, t, 0, 0)
            windows(act, body, SLOTS * (WINDOWS + 1) + 3)

        @block.vector
        def _(dve):
            dve.wait_ge(lens_in, 16)
            nc.vector.tensor_copy(lens_f[:, :], lens_i[:, :]).then_inc(lens_done, 1)
            dve.wait_ge(lens_done, 1)
            for k in range(CHUNKS):
                nc.vector.tensor_scalar(left[:, :, k], lens_f[:, :], float(-CHUNK * k), None, ALU.add).then_inc(left_done, 1)
            dve.wait_ge(left_done, CHUNKS)
            dve.wait_ge(ready, 6)

            def body(w, n, s):
                slot = SLOTS * w + s
                if (found := head(w, n, s, 5)) and found[1] % 2 == 1:
                    no, h, cw, par = found
                    p, pair = HH // 2 * cw + h // 2, h // 2
                    dve.wait_ge(pv_done, no + 1)
                    dve.wait_ge(scaled_done, p + 1)
                    o_at = o_acc[:, cw // CHUNKS, h - 1:h + 1, :]
                    nc.vector.tensor_tensor(o_at, o_at, o_pair[pair % 2].rearrange("p (h v) -> p h v", h=2),
                                            ALU.add).then_inc(added_done, 1)
                looped = not isinstance(w, int)

                def before_maximum(no, cw):
                    dve.wait_ge(s_done, no + 1)
                    dve.wait_ge(mask_done, cw + 1)
                    wait(dve, p_tr_done, no - 3)

                if looped and (found := head(w, n, s, 1)):
                    before_maximum(found[0], found[2])
                if found := head(w, n, s, 4):
                    no, h, cw, par = found
                    dve.wait_ge(pt_hi_done, no + 1)
                    nc.vector.tensor_tensor(pt_lo[h % 2][:, :], p_turn[:, :], pt_hi[h % 2][:, :],
                                            ALU.subtract).then_inc(pt_lo_done, 1)
                if found := head(w, n, s, 1):
                    no, h, cw, par = found
                    p, pair = HH // 2 * cw + h // 2, h // 2
                    if not looped:
                        before_maximum(no, cw)
                    nc.vector.tensor_tensor_reduce(probs[h % 4][:, :], scores[:, :], mask[:, :], 1.0, LOWEST, ALU.add,
                                                   ALU.max, chunk_max[:, h % 4:h % 4 + 1]).then_inc(s_max_done, 1)
                    if h % 2 == 1:
                        u, two = cw // CHUNKS, slice(h - 1, h + 1)
                        dve.wait_ge(s_max_done, no + 1)
                        wait(dve, kept_done, p)
                        nc.vector.tensor_tensor(new_max[pair % 2][:, :], run_max[:, u, two],
                                                chunk_max[:, (h - 1) % 4:(h - 1) % 4 + 2], ALU.max).then_inc(new_max_done, 1)
                        dve.wait_ge(new_max_done, p + 1)
                        wait(dve, p_done, 2 * p - 2)
                        nc.vector.tensor_scalar(neg_max[pair % 2][:, :], new_max[pair % 2][:, :], -S_SCALE, LN_P_UP,
                                                ALU.mult, ALU.add).then_inc(neg_max_done, 1)
                        wait(dve, alpha_done, p - 1)
                        nc.vector.tensor_tensor(max_step[pair % 2][:, :], run_max[:, u, two], new_max[pair % 2][:, :],
                                                ALU.subtract).then_inc(step_done, 1)
                        dve.wait_ge(step_done, p + 1)
                        nc.vector.tensor_tensor(run_max[:, u, two], run_max[:, u, two], new_max[pair % 2][:, :],
                                                ALU.max).then_inc(kept_done, 1)
                if s == 0 and 1 <= n <= WINDOWS:
                    wait(dve, s_max_done, HH * (w - 1))
                    at = (w - 1) % (B * CHUNKS)
                    nc.vector.tensor_scalar(mask[:, :], key_no[:, :], left[:, :, :].rearrange("p b k -> p (b k)")[:, bass.ds(at, 1)],
                                            NEG, ALU.is_ge, ALU.mult).then_inc(mask_done, 1)
                if found := k_tile(w, n, s, 5):
                    tile, t = found
                    par = (n - (1 if s < 5 else 0)) % 2
                    dve.wait_ge(k_tr_done, tile + 1)
                    wait(dve, s_done, HH * (w - (2 if s < 5 else 1)))
                    nc.vector.tensor_copy(kt[par][:, :, t * P:(t + 1) * P],
                                          k_turn[:, :].rearrange("p (h q) -> p h q", h=HH)).then_inc(kt_done, 1)
                if found := k_tile(w, n, s, 1):
                    tile, t = found
                    dve.wait_ge(k_sq_done, tile + 1)
                    wait(dve, k_ms_done, tile)
                    nc.vector.tensor_reduce(k_ss[:, :], k_sq[:, :].rearrange("p (h d) -> p h d", h=HH), AX_X,
                                            ALU.add).then_inc(k_ss_done, 1)
                if found := v_tile(w, n, s, 1):
                    tile, t, par = found
                    dve.wait_ge(v_hi_done, tile + 1)
                    nc.vector.scalar_tensor_tensor(v_lo[par][:, t, :, 0:HD], bank[t][:, :].rearrange("p (h d) -> p h d", h=HH),
                                                   V_UP, v_hi[par][:, t, :, 0:HD], ALU.mult,
                                                   ALU.subtract).then_inc(v_lo_done, 1)
                if found := k_tile(w, n, s, 1):
                    tile, t = found
                    dve.wait_ge(k_ss_done, tile + 1)
                    wait(dve, k_rinv_done, tile - 1)
                    nc.vector.tensor_scalar(k_ms[t % 2][:, :], k_ss[:, :], K_UP ** -2 / HD, K_UP ** -2 * RMS_EPS,
                                            ALU.mult, ALU.add).then_inc(k_ms_done, 1)
                if found := k_tile(w, n, s, 2):
                    tile, t = found
                    dve.wait_ge(k_rinv_done, tile + 1)
                    dve.wait_ge(k_raw_done, tile + 1)
                    wait(dve, k_lo_done, tile - 1)
                    nc.vector.tensor_tensor(k_n[t % 2][:, :, :], k_raw[t % 2][:, :].rearrange("p (h d) -> p h d", h=HH),
                                            k_rinv[t % 2][:, :].unsqueeze(2).to_broadcast([P, HH, HD]),
                                            ALU.mult).then_inc(k_n_done, 1)

            windows(dve, body, SLOTS * (WINDOWS + 1) + 4)

        @block.tensor
        def _(pe):
            pe.wait_ge(ready, 6)

            def body(w, n, s):
                slot = SLOTS * w + s
                if n < WINDOWS:
                    t, half = s % TILES, w // (B * CHUNKS)
                    if s < TILES:
                        pe.wait_ge(ctx_lo_done, TILES * w + t + 1)
                        wait(pe, v_lo_done, TILES * (w - 1) + t + 1)
                        w_hi, w_lo = g["wk_hi"], g["wk_lo"]
                    else:
                        pe.wait_ge(k_raw_done, TILES * w + t + 1)
                        w_hi, w_lo = g["wv_hi"], g["wv_lo"]
                    project(nc, bank[t][:, :], [ctx_hi[t][:, k, :] for k in range(KD)],
                            [ctx_lo[t][:, k, :] for k in range(KD)],
                            [w_hi[:, k, bass.ds(half * 512, 512)] for k in range(KD)],
                            [w_lo[:, k, bass.ds(half * 512, 512)] for k in range(KD)]).then_inc(proj_done, 1)
                if found := head(w, n, s, 3):
                    no, h, cw, par = found
                    pe.wait_ge(p_done, no + 1)
                    wait(pe, pt_lo_done, no)
                    for k in range(TILES):
                        mm = nc.tensor.transpose(p_turn[:, k * P:(k + 1) * P], probs[h % 4][:, k * P:(k + 1) * P],
                                                 ident[:, :])
                    mm.then_inc(p_tr_done, 1)
                if found := k_tile(w, n, s, 4):
                    tile, t = found
                    pe.wait_ge(k_lo_done, tile + 1)
                    wait(pe, kt_done, tile)
                    for h in range(HH):
                        mm = nc.tensor.transpose(k_turn[:, h * P:(h + 1) * P],
                                                 k_lh[t % 2][:, h, :, :].rearrange("p a d -> p (a d)"), ident16[:, :])
                    mm.then_inc(k_tr_done, 1)
                if found := head(w, n, s, 4):
                    no, h, cw, par = found
                    pair = h // 2
                    pe.wait_ge(pt_lo_done, no + 1)
                    pe.wait_ge(v_lo_done, TILES * (cw + 1))
                    if h % 2 == 0:
                        wait(pe, added_done, HH // 2 * cw + pair)
                    to = o_pair[pair % 2][:, (h % 2) * VW:(h % 2 + 1) * VW]
                    for k in range(TILES):
                        at = slice(k * P, (k + 1) * P)
                        nc.tensor.matmul(to, pt_hi[h % 2][:, at], v_hi[par][:, k, h, :], start=(k == 0), stop=False)
                        nc.tensor.matmul(to, pt_hi[h % 2][:, at], v_lo[par][:, k, h, :], start=False, stop=False)
                        mm = nc.tensor.matmul(to, pt_lo[h % 2][:, at], v_hi[par][:, k, h, :], start=False,
                                              stop=(k == TILES - 1))
                    mm.then_inc(pv_done, 1)
                if found := head(w, n, s, 0):
                    no, h, cw, par = found
                    pe.wait_ge(kt_done, TILES * (cw + 1))
                    wait(pe, s_max_done, no)
                    for i in range(2):
                        mm = nc.tensor.matmul(scores[:, :], q_st[:, cw // CHUNKS, i, h, :], kt[par][:, h, :],
                                              start=(i == 0), stop=(i == 1))
                    mm.then_inc(s_done, 1)

            windows(pe, body, SLOTS * (WINDOWS + 1) + 3)


def layer_norm(nc, sems, sb, c, tag, resid, half_neg, xn, x_tops):
    stats = sb(tag + "_stats", [P, B, 6], F32, c)
    mean_var = sb(tag + "_mean_var", [P, B, 2], F32, c)
    rstd = sb(tag + "_rstd", [P, B], F32, c)
    var_eps = sb(tag + "_var_eps", [P, B], F32, c)
    stat, agg, v_eps, rs, x_n, x_top = sems(c, " ".join(tag + "_" + n for n in "stat agg v_eps rs x_n x_top".split()))

    def moments(dve, b, added, count):
        dve.wait_ge(added, count)
        nc.vector.bn_stats(stats[:, b, :], resid[:, b, :]).then_inc(stat, 1)
        dve.wait_ge(stat, b + 1)
        nc.vector.bn_aggr(mean_var[:, b, :], stats[:, b, :]).then_inc(agg, 1)

    def normed(dve, b):
        dve.wait_ge(rs, b + 1)
        nc.vector.tensor_scalar(xn[:, b, :], resid[:, b, :], mean_var[:, b, 0:1], rstd[:, b:b + 1],
                                ALU.subtract, ALU.mult).then_inc(x_n, 1)
        if x_tops is not None:
            dve.wait_ge(x_n, b + 1)
            nc.vector.tensor_reduce(x_tops[:, b:b + 1], xn[:, b, :], AX_X, ALU.max,
                                    apply_absolute_value=True).then_inc(x_top, 1)

    def roots(pool, b):
        pool.wait_ge(agg, b + 1)
        nc.gpsimd.tensor_scalar(var_eps[:, b:b + 1], mean_var[:, b, 1:2], LN_EPS, None, ALU.add).then_inc(v_eps, 1)
        pool.wait_ge(v_eps, b + 1)
        nc.gpsimd.tensor_tensor(rstd[:, b:b + 1], var_eps[:, b:b + 1], half_neg[:, 0:1], ALU.pow).then_inc(rs, 1)

    return moments, normed, roots


def turn_rows(nc, sems, sb, c, tag, rows, rows_done, ident, banks):
    xt_hi, xt_lo = (sb(tag + n, [P, KD, B * P], F32R, c) for n in ("_xt_hi", "_xt_lo"))
    x_tr, x_hi, x_lo = sems(c, " ".join(tag + n for n in ("_x_tr", "_x_hi", "_x_lo")))

    def tensor(pe):
        for b in range(B):
            if rows_done is not None:
                pe.wait_ge(rows_done, b + 1)
            for k in range(KD):
                mm = nc.tensor.transpose(banks[b][:, k * P:(k + 1) * P], rows[:, b, k * P:(k + 1) * P], ident[:, :])
            mm.then_inc(x_tr, 1)

    def scalar(act):
        for b in range(B):
            act.wait_ge(x_tr, b + 1)
            nc.scalar.activation(xt_hi[:, :, b * P:(b + 1) * P], banks[b][:, :].rearrange("p (k q) -> p k q", k=KD),
                                 ACT.Copy).then_inc(x_hi, 1)

    def vector(dve):
        for b in range(B):
            dve.wait_ge(x_hi, b + 1)
            nc.vector.tensor_tensor(xt_lo[:, :, b * P:(b + 1) * P], banks[b][:, :].rearrange("p (k q) -> p k q", k=KD),
                                    xt_hi[:, :, b * P:(b + 1) * P].bitcast(F32), ALU.subtract).then_inc(x_lo, 1)

    return xt_hi, xt_lo, tensor, scalar, vector, x_lo


def output_projection(nc, sems, sb, bank, g, tag, o_acc, weights, bias, xn, x_tops, then_split=None,
                      meanwhile=None, prefetch=None):
    with ExitStack() as c:
        resid, ident = g["resid"], g["ident"]
        rec, rec_up = (sb(tag + n, [P, UNITS, HH], F32, c) for n in ("_rec", "_rec_up"))
        o_n = [sb(f"{tag}_o_n{i}", [P, HALVES, HH, HD], F32, c) for i in range(2)]
        ot_hi = [sb(f"{tag}_ot_hi{i}", [P, E // P, P], F32R, c) for i in range(2)]
        ot_lo = [sb(f"{tag}_ot_lo{i}", [P, E // P, P], F32R, c) for i in range(2)]
        w_hi, w_lo = (sb(tag + n, [P, E // P, D], F32R, c) for n in ("_w_hi", "_w_lo"))
        raws = 4
        raw = [sb(f"{tag}_raw{i}", [P, 2 * D], F32, c) for i in range(raws)]
        own = E // P // 2
        extra = then_split[0].shape[1] // (2 * D) * KD if then_split else 0
        steps, other = meanwhile(c, bank[6:8]) if meanwhile else (0, None)
        per = steps // (B - 1)
        if bias is not None:
            bias_rows = sb(tag + "_bias", [P, D], F32, c)
        w_in = sems(c, " ".join(f"{tag}_w_in{i}" for i in range(raws)))
        b_in, bias_done, pool_wl_done, wh_done, wl_done, rec_done, rec_up_done, on_done, tr_done, oh_done, ol_done, y_done, r_done = sems(
            c, " ".join(tag + n for n in "_b_in _bias_done _pool_wl _wh _wl _rec_d _rec_up_d _on _tr _oh _ol _y _r".split()))
        moments, rows_normed, roots = layer_norm(nc, sems, sb, c, tag + "_ln", resid, g["half_neg"], xn, x_tops)
        block = c.enter_context(nc.Block())

        def piece(j):
            if j < own:
                src = weights.rearrange("(k p) n -> p k n", p=P)[:, 2 * j:2 * j + 2, :]
                return src, w_hi[:, 2 * j:2 * j + 2, :], w_lo[:, 2 * j:2 * j + 2, :]
            k, n = (j - own) % KD, (j - own) // KD
            at = slice(2 * D * n, 2 * D * (n + 1))
            return then_split[0].rearrange("(k p) n -> p k n", p=P)[:, k, at], then_split[1][:, k, at], then_split[2][:, k, at]

        def on_pool(j):
            return j >= own and (j - own) % 2 == 0

        def after_low(eng, j):
            if j >= 0:
                done = sum(on_pool(i) == on_pool(j) for i in range(j + 1))
                eng.wait_ge(pool_wl_done if on_pool(j) else wl_done, done)

        def shaped(j, t):
            return t[:, :].rearrange("p (k n) -> p k n", k=2) if j < own else t[:, :]

        def low(eng, j, done):
            eng.wait_ge(wh_done, j + 1)
            eng.tensor_tensor(piece(j)[2], shaped(j, raw[j % raws]), piece(j)[1].bitcast(F32),
                              ALU.subtract).then_inc(done, 1)

        @block.sync
        def _(sp):
            if bias is not None:
                sp.dma_start(bias_rows[:, :], bias.partition_broadcast(P)).then_inc(b_in, 16)
            for j in range(own + extra):
                after_low(sp, j - raws)
                sp.dma_start(shaped(j, raw[j % raws]), piece(j)[0]).then_inc(w_in[j % raws], 16)
            for j in range(steps):
                other["load"](sp, j)
            if prefetch:
                prefetch(sp)

        @block.gpsimd
        def _(pool):
            if bias is not None:
                pool.wait_ge(b_in, 16)
                for b in range(B):
                    nc.gpsimd.tensor_tensor(resid[:, b, :], resid[:, b, :], bias_rows[:, :], ALU.add).then_inc(bias_done, 1)
            for b in range(B):
                for j in range(own + extra * b // B, own + extra * (b + 1) // B):
                    if on_pool(j):
                        low(pool, j, pool_wl_done)
                if not steps:
                    roots(pool, b)
            for j in range(steps + 2 if steps else 0):
                other["gpsimd"](pool, j)
                if j % per == 0 and j >= 2 * per:
                    roots(pool, j // per - 2)
            for b in range((steps + 1) // per - 1 if steps else B, B):
                roots(pool, b)

        @block.scalar
        def _(act):
            def high(j):
                act.wait_ge(w_in[j % raws], 16 * (j // raws + 1))
                nc.scalar.activation(piece(j)[1], shaped(j, raw[j % raws]), ACT.Copy).then_inc(wh_done, 1)

            for b in range(B):
                if b == 1:
                    for j in range(own):
                        high(j)
                for i in range(2):
                    act.wait_ge(tr_done, 2 * b + i + 1)
                    wait(act, y_done, b - 1)
                    nc.scalar.activation(ot_hi[b % 2][:, 4 * i:4 * i + 4, :],
                                         bank[2 * (b % 2) + i][:, :].rearrange("p (k q) -> p k q", k=4),
                                         ACT.Copy).then_inc(oh_done, 1)
                for j in range(own + extra * (b - 1) // B if b else own, own + extra * b // B):
                    high(j)
                for j in range(per * (b - 2) if b >= 2 else 0, per * (b - 1)):
                    other["scalar"](act, j)
            for j in range(own + extra * (B - 1) // B, own + extra):
                high(j)
            for j in range(per * (B - 2), steps):
                other["scalar"](act, j)

        @block.vector
        def _(dve):
            def normed(b):
                wait(dve, tr_done, 2 * (b - 1))
                for half in range(HALVES):
                    u = half * B + b
                    nc.vector.tensor_tensor(o_n[b % 2][:, half, :, :], o_acc[:, u, :, 0:HD],
                                            rec_up[:, u, :].unsqueeze(2).to_broadcast([P, HH, HD]),
                                            ALU.mult).then_inc(on_done, 1)

            nc.vector.reciprocal(rec[:, :, :], o_acc[:, :, :, HD]).then_inc(rec_done, 1)
            dve.wait_ge(rec_done, 1)
            nc.vector.tensor_scalar(rec_up[:, :, :], rec[:, :, :], 1.0 / V_UP, None, ALU.mult).then_inc(rec_up_done, 1)
            dve.wait_ge(rec_up_done, 1)
            normed(0)
            for b in range(B):
                if b + 1 < B:
                    normed(b + 1)
                if b >= 1:
                    for j in range(own + extra * (b - 1) // B, own + extra * b // B):
                        if not on_pool(j):
                            low(dve, j, wl_done)
                for i in range(2):
                    dve.wait_ge(oh_done, 2 * b + i + 1)
                    nc.vector.tensor_tensor(ot_lo[b % 2][:, 4 * i:4 * i + 4, :],
                                            bank[2 * (b % 2) + i][:, :].rearrange("p (k q) -> p k q", k=4),
                                            ot_hi[b % 2][:, 4 * i:4 * i + 4, :].bitcast(F32),
                                            ALU.subtract).then_inc(ol_done, 1)
                if b == 0:
                    for j in range(own):
                        low(dve, j, wl_done)
                for j in range(per * b, per * (b + 1)):
                    other["vector"](dve, j)
                if b >= 1:
                    add(nc, dve, b - 1, y_done, resid, bank, r_done, bias_done if bias is not None else None)
                    moments(dve, b - 1, r_done, b)
                if b >= 2:
                    rows_normed(dve, b - 2)
            for j in range(own + extra * (B - 1) // B, own + extra):
                if not on_pool(j):
                    low(dve, j, wl_done)
            if steps:
                for j in range(per * B, steps + other["drain"]):
                    other["vector"](dve, j)
            add(nc, dve, B - 1, y_done, resid, bank, r_done, bias_done if bias is not None else None)
            moments(dve, B - 1, r_done, B)
            rows_normed(dve, B - 2)
            rows_normed(dve, B - 1)

        @block.tensor
        def _(pe):
            for b in range(B + 1):
                if b < B:
                    pe.wait_ge(on_done, 2 * (b + 1))
                    wait(pe, ol_done, 2 * (b - 1))
                    for i in range(2):
                        for k in range(4):
                            at = 4 * i + k
                            mm = nc.tensor.transpose(
                                bank[2 * (b % 2) + i][:, k * P:(k + 1) * P],
                                o_n[b % 2][:, :, :, :].rearrange("p a h d -> p (a h d)")[:, at * P:(at + 1) * P], ident[:, :])
                        mm.then_inc(tr_done, 1)
                if b >= 1:
                    m = b - 1

                    def step_between(k, m=m, n=E // P):
                        if m == 0 and k % 2 == 0:
                            pe.wait_ge(wl_done, k // 2 + 1)
                        for i in range(per if m >= 1 else 0):
                            if k == (i + 1) * n // (per + 1):
                                other["tensor"](pe, per * (m - 1) + i)

                    pe.wait_ge(ol_done, 2 * (m + 1))
                    if m >= 2:
                        pe.wait_ge(r_done, m - 1)
                    n = E // P
                    project(nc, bank[4 + m % 2][:, :], [ot_hi[m % 2][:, k, :] for k in range(n)],
                            [ot_lo[m % 2][:, k, :] for k in range(n)], [w_hi[:, k, :] for k in range(n)],
                            [w_lo[:, k, :] for k in range(n)], step_between).then_inc(y_done, 1)


def add(nc, dve, b, y_done, resid, bank, r_done, bias_done):
    dve.wait_ge(y_done, b + 1)
    if bias_done is not None:
        dve.wait_ge(bias_done, b + 1)
    nc.vector.tensor_tensor(resid[:, b, :], resid[:, b, :], bank[4 + b % 2][:, :], ALU.add).then_inc(r_done, 1)


def self_attention(nc, sems, sb, bank, g, xn, w_hi, w_lo, o_self):
    with ExitStack() as c:
        resid, ident, ident16 = g["resid"], g["ident"], g["ident16"]
        xt_hi, xt_lo, turn_pe, turn_act, turn_dve, x_lo = turn_rows(nc, sems, sb, c, "self", xn, None, ident, bank)
        bias_rows = sb("self_bias", [P, 3, HALVES, HH * HD], F32, c)
        causal = sb("causal", [P, P], F32, c)
        ln_up = sb("ln_up", [P, 1], F32, c)
        biased = [sb(f"biased{i}", [P, HH, HD], F32, c) for i in range(3)]
        stack_q = [sb(f"stack_q{i}", [P, HH, 3, HD], F16, c) for i in range(2)]
        stack_k = [sb(f"stack_k{i}", [P, HH, 2, HD], F16, c) for i in range(2)]
        v_hi = [sb(f"self_v_hi{i}", [P, HH, VW], F16, c) for i in range(4)]
        v_lo = [sb(f"self_v_lo{i}", [P, HH, VW], F16, c) for i in range(4)]
        qt_a, qt_b, kt = ([sb(f"{n}{i}", [P, HH, P], F16, c) for i in range(2)] for n in ("qt_a", "qt_b", "self_kt"))
        probs = [sb(f"self_probs{i}", [P, HH, P], F32, c) for i in range(2)]
        row_max = [sb(f"row_max{i}", [P, HH], F32, c) for i in range(2)]
        pt_hi, pt_lo = (sb(n, [P, HH, P], F16, c) for n in ("self_pt_hi", "self_pt_lo"))
        b_in, ready, qkv_done, biased_done, hi_done, dup_done, lo_done = sems(
            c, "self_b_in self_ready qkv_done biased_done self_hi self_dup self_lo")
        qa_tr, qb_tr, k_tr, qa_kept, qb_kept, k_kept, s_done, masked, max_done, less_max, p_done = sems(
            c, "qa_tr qb_tr self_k_tr qa_kept qb_kept self_k_kept self_s masked self_max less_max self_p")
        p_tr, ph_done, pl_done, pv_done, o_done = sems(c, "self_p_tr self_ph self_pl self_pv self_o")
        turn_a, turn_b = bank[3], bank[6]
        a16, b16 = turn_a[:, :].bitcast(F16), turn_b[:, :].bitcast(F16)
        UP = V_UP
        scale = 1.0 / (UP * UP * 8.0)
        block = c.enter_context(nc.Block())

        @block.sync
        def _(sp):
            sp.dma_start(bias_rows[:, :, :, :].rearrange("p t a n -> p (t a n)"),
                         g["b_qkv"].partition_broadcast(P)).then_inc(b_in, 16)

        @block.gpsimd
        def _(pool):
            nc.gpsimd.memset(causal[:, :], 0.0).then_inc(ready, 1)
            nc.gpsimd.memset(ln_up[:, :], LN_P_UP).then_inc(ready, 1)
            for i in range(4):
                nc.gpsimd.memset(v_hi[i][:, :, HD:VW], 1.0).then_inc(ready, 1)
                nc.gpsimd.memset(v_lo[i][:, :, HD:VW], 0.0).then_inc(ready, 1)
            pool.wait_ge(ready, 10)
            nc.gpsimd.affine_select(out=causal[:, :], in_=causal[:, :], compare_op=ALU.is_ge, fill=-1e9 / scale, base=0,
                                    pattern=[[-1, P]], channel_multiplier=1).then_inc(ready, 1)
            for m in range(UNITS):
                pool.wait_ge(max_done, m + 1)
                nc.gpsimd.tensor_tensor(probs[m % 2][:, :, :], probs[m % 2][:, :, :],
                                        row_max[m % 2][:, :].unsqueeze(2).to_broadcast([P, HH, P]),
                                        ALU.subtract).then_inc(less_max, 1)

        @block.tensor
        def _(pe):
            turn_pe(pe)

            def projected(n, t):
                if n >= UNITS:
                    return
                b, half = n // HALVES, n % HALVES
                if n == 0:
                    pe.wait_ge(x_lo, t + 1)
                wait(pe, biased_done, 3 * (n - 1) + t + 1)
                at = slice((t * HALVES + half) * 512, (t * HALVES + half + 1) * 512)
                project(nc, bank[t][:, :], [xt_hi[:, k, b * P:(b + 1) * P] for k in range(KD)],
                        [xt_lo[:, k, b * P:(b + 1) * P] for k in range(KD)],
                        [w_hi[:, k, at] for k in range(KD)], [w_lo[:, k, at] for k in range(KD)]).then_inc(qkv_done, 1)

            def turned(to, stack, first):
                for h in range(HH):
                    mm = nc.tensor.transpose(to[:, h * P:(h + 1) * P],
                                             stack[:, h, first:first + 2, :].rearrange("p a d -> p (a d)"), ident16[:, :])
                return mm

            def queries_turned(m):
                pe.wait_ge(lo_done, 3 * m + 1)
                pe.wait_ge(dup_done, m + 1)
                if m == 0:
                    pe.wait_ge(x_lo, B)
                wait(pe, pl_done, 2 * (m - 1))
                wait(pe, k_kept, m)
                wait(pe, qb_kept, m)
                turned(a16, stack_q[m % 2], 0).then_inc(qa_tr, 1)
                turned(b16, stack_q[m % 2], 1).then_inc(qb_tr, 1)

            def keys_turned(m):
                pe.wait_ge(lo_done, 3 * m + 2)
                pe.wait_ge(qa_kept, m + 1)
                turned(a16, stack_k[m % 2], 0).then_inc(k_tr, 1)

            def scored(m):
                pe.wait_ge(k_kept, m + 1)
                pe.wait_ge(qb_kept, m + 1)
                for h in range(HH):
                    if h % 4 == 0:
                        wait(pe, masked, 2 * (m - 1) + h // 4 + 1)
                    to = bank[4 + h // 4][:, (h % 4) * P:(h % 4 + 1) * P]
                    nc.tensor.matmul(to, qt_a[m % 2][:, h, :], kt[m % 2][:, h, :], start=True, stop=False)
                    mm = nc.tensor.matmul(to, qt_b[m % 2][:, h, :], kt[m % 2][:, h, :], start=False, stop=True)
                    if h % 4 == 3:
                        mm.then_inc(s_done, 1)

            def weights_turned(m):
                pe.wait_ge(p_done, m + 1)
                last = min(m + 2, UNITS)
                for i, (to, kept) in enumerate(((turn_b, qb_kept), (turn_a, k_kept))):
                    pe.wait_ge(kept, last)
                    wait(pe, pl_done, 2 * (m - 1) + i + 1)
                    for k in range(4):
                        mm = nc.tensor.transpose(to[:, k * P:(k + 1) * P], probs[m % 2][:, 4 * i + k, :], ident[:, :])
                    mm.then_inc(p_tr, 1)

            def valued(m):
                pe.wait_ge(lo_done, 3 * (m + 1))
                for i in range(2):
                    pe.wait_ge(pl_done, 2 * m + i + 1)
                    wait(pe, o_done, 2 * m + i)
                    for h in range(4 * i, 4 * i + 4):
                        to = bank[7][:, (h % 4) * VW:(h % 4 + 1) * VW]
                        nc.tensor.matmul(to, pt_hi[:, h, :], v_hi[m % 4][:, h, :], start=True, stop=False)
                        nc.tensor.matmul(to, pt_hi[:, h, :], v_lo[m % 4][:, h, :], start=False, stop=False)
                        mm = nc.tensor.matmul(to, pt_lo[:, h, :], v_hi[m % 4][:, h, :], start=False, stop=True)
                    mm.then_inc(pv_done, 1)

            for n in range(UNITS + 3):
                if n >= 3:
                    weights_turned(n - 3)
                projected(n, 0)
                if n >= 3:
                    valued(n - 3)
                if 1 <= n <= UNITS:
                    queries_turned(n - 1)
                projected(n, 1)
                if 1 <= n <= UNITS:
                    keys_turned(n - 1)
                projected(n, 2)
                if 1 <= n <= UNITS:
                    scored(n - 1)

        @block.scalar
        def _(act):
            turn_act(act)
            act.wait_ge(ready, 11)

            def high(n, t):
                if n >= UNITS:
                    return
                to = (stack_q[n % 2][:, :, 0, :], stack_k[n % 2][:, :, 1, :], v_hi[n % 4][:, :, 0:HD])[t]
                act.wait_ge(biased_done, 3 * n + t + 1)
                if t == 0:
                    wait(act, k_tr, n - 1)
                    wait(act, pv_done, 2 * (n - 3))
                nc.scalar.activation(to, biased[t][:, :, :], ACT.Copy, scale=UP).then_inc(hi_done, 1)

            for n in range(UNITS + 3):
                if n >= 3:
                    m = n - 3
                    for i, src in enumerate((turn_b, turn_a)):
                        act.wait_ge(p_tr, 2 * m + i + 1)
                        wait(act, pv_done, 2 * m)
                        nc.scalar.activation(pt_hi[:, 4 * i:4 * i + 4, :].rearrange("p h q -> p (h q)"), src[:, :],
                                             ACT.Copy).then_inc(ph_done, 1)
                high(n, 0)
                if 1 <= n <= UNITS:
                    m = n - 1
                    act.wait_ge(qb_tr, m + 1)
                    wait(act, s_done, 2 * (m - 1))
                    nc.scalar.activation(qt_b[m % 2][:, :, :].rearrange("p h q -> p (h q)"), b16[:, :],
                                         ACT.Copy).then_inc(qb_kept, 1)
                high(n, 1)
                if 2 <= n <= UNITS + 1:
                    m = n - 2
                    act.wait_ge(less_max, m + 1)
                    nc.scalar.activation(probs[m % 2][:, :, :], probs[m % 2][:, :, :], ACT.Exp, scale=scale,
                                         bias=ln_up[:, 0:1]).then_inc(p_done, 1)
                high(n, 2)

        @block.vector
        def _(dve):
            turn_dve(dve)
            dve.wait_ge(b_in, 16)
            dve.wait_ge(ready, 11)

            def with_bias(n, t):
                if n >= UNITS:
                    return
                dve.wait_ge(qkv_done, 3 * n + t + 1)
                wait(dve, lo_done, 3 * (n - 1) + t + 1)
                nc.vector.tensor_tensor(biased[t][:, :, :].rearrange("p h d -> p (h d)"), bank[t][:, :],
                                        bias_rows[:, t, n % HALVES, :], ALU.add).then_inc(biased_done, 1)

            def low(n, t):
                if not 0 <= n < UNITS:
                    return
                to, hi = ((stack_q[n % 2][:, :, 1, :], stack_q[n % 2][:, :, 0, :]),
                          (stack_k[n % 2][:, :, 0, :], stack_k[n % 2][:, :, 1, :]),
                          (v_lo[n % 4][:, :, 0:HD], v_hi[n % 4][:, :, 0:HD]))[t]
                dve.wait_ge(hi_done, 3 * n + t + 1)
                nc.vector.scalar_tensor_tensor(to, biased[t][:, :, :], UP, hi, ALU.mult, ALU.subtract).then_inc(lo_done, 1)
                if t == 0:
                    nc.vector.tensor_copy(stack_q[n % 2][:, :, 2, :], hi).then_inc(dup_done, 1)

            for n in range(UNITS + 3):
                low(n - 1, 2)
                if 2 <= n <= UNITS + 1:
                    m = n - 2
                    for i in range(2):
                        dve.wait_ge(s_done, 2 * m + i + 1)
                        wait(dve, p_tr, 2 * (m - 1))
                        nc.vector.tensor_tensor(probs[m % 2][:, 4 * i:4 * i + 4, :],
                                                bank[4 + i][:, :].rearrange("p (h q) -> p h q", h=4),
                                                causal[:, :].unsqueeze(1).to_broadcast([P, 4, P]), ALU.add).then_inc(masked, 1)
                if n >= 3:
                    m = n - 3
                    for i, src in enumerate((turn_b, turn_a)):
                        dve.wait_ge(ph_done, 2 * m + i + 1)
                        nc.vector.tensor_tensor(pt_lo[:, 4 * i:4 * i + 4, :].rearrange("p h q -> p (h q)"), src[:, :],
                                                pt_hi[:, 4 * i:4 * i + 4, :].rearrange("p h q -> p (h q)"),
                                                ALU.subtract).then_inc(pl_done, 1)
                if 2 <= n <= UNITS + 1:
                    m = n - 2
                    dve.wait_ge(masked, 2 * (m + 1))
                    wait(dve, less_max, m - 1)
                    nc.vector.tensor_reduce(row_max[m % 2][:, :], probs[m % 2][:, :, :], AX_X, ALU.max).then_inc(max_done, 1)
                with_bias(n, 0)
                if n >= 3:
                    m = n - 3
                    u = (m % HALVES) * B + m // HALVES
                    for i in range(2):
                        dve.wait_ge(pv_done, 2 * m + i + 1)
                        nc.vector.tensor_copy(o_self[:, u, 4 * i:4 * i + 4, :],
                                              bank[7][:, 0:4 * VW].rearrange("p (h v) -> p h v", h=4)).then_inc(o_done, 1)
                if 1 <= n <= UNITS:
                    m = n - 1
                    dve.wait_ge(qa_tr, m + 1)
                    wait(dve, s_done, 2 * (m - 1))
                    nc.vector.tensor_copy(qt_a[m % 2][:, :, :].rearrange("p h q -> p (h q)"), a16[:, :]).then_inc(qa_kept, 1)
                low(n, 0)
                with_bias(n, 1)
                if 1 <= n <= UNITS:
                    m = n - 1
                    dve.wait_ge(k_tr, m + 1)
                    nc.vector.tensor_copy(kt[m % 2][:, :, :].rearrange("p h q -> p (h q)"), a16[:, :]).then_inc(k_kept, 1)
                low(n, 1)
                with_bias(n, 2)


QMAX = 32767.0
MIN_SCALE = 1e-12
ROUND = 1.5 * 2.0 ** 23


def feed_forward(nc, sems, sb, bank, g, xn, x_tops, wd_hi, wd_lo, out):
    I16, U16 = mybir.dt.int16, mybir.dt.uint16
    with ExitStack() as c:
        resid, ident = g["resid"], g["ident"]
        up_raw = sb("up_raw", [P, KF, B * P], F32, c)
        gate_raw = sb("gate_raw", [P, KF, B * P], F32, c)
        top2 = sb("top2", [P, 2], F32, c)
        x_scale = sb("x_scale", [P, 1], F32, c)
        ffn_in(nc, sems, sb, bank, g, xn, x_tops, up_raw, gate_raw, top2, x_scale)
        ffn_out(nc, sems, sb, bank, g, up_raw, gate_raw, wd_hi, wd_lo, top2, x_scale, out)


def scale_of(nc, dve, top, times, to, inverse, tmp, done, at):
    nc.vector.tensor_scalar(tmp, top, times, 1.0 / QMAX, ALU.mult, ALU.mult).then_inc(done, 1)
    dve.wait_ge(done, at + 1)
    nc.vector.tensor_scalar(to, tmp, MIN_SCALE, None, ALU.max).then_inc(done, 1)
    dve.wait_ge(done, at + 2)
    nc.vector.reciprocal(inverse, to).then_inc(done, 1)
    dve.wait_ge(done, at + 3)
    return at + 3


def down_weights(nc, sems, sb, c, banks, ident, w_down, wd_hi, wd_lo):
    LAST = 7
    NB, pieces = D // BLOCK, KF
    raws = 4
    raw = [sb(f"down_raw{i}", [P, NB, BLOCK], F32, c) for i in range(raws)]
    top = [sb(f"down_top{i}", [P, NB], F32, c) for i in range(2)]
    scale = [sb(f"down_scale{i}", [P, NB], F32, c) for i in range(4)]
    inverse = [sb(f"down_inverse{i}", [P, NB], F32, c) for i in range(3)]
    quotient, integer, scaled = ([sb(f"down_{n}{i}", [P, NB, BLOCK], F32, c) for i in range(3)]
                                 for n in ("quotient", "integer", "scaled"))
    w_in = sems(c, " ".join(f"down_in{i}" for i in range(raws)))
    top_done, scale_done, inverse_done, div_done, int_done, scaled_done, tr_done, hi_done, lo_done = sems(
        c, "down_top down_sc down_inv down_div down_int down_scaled down_tr down_hi down_lo")

    def at(j):
        ot, ci = j // (KF // KD), j % (KF // KD)
        return slice(ot * P, (ot + 1) * P), slice(KD * ci, KD * (ci + 1)), slice(ci * D, (ci + 1) * D)

    def load(sp, j):
        wait(sp, div_done, j - raws + 1)
        sp.dma_start(raw[j % raws][:, :, :].rearrange("p a i -> p (a i)"),
                     w_down[at(j)[0], at(j)[2]]).then_inc(w_in[j % raws], 16)

    def vector(dve, j):
        if j < pieces:
            dve.wait_ge(w_in[j % raws], 16 * (j // raws + 1))
            nc.vector.tensor_reduce(top[j % 2][:, :], raw[j % raws][:, :, :], AX_X, ALU.max,
                                    apply_absolute_value=True).then_inc(top_done, 1)
        if 2 <= j < pieces + 2:
            m = j - 2
            dve.wait_ge(div_done, m + 1)
            wait(dve, scaled_done, m - 2)
            nc.vector.tensor_scalar(integer[m % 3][:, :, :], quotient[m % 3][:, :, :], ROUND, ROUND, ALU.add,
                                    ALU.subtract).then_inc(int_done, 1)
        if j < pieces:
            dve.wait_ge(top_done, j + 1)
            wait(dve, scaled_done, j - 3)
            nc.vector.tensor_scalar(scale[j % 4][:, :], top[j % 2][:, :], 1.0 / 7.0, MIN_SCALE, ALU.mult,
                                    ALU.max).then_inc(scale_done, 1)
            dve.wait_ge(scale_done, j + 1)
            wait(dve, div_done, j - 2)
            nc.vector.reciprocal(inverse[j % 3][:, :], scale[j % 4][:, :]).then_inc(inverse_done, 1)
        if j >= LAST:
            m = j - LAST
            dve.wait_ge(hi_done, m + 1)
            nc.vector.tensor_tensor(wd_lo[:, at(m)[1], at(m)[0]], banks[m % 2][:, :].rearrange("p (k q) -> p k q", k=KD),
                                    wd_hi[:, at(m)[1], at(m)[0]].bitcast(F32), ALU.subtract).then_inc(lo_done, 1)

    def gpsimd(pool, j):
        if j < pieces:
            pool.wait_ge(inverse_done, j + 1)
            wait(pool, int_done, j - 2)
            nc.gpsimd.tensor_tensor(quotient[j % 3][:, :, :], raw[j % raws][:, :, :],
                                    inverse[j % 3][:, :].unsqueeze(2).to_broadcast([P, NB, BLOCK]),
                                    ALU.mult).then_inc(div_done, 1)
        if 2 <= j < pieces + 2:
            m = j - 2
            pool.wait_ge(int_done, m + 1)
            wait(pool, tr_done, m - 2)
            nc.gpsimd.tensor_tensor(scaled[m % 3][:, :, :], integer[m % 3][:, :, :],
                                    scale[m % 4][:, :].unsqueeze(2).to_broadcast([P, NB, BLOCK]),
                                    ALU.mult).then_inc(scaled_done, 1)

    def tensor(pe, j):
        pe.wait_ge(scaled_done, j + 1)
        wait(pe, lo_done, j - 1)
        for k in range(KD):
            mm = nc.tensor.transpose(banks[j % 2][:, k * P:(k + 1) * P],
                                     scaled[j % 3][:, :, :].rearrange("p a i -> p (a i)")[:, k * P:(k + 1) * P],
                                     ident[:, :])
        mm.then_inc(tr_done, 1)

    def scalar(act, j):
        act.wait_ge(tr_done, j + 1)
        nc.scalar.activation(wd_hi[:, at(j)[1], at(j)[0]], banks[j % 2][:, :].rearrange("p (k q) -> p k q", k=KD),
                             ACT.Copy).then_inc(hi_done, 1)

    return pieces, {"drain": LAST, "load": load, "vector": vector, "gpsimd": gpsimd, "tensor": tensor, "scalar": scalar}


def ffn_in(nc, sems, sb, bank, g, xn, x_tops, up_raw, gate_raw, top2, x_scale):
    I16 = mybir.dt.int16
    NB = D // BLOCK
    PIECES = 2 * KF
    with ExitStack() as c:
        ident = g["ident"]
        x_top, x_gtop, x_tmp, x_inv = (sb(n, [P, 1], F32, c) for n in ("x_top", "x_gtop", "x_tmp", "x_inv"))
        xi = sb("xi", [P, B, D], I16, c)
        xf = sb("xf", [P, B, D], F32, c)
        rows_done, top_done, all_done, sc_done, xi_done = sems(c, "rows_done top_done all_done sc_done xi_done")
        xt_hi, xt_lo, turn_pe, turn_act, turn_dve, x_lo = turn_rows(nc, sems, sb, c, "ffn", xf, rows_done, ident, bank)
        raws, raw, w_in = RAWS, g["ffn_raw"], g["ffn_w_in"]
        w_top = [sb(f"w_top{i}", [P, NB], F32, c) for i in range(2)]
        w_sc = [sb(f"w_sc{i}", [P, NB], F32, c) for i in range(4)]
        w_inv = [sb(f"w_inv{i}", [P, NB], F32, c) for i in range(3)]
        w_div = [sb(f"w_div{i}", [P, NB, BLOCK], F32, c) for i in range(3)]
        w_int = [sb(f"w_int{i}", [P, NB, BLOCK], F32, c) for i in range(3)]
        w_deq = [sb(f"w_deq{i}", [P, NB, BLOCK], F32, c) for i in range(3)]
        wt_hi = [sb(f"wt_hi{i}", [P, KD, P], F32R, c) for i in range(3)]
        wt_lo = [sb(f"wt_lo{i}", [P, KD, P], F32R, c) for i in range(3)]
        tops = sb("tops", [P, 2, KF], F32, c)
        wtop_done, wsc_done, winv_done, wdiv_done, wint_done, wdeq_done, wtr_done, whi_done, wlo_done = sems(
            c, "wtop_done wsc_done winv_done wdiv_done wint_done wdeq_done wtr_done whi_done wlo_done")
        y_done, kept_done, tops_done, mine_done, both_done = sems(c, "ffn_y ffn_kept tops_done mine_done both_done")
        top_mine = sb("top_mine", [P, 2], F32, c)
        block = c.enter_context(nc.Block())

        def parts(j):
            return wt_hi[j % 3][:, :, :], wt_lo[j % 3][:, :, :]

        def scales(j):
            return w_sc[j % 4][:, :].unsqueeze(2).to_broadcast([P, NB, BLOCK])

        @block.sync
        def _(sp):
            for j in range(raws, PIECES):
                sp.wait_ge(wdiv_done, j - raws + 1)
                g["ffn_load"](sp, j)

        @block.gpsimd
        def _(pool):
            def divided(j):
                pool.wait_ge(winv_done, j + 1)
                wait(pool, wint_done, j - 2)
                nc.gpsimd.tensor_tensor(w_div[j % 3][:, :, :], raw[j % raws][:, :, :],
                                        w_inv[j % 3][:, :].unsqueeze(2).to_broadcast([P, NB, BLOCK]),
                                        ALU.mult).then_inc(wdiv_done, 1)

            def dequantised(j):
                pool.wait_ge(wint_done, j + 1)
                wait(pool, wtr_done, j - 2)
                nc.gpsimd.tensor_tensor(w_deq[j % 3][:, :, :], w_int[j % 3][:, :, :], scales(j),
                                        ALU.mult).then_inc(wdeq_done, 1)

            pool.wait_ge(top_done, 1)
            nc.gpsimd.partition_all_reduce(x_gtop[:, :], x_top[:, :], P, ABSMAX).then_inc(all_done, 1)
            divided(0)
            for j in range(1, PIECES + 2):
                if j >= 2:
                    dequantised(j - 2)
                if j < PIECES:
                    divided(j)
            pool.wait_ge(mine_done, 1)
            nc.gpsimd.partition_all_reduce(top2[:, :], top_mine[:, :], P, ABSMAX).then_inc(both_done, 1)

        @block.vector
        def _(dve):
            def tops_of(j):
                dve.wait_ge(w_in[j % raws], 16 * (j // raws + 1))
                nc.vector.tensor_reduce(w_top[j % 2][:, :], raw[j % raws][:, :, :], AX_X, ALU.max,
                                        apply_absolute_value=True).then_inc(wtop_done, 1)

            def scale_for(j):
                dve.wait_ge(wtop_done, j + 1)
                wait(dve, wdeq_done, j - 3)
                nc.vector.tensor_scalar(w_sc[j % 4][:, :], w_top[j % 2][:, :], 1.0 / 7.0, MIN_SCALE, ALU.mult,
                                        ALU.max).then_inc(wsc_done, 1)

            def inverse_of(j):
                dve.wait_ge(wsc_done, j + 1)
                wait(dve, wdiv_done, j - 2)
                nc.vector.reciprocal(w_inv[j % 3][:, :], w_sc[j % 4][:, :]).then_inc(winv_done, 1)

            def rounded(j):
                dve.wait_ge(wdiv_done, j + 1)
                nc.vector.tensor_scalar(w_int[j % 3][:, :, :], w_div[j % 3][:, :, :], ROUND, ROUND, ALU.add,
                                        ALU.subtract).then_inc(wint_done, 1)

            def low(j):
                dve.wait_ge(whi_done, j + 1)
                hi, lo = parts(j)
                nc.vector.tensor_tensor(lo, bank[4 + j % 4][:, :].rearrange("p (k q) -> p k q", k=KD), hi.bitcast(F32),
                                        ALU.subtract).then_inc(wlo_done, 1)

            def top_of(m):
                dve.wait_ge(kept_done, m + 1)
                src = (up_raw, gate_raw)[m // KF][:, m % KF, :]
                nc.vector.tensor_reduce(tops[:, m // KF, m % KF:m % KF + 1], src, AX_X, ALU.max,
                                        apply_absolute_value=True).then_inc(tops_done, 1)
                if m == PIECES - 1:
                    dve.wait_ge(tops_done, PIECES)
                    nc.vector.tensor_reduce(top_mine[:, :], tops[:, :, :], AX_X, ALU.max).then_inc(mine_done, 1)

            def prepared(j):
                tops_of(j)
                scale_for(j)
                inverse_of(j)

            nc.vector.tensor_reduce(x_top[:, :], x_tops[:, :], AX_X, ALU.max).then_inc(top_done, 1)
            prepared(0)
            prepared(1)
            dve.wait_ge(all_done, 1)
            scale_of(nc, dve, x_gtop[:, :], 1.0, x_scale[:, :], x_inv[:, :], x_tmp[:, :], sc_done, 0)
            for b in range(B):
                nc.vector.tensor_scalar(xi[:, b, :], xn[:, b, :], x_inv[:, 0:1], None, ALU.mult).then_inc(xi_done, 1)
            for b in range(B):
                dve.wait_ge(xi_done, b + 1)
                nc.vector.tensor_copy(xf[:, b, :], xi[:, b, :]).then_inc(rows_done, 1)
            rounded(0)
            rounded(1)
            turn_dve(dve)
            prepared(2)
            for j in range(3, PIECES + 8):
                if j < PIECES:
                    tops_of(j)
                if 4 <= j <= PIECES + 1:
                    rounded(j - 2)
                if j < PIECES:
                    scale_for(j)
                if 4 <= j <= PIECES + 3:
                    low(j - 4)
                if j < PIECES:
                    inverse_of(j)
                if j >= 8:
                    top_of(j - 8)

        @block.scalar
        def _(act):
            turn_act(act)

            def high(j):
                act.wait_ge(wtr_done, j + 1)
                wait(act, y_done, j - 2)
                nc.scalar.activation(parts(j)[0], bank[4 + j % 4][:, :].rearrange("p (k q) -> p k q", k=KD),
                                     ACT.Copy).then_inc(whi_done, 1)

            for j in range(PIECES + 3):
                if j < PIECES:
                    high(j)
                if j >= 3:
                    m = j - 3
                    act.wait_ge(y_done, m + 1)
                    nc.scalar.activation((up_raw, gate_raw)[m // KF][:, m % KF, :], bank[m % 4][:, :],
                                         ACT.Copy).then_inc(kept_done, 1)

        @block.tensor
        def _(pe):
            turn_pe(pe)
            for j in range(PIECES + 2):
                if j < PIECES:
                    pe.wait_ge(wdeq_done, j + 1)
                    wait(pe, wlo_done, j - 3)
                    for k in range(KD):
                        mm = nc.tensor.transpose(bank[4 + j % 4][:, k * P:(k + 1) * P],
                                                 w_deq[j % 3][:, :, :].rearrange("p a i -> p (a i)")[:, k * P:(k + 1) * P],
                                                 ident[:, :])
                    mm.then_inc(wtr_done, 1)
                if j >= 2:
                    m = j - 2
                    if m == 0:
                        pe.wait_ge(x_lo, B)
                    pe.wait_ge(wlo_done, j - 1)
                    wait(pe, kept_done, m - 3)
                    project(nc, bank[m % 4][:, :], [wt_hi[m % 3][:, k, :] for k in range(KD)],
                            [wt_lo[m % 3][:, k, :] for k in range(KD)], [xt_hi[:, k, :] for k in range(KD)],
                            [xt_lo[:, k, :] for k in range(KD)]).then_inc(y_done, 1)


def ffn_out(nc, sems, sb, bank, g, up_raw, gate_raw, wd_hi, wd_lo, top2, x_scale, out):
    I16, U16 = mybir.dt.int16, mybir.dt.uint16
    UNIT = 1.0 / 65536.0
    with ExitStack() as c:
        resid = g["resid"]
        up_i, gate_i = (sb(n, [P, KF, B * P], I16, c) for n in ("up_i", "gate_i"))
        sig = [sb(f"sig{i}", [P, B * P], F32, c) for i in range(2)]
        sig_i = [sb(f"sig_i{i}", [P, B * P], U16, c) for i in range(2)]
        o_hi = [sb(f"o_hi{i}", [P, B * P], F32R, c) for i in range(3)]
        o_lo = [sb(f"o_lo{i}", [P, B * P], F32R, c) for i in range(3)]
        y = sb("y_rows", [P, B, D], F32, c)
        tmp2, scale2, inv2, raw_inv2 = (sb(n, [P, 2], F32, c) for n in ("tmp2", "scale2", "inv2", "raw_inv2"))
        tops3, tops4 = (sb(n, [P, KF], F32, c) for n in ("tops3", "tops4"))
        top3, gtop3, tmp3, scale3, inv3, raw_inv3 = (sb(n, [P, 1], F32, c) for n in
                                                     ("top3", "gtop3", "tmp3", "scale3", "inv3", "raw_inv3"))
        top4, gtop4, tmp4, scale4, inv4, raw_inv4, both_sc = (
            sb(n, [P, 1], F32, c) for n in ("top4", "gtop4", "tmp4", "scale4", "inv4", "raw_inv4", "both_sc"))
        pool_up_done, = sems(c, "pool_up_done")
        sc_done, inv_done, up_done, gate_done, sig_done, sigi_done, act_done, t3_done, m3_done, g3_done = sems(
            c, "o_sc o_inv up_done gate_done sig_done sigi_done act_done t3_done m3_done g3_done")
        inv3_done, gi_done, prod_done, t4_done, m4_done, g4_done, inv4_done, oi_done, oh_done, ol_done, down_done, y_done, sent = sems(
            c, "inv3_done gi_done prod_done t4_done m4_done g4_done inv4_done oi_done oh_done ol_done down_done y_done sent")
        block = c.enter_context(nc.Block())

        @block.sync
        def _(sp):
            for b in range(B):
                sp.wait_ge(y_done, b + 1)
                sp.dma_start(out[b], y[:, b, :]).then_inc(sent, 16)
            sp.wait_ge(sent, 16 * B)

        on_act = [k for k in range(KF) if k % 3 == 2]

        @block.gpsimd
        def _(pool):
            pool.wait_ge(inv_done, 1)
            for k in range(KF):
                if k not in on_act:
                    nc.gpsimd.tensor_scalar(up_i[:, k, :], up_raw[:, k, :], raw_inv2[:, 0:1], None,
                                            ALU.mult).then_inc(pool_up_done, 1)
            pool.wait_ge(m3_done, 1)
            nc.gpsimd.partition_all_reduce(gtop3[:, :], top3[:, :], P, ABSMAX).then_inc(g3_done, 1)
            pool.wait_ge(m4_done, 1)
            nc.gpsimd.partition_all_reduce(gtop4[:, :], top4[:, :], P, ABSMAX).then_inc(g4_done, 1)

        @block.vector
        def _(dve):
            at = scale_of(nc, dve, top2[:, :], x_scale[:, 0:1], scale2[:, :], inv2[:, :], tmp2[:, :], sc_done, 0)
            nc.vector.tensor_scalar(raw_inv2[:, :], inv2[:, :], x_scale[:, 0:1], None, ALU.mult).then_inc(inv_done, 1)
            def top_of_gate(k):
                dve.wait_ge(act_done, k + 1)
                nc.vector.tensor_reduce(tops3[:, k:k + 1], gate_raw[:, k, :], AX_X, ALU.max,
                                        apply_absolute_value=True).then_inc(t3_done, 1)

            for k in range(KF):
                dve.wait_ge(sig_done, k + 1)
                nc.vector.tensor_scalar(sig_i[k % 2][:, :], sig[k % 2][:, :], 65536.0, None, ALU.mult).then_inc(sigi_done, 1)
                if k >= 1:
                    top_of_gate(k - 1)
                dve.wait_ge(sigi_done, k + 1)
                nc.vector.scalar_tensor_tensor(gate_raw[:, k, :], gate_i[:, k, :], scale2[:, 1:2], sig_i[k % 2][:, :],
                                               ALU.mult, ALU.mult).then_inc(act_done, 1)
            top_of_gate(KF - 1)
            dve.wait_ge(t3_done, KF)
            nc.vector.tensor_reduce(top3[:, :], tops3[:, :], AX_X, ALU.max).then_inc(m3_done, 1)
            dve.wait_ge(g3_done, 1)
            at = scale_of(nc, dve, gtop3[:, :], UNIT, scale3[:, :], inv3[:, :], tmp3[:, :], sc_done, at)
            nc.vector.tensor_scalar(raw_inv3[:, :], inv3[:, :], UNIT, None, ALU.mult).then_inc(inv3_done, 1)
            dve.wait_ge(up_done, len(on_act))
            dve.wait_ge(pool_up_done, KF - len(on_act))

            def top_of_product(k):
                dve.wait_ge(prod_done, k + 1)
                nc.vector.tensor_reduce(tops4[:, k:k + 1], gate_raw[:, k, :], AX_X, ALU.max,
                                        apply_absolute_value=True).then_inc(t4_done, 1)

            for k in range(KF):
                dve.wait_ge(gi_done, k + 1)
                nc.vector.tensor_tensor(gate_raw[:, k, :], gate_i[:, k, :], up_i[:, k, :], ALU.mult).then_inc(prod_done, 1)
                if k >= 1:
                    top_of_product(k - 1)
            top_of_product(KF - 1)
            dve.wait_ge(t4_done, KF)
            nc.vector.tensor_reduce(top4[:, :], tops4[:, :], AX_X, ALU.max).then_inc(m4_done, 1)
            nc.vector.tensor_scalar(both_sc[:, :], scale3[:, :], scale2[:, 0:1], None, ALU.mult).then_inc(m4_done, 1)
            dve.wait_ge(m4_done, 2)
            dve.wait_ge(g4_done, 1)
            at = scale_of(nc, dve, gtop4[:, :], both_sc[:, 0:1], scale4[:, :], inv4[:, :], tmp4[:, :], sc_done, at)
            nc.vector.tensor_scalar(raw_inv4[:, :], inv4[:, :], both_sc[:, 0:1], None, ALU.mult).then_inc(inv4_done, 1)
            for k in range(KF):
                dve.wait_ge(oi_done, k + 1)
                wait(dve, down_done, k - 2)
                nc.vector.tensor_copy(o_hi[k % 3][:, :], up_i[:, k, :]).then_inc(oh_done, 1)
                dve.wait_ge(oh_done, k + 1)
                nc.vector.tensor_tensor(o_lo[k % 3][:, :], up_i[:, k, :], o_hi[k % 3][:, :].bitcast(F32),
                                        ALU.subtract).then_inc(ol_done, 1)
            for b in range(B):
                dve.wait_ge(down_done, KF + b)
                nc.vector.scalar_tensor_tensor(y[:, b, :], bank[b][:, :], scale4[:, 0:1], resid[:, b, :], ALU.mult,
                                               ALU.add).then_inc(y_done, 1)

        @block.scalar
        def _(act):
            act.wait_ge(inv_done, 1)

            def gate_int(k):
                nc.scalar.activation(gate_i[:, k, :], gate_raw[:, k, :], ACT.Copy, scale=raw_inv2[:, 1:2]).then_inc(gate_done, 1)

            gate_int(0)
            for k in range(KF):
                if k + 1 < KF:
                    gate_int(k + 1)
                act.wait_ge(gate_done, k + 1)
                wait(act, sigi_done, k - 1)
                nc.scalar.activation(sig[k % 2][:, :], gate_i[:, k, :], ACT.Sigmoid, scale=scale2[:, 1:2]).then_inc(sig_done, 1)
                if k in on_act:
                    nc.scalar.activation(up_i[:, k, :], up_raw[:, k, :], ACT.Copy, scale=raw_inv2[:, 0:1]).then_inc(up_done, 1)
            act.wait_ge(inv3_done, 1)
            for k in range(KF):
                nc.scalar.activation(gate_i[:, k, :], gate_raw[:, k, :], ACT.Copy, scale=raw_inv3[:, 0:1]).then_inc(gi_done, 1)
            act.wait_ge(inv4_done, 1)
            for k in range(KF):
                nc.scalar.activation(up_i[:, k, :], gate_raw[:, k, :], ACT.Copy, scale=raw_inv4[:, 0:1]).then_inc(oi_done, 1)

        @block.tensor
        def _(pe):
            for k in range(KF):
                pe.wait_ge(ol_done, k + 1)
                for b in range(B):
                    at = slice(b * P, (b + 1) * P)
                    nc.tensor.matmul(bank[b][:, :], o_hi[k % 3][:, at], wd_hi[:, k, :], start=(k == 0), stop=False)
                    nc.tensor.matmul(bank[b][:, :], o_hi[k % 3][:, at], wd_lo[:, k, :], start=False, stop=False)
                    mm = nc.tensor.matmul(bank[b][:, :], o_lo[k % 3][:, at], wd_hi[:, k, :], start=False, stop=(k == KF - 1))
                    if b == B - 1 or k == KF - 1:
                        mm.then_inc(down_done, 1)


_OUTS = [((4, 128, 512), "float32")]


def kernel(**inputs):
    import numpy as _np
    import concourse.bacc as _bacc
    from concourse import mybir as _mybir
    from concourse.bass_utils import run_bass_kernel_spmd as _run

    def whole(name):
        return _np.ascontiguousarray(inputs[name])

    context = whole("ctx_1024").reshape(B, CHUNKS, TILES, P, KD, P).transpose(0, 1, 2, 5, 4, 3)
    laid = {
        "x": whole("x"),
        "ctx_t": _np.ascontiguousarray(context.reshape(B * CHUNKS, TILES, P, KD, P)),
        "lens": whole("_lenS2"),
        "wq": whole("L0_xattn_Wq"), "wk": whole("L0_xattn_Wk"), "wv": whole("L0_xattn_Wv"), "wo": whole("L0_xattn_Wo"),
        "q_norm": whole("L0_xattn_q_norm_w"), "k_norm": whole("L0_xattn_k_norm_w"),
        "w_qkv": whole("L0_attn_w_qkv").reshape(D, 3 * E), "b_qkv": whole("L0_attn_b_qkv").reshape(3 * E),
        "w_out": whole("L0_attn_w_out").reshape(E, D), "b_out": whole("L0_attn_b_out"),
        "w_gate": whole("L0_ffn_w_gate"), "w_up": whole("L0_ffn_w_up"), "w_down": whole("L0_ffn_w_down"),
    }
    nc = _bacc.Bacc("TRN2", target_bir_lowering=False, num_devices=1)
    args = [nc.dram_tensor(f"in_{n}_dram", a.shape, _mybir.dt.from_np(a.dtype), kind="ExternalInput").ap()
            for n, a in laid.items()]
    for i, (shape, dtype) in enumerate(_OUTS):
        args.append(nc.dram_tensor(f"out_{i}_dram", shape, _mybir.dt.from_np(_np.dtype(dtype)), kind="ExternalOutput").ap())
    program(nc, *args)
    r = _run(nc, [{f"in_{n}_dram": a for n, a in laid.items()}], core_ids=[0])
    return r.results[0]["out_0_dram"]
```
